# Optimizing a Trainium2 kernel written in Bass

```python
import numpy as np
import jax
import jax.numpy as jnp

def _softmax(x, axis=-1):
    return jax.nn.softmax(x, axis=axis)

def _gelu(x):
    return jax.nn.gelu(x, approximate=True)

def _silu(x):
    return jax.nn.silu(x)

def _sigmoid(x):
    return jax.nn.sigmoid(x)

def _layernorm(x, axis=-1, eps=1e-05):
    m = jnp.mean(x, axis=axis, keepdims=True)
    v = jnp.var(x, axis=axis, keepdims=True)
    return (x - m) / jnp.sqrt(v + eps)

def _scatter_add(tgt, idx, src, axis=0):
    return tgt.at[idx].add(src)

def _segment_sum(src, seg, n):
    return jax.ops.segment_sum(src, seg, n)
kernel_name = 'mk_flamingo_gated_d2_seqx_r8_e82457'

def setup_inputs(seed: int=0):
    np.random.seed(seed)
    _w = jnp.asarray

    def _rec_inputs():
        import jax
        import jax.numpy as jnp
        _rk = jax.random.key(seed)
        x = 0.0003765 + 1 * jax.random.normal(jax.random.fold_in(_rk, 1), (16, 56, 128), jnp.float32)
        _lenS = 56 - jax.random.randint(jax.random.fold_in(_rk, 7), (16,), 0, max(1, 56 // 4) + 1, jnp.int32)
        _lenS2 = 1500 - jax.random.randint(jax.random.fold_in(_rk, 8), (16,), 0, max(1, 1500 // 4) + 1, jnp.int32)
        _ctx_1024P = jax.random.normal(jax.random.fold_in(_rk, 11), (16, 16, 128), jnp.float32)
        _ctx_1024c = jax.random.dirichlet(jax.random.fold_in(_rk, 511), 0.3 * jnp.ones((16,), jnp.float32), (16, 1500))
        _ctx_1024t = jnp.einsum('bsk,bkd->bsd', _ctx_1024c, _ctx_1024P)
        _ctx_1024t = _ctx_1024t * jax.lax.rsqrt(jnp.mean(jnp.square(_ctx_1024t)) + 1e-12) * 0.953939
        ctx_1024 = -0.000292821 + 1.00034 * (_ctx_1024t + 0.3 * jax.random.normal(jax.random.fold_in(_rk, 611), (16, 1500, 128), jnp.float32))
        _validS = jnp.arange(56)[None, :] < _lenS[:, None]
        _validS2 = jnp.arange(1500)[None, :] < _lenS2[:, None]
        _causal = jnp.tril(jnp.ones((56, 56), dtype=bool))
        mask_Bx1xSxS2_if1 = jnp.where(jnp.ones((16, 1, 56, 1500), dtype=bool), 1, 0).astype(jnp.int32)
        _g = jax.random.normal(jax.random.fold_in(_rk, 9001), (2, 2), jnp.float32)
        _g = jnp.sign(_g) * jnp.maximum(jnp.abs(_g), 1.0) + (_g == 0) * 1.0
        g_xattn = _g[0]
        g_ffn = _g[1]
        return (x, ctx_1024, mask_Bx1xSxS2_if1, g_xattn, g_ffn)
    x, ctx_1024, mask_Bx1xSxS2_if1, g_xattn, g_ffn = _rec_inputs()

    def _L0_xattn_setup():
        import jax, jax.numpy as jnp
        import numpy as np
        HEADS = 16
        key = jax.random.key(seed)
        ks = jax.random.split(key, 8)
        N, S, E = (2, 256, 128)
        D = E // HEADS
        return {'values': jax.random.normal(ks[0], (N, S, E), jnp.float32), 'keys': jax.random.normal(ks[1], (N, S, E), jnp.float32), 'queries': jax.random.normal(ks[2], (N, S, E), jnp.float32), 'mask': jnp.ones((N, 1, S, S), jnp.int32), 'Wv': jax.random.normal(ks[3], (D, D), jnp.float32) * D ** (-0.5), 'Wk': jax.random.normal(ks[4], (D, D), jnp.float32) * D ** (-0.5), 'Wq': jax.random.normal(ks[5], (D, D), jnp.float32) * D ** (-0.5), 'Wo': jax.random.normal(ks[6], (E, E), jnp.float32) * E ** (-0.5), 'bo': jnp.zeros((E,), jnp.float32)}
    _L0_xattn_all = _L0_xattn_setup()
    _L0_xattn_in = {k: v for k, v in _L0_xattn_all.items() if k in ('Wv', 'Wk', 'Wq', 'Wo', 'bo')}
    del _L0_xattn_all

    def _L0_ffn_setup():
        import jax, jax.numpy as jnp
        import numpy as np
        H = 128
        I = 256
        E = 8
        B, S = (2, 128)

        def _swiglu(x, wg, wu, wd):
            return jax.nn.silu(x @ wg) * (x @ wu) @ wd
        key = jax.random.key(seed)
        ks = jax.random.split(key, 8)
        sc_h = 1.0 / np.sqrt(H)
        sc_i = 1.0 / np.sqrt(I)
        return {'hidden_states': jax.random.normal(ks[0], (B, S, H), jnp.float32), 'gate_w': jax.random.normal(ks[1], (H, E), jnp.float32) * sc_h, 'sh_gate': jax.random.normal(ks[2], (H, I), jnp.float32) * sc_h, 'sh_up': jax.random.normal(ks[3], (H, I), jnp.float32) * sc_h, 'sh_down': jax.random.normal(ks[4], (I, H), jnp.float32) * sc_i, 'rt_gate': jax.random.normal(ks[5], (E, H, I), jnp.float32) * sc_h, 'rt_up': jax.random.normal(ks[6], (E, H, I), jnp.float32) * sc_h, 'rt_down': jax.random.normal(ks[7], (E, I, H), jnp.float32) * sc_i}
    _L0_ffn_all = _L0_ffn_setup()
    _L0_ffn_in = {k: v for k, v in _L0_ffn_all.items() if k in ('gate_w', 'sh_gate', 'sh_up', 'sh_down', 'rt_gate', 'rt_up', 'rt_down')}
    del _L0_ffn_all

    def _L1_xattn_setup():
        import jax, jax.numpy as jnp
        import numpy as np
        EMBED_DIM = 128
        D_QKV = 64
        N_HEADS = 16
        SCALE = D_QKV ** 0.5
        key = jax.random.key(seed)
        ks = jax.random.split(key, 8)
        b, lq, lk, e = (2, 256, 256, EMBED_DIM)
        h, d = (N_HEADS, D_QKV)
        X = jax.random.normal(ks[0], (b, lq, e), dtype=jnp.float32)
        encoder_out = jax.random.normal(ks[1], (b, lk, e), dtype=jnp.float32)
        Wq = jax.random.normal(ks[2], (h * d, e), dtype=jnp.float32) * 0.02
        bq = jnp.zeros((h * d,), dtype=jnp.float32)
        Wkv = jax.random.normal(ks[3], (h * 2 * d, e), dtype=jnp.float32) * 0.02
        bkv = jnp.zeros((h * 2 * d,), dtype=jnp.float32)
        Wo = jax.random.normal(ks[4], (e, h * d), dtype=jnp.float32) * 0.02
        bo = jnp.zeros((e,), dtype=jnp.float32)
        return {'X': X, 'encoder_out': encoder_out, 'Wq': Wq, 'bq': bq, 'Wkv': Wkv, 'bkv': bkv, 'Wo': Wo, 'bo': bo}
    _L1_xattn_all = _L1_xattn_setup()
    _L1_xattn_in = {k: v for k, v in _L1_xattn_all.items() if k in ('Wq', 'bq', 'Wkv', 'bkv', 'Wo', 'bo')}
    del _L1_xattn_all

    def _L1_ffn_setup():
        import jax, jax.numpy as jnp
        import numpy as np
        HIDDEN = 128
        INNER = 512

        def _weight_quant(w):
            scale = 1.0 / jnp.clip(jnp.mean(jnp.abs(w)), 1e-05)
            wq = jnp.clip(jnp.round(w * scale), -1.0, 1.0) / scale
            return w + jax.lax.stop_gradient(wq - w)

        def _act_quant(x):
            scale = 127.0 / jnp.clip(jnp.max(jnp.abs(x), axis=-1, keepdims=True), 1e-05)
            xq = jnp.clip(jnp.round(x * scale), -128.0, 127.0) / scale
            return x + jax.lax.stop_gradient(xq - x)

        def _bitlinear(x, w):
            return jnp.einsum('bsi,oi->bso', _act_quant(x), _weight_quant(w))
        key = jax.random.key(seed)
        k0, k1, k2, k3 = jax.random.split(key, 4)
        x = jax.random.normal(k0, (4, 256, HIDDEN), dtype=jnp.float32)
        w_gate = jax.random.normal(k1, (INNER, HIDDEN), dtype=jnp.float32) / np.sqrt(HIDDEN)
        w_up = jax.random.normal(k2, (INNER, HIDDEN), dtype=jnp.float32) / np.sqrt(HIDDEN)
        w_down = jax.random.normal(k3, (HIDDEN, INNER), dtype=jnp.float32) / np.sqrt(INNER)
        return {'x': x, 'w_gate': w_gate, 'w_up': w_up, 'w_down': w_down}
    _L1_ffn_all = _L1_ffn_setup()
    _L1_ffn_in = {k: v for k, v in _L1_ffn_all.items() if k in ('w_gate', 'w_up', 'w_down')}
    del _L1_ffn_all
    return {'x': x, 'ctx_1024': ctx_1024, 'mask_Bx1xSxS2_if1': mask_Bx1xSxS2_if1, 'g_xattn': g_xattn, 'g_ffn': g_ffn, 'L0_xattn_Wv': _L0_xattn_in['Wv'], 'L0_xattn_Wk': _L0_xattn_in['Wk'], 'L0_xattn_Wq': _L0_xattn_in['Wq'], 'L0_xattn_Wo': _L0_xattn_in['Wo'], 'L0_xattn_bo': _L0_xattn_in['bo'], 'L0_ffn_gate_w': _L0_ffn_in['gate_w'], 'L0_ffn_sh_gate': _L0_ffn_in['sh_gate'], 'L0_ffn_sh_up': _L0_ffn_in['sh_up'], 'L0_ffn_sh_down': _L0_ffn_in['sh_down'], 'L0_ffn_rt_gate': _L0_ffn_in['rt_gate'], 'L0_ffn_rt_up': _L0_ffn_in['rt_up'], 'L0_ffn_rt_down': _L0_ffn_in['rt_down'], 'L1_xattn_Wq': _L1_xattn_in['Wq'], 'L1_xattn_bq': _L1_xattn_in['bq'], 'L1_xattn_Wkv': _L1_xattn_in['Wkv'], 'L1_xattn_bkv': _L1_xattn_in['bkv'], 'L1_xattn_Wo': _L1_xattn_in['Wo'], 'L1_xattn_bo': _L1_xattn_in['bo'], 'L1_ffn_w_gate': _L1_ffn_in['w_gate'], 'L1_ffn_w_up': _L1_ffn_in['w_up'], 'L1_ffn_w_down': _L1_ffn_in['w_down']}

def reference(x, ctx_1024, mask_Bx1xSxS2_if1, g_xattn, g_ffn, L0_xattn_Wv, L0_xattn_Wk, L0_xattn_Wq, L0_xattn_Wo, L0_xattn_bo, L0_ffn_gate_w, L0_ffn_sh_gate, L0_ffn_sh_up, L0_ffn_sh_down, L0_ffn_rt_gate, L0_ffn_rt_up, L0_ffn_rt_down, L1_xattn_Wq, L1_xattn_bq, L1_xattn_Wkv, L1_xattn_bkv, L1_xattn_Wo, L1_xattn_bo, L1_ffn_w_gate, L1_ffn_w_up, L1_ffn_w_down):
    import jax
    import jax.numpy as jnp

    def _L0_xattn_ref(values, keys, queries, mask, Wv, Wk, Wq, Wo, bo):
        import jax, jax.numpy as jnp
        import numpy as np
        HEADS = 16
        N, Sq, E = queries.shape
        H = HEADS
        D = E // H
        v = values.reshape(N, -1, H, D)
        k = keys.reshape(N, -1, H, D)
        q = queries.reshape(N, Sq, H, D)
        v = jnp.einsum('nlhd,od->nlho', v, Wv)
        k = jnp.einsum('nlhd,od->nlho', k, Wk)
        q = jnp.einsum('nqhd,od->nqho', q, Wq)
        energy = jnp.einsum('nqhd,nkhd->nhqk', q, k)
        energy = jnp.where(mask == 0, jnp.float32(-1e+20), energy)
        attn = jax.nn.softmax(energy * (1.0 / E ** 0.5), axis=3)
        out = jnp.einsum('nhqk,nkhd->nqhd', attn, v).reshape(N, Sq, E)
        return out @ Wo.T + bo

    def _L0_ffn_ref(hidden_states, gate_w, sh_gate, sh_up, sh_down, rt_gate, rt_up, rt_down):
        import jax, jax.numpy as jnp
        import numpy as np
        H = 128
        I = 256
        E = 8
        B, S = (2, 128)

        def _swiglu(x, wg, wu, wd):
            return jax.nn.silu(x @ wg) * (x @ wu) @ wd
        b, s, h = hidden_states.shape
        x = hidden_states.reshape(-1, h)
        logits = x @ gate_w
        top_val = jnp.max(logits, axis=-1, keepdims=True)
        top_id = jnp.argmax(logits, axis=-1)
        score = jax.nn.sigmoid(top_val)
        xs = x * score
        g = jnp.einsum('th,ehi->eti', xs, rt_gate)
        u = jnp.einsum('th,ehi->eti', xs, rt_up)
        act = jax.nn.silu(g) * u
        y = jnp.einsum('eti,eih->eth', act, rt_down)
        onehot = jax.nn.one_hot(top_id, E, dtype=x.dtype)
        routed = jnp.einsum('eth,te->th', y, onehot)
        shared = _swiglu(x, sh_gate, sh_up, sh_down)
        return (shared + routed).reshape(b, s, h)

    def _L1_xattn_ref(X, encoder_out, Wq, bq, Wkv, bkv, Wo, bo):
        import jax, jax.numpy as jnp
        import numpy as np
        EMBED_DIM = 128
        D_QKV = 64
        N_HEADS = 16
        SCALE = D_QKV ** 0.5
        b, lq, e = X.shape
        lk = encoder_out.shape[1]
        h, d = (N_HEADS, D_QKV)
        Q = (X @ Wq.T + bq).reshape(b, lq, h, d)
        KV = (encoder_out @ Wkv.T + bkv).reshape(b, lk, h, 2 * d)
        K, V = (KV[..., :d], KV[..., d:])
        scores = jnp.einsum('bqhd,bkhd->bhqk', Q, K) / SCALE
        weights = jax.nn.softmax(scores, axis=-1)
        attn = jnp.einsum('bhqk,bkhd->bqhd', weights, V).reshape(b, lq, h * d)
        out = attn @ Wo.T + bo
        return out

    def _L1_ffn_ref(x, w_gate, w_up, w_down):
        import jax, jax.numpy as jnp
        import numpy as np
        HIDDEN = 128
        INNER = 512

        def _weight_quant(w):
            scale = 1.0 / jnp.clip(jnp.mean(jnp.abs(w)), 1e-05)
            wq = jnp.clip(jnp.round(w * scale), -1.0, 1.0) / scale
            return w + jax.lax.stop_gradient(wq - w)

        def _act_quant(x):
            scale = 127.0 / jnp.clip(jnp.max(jnp.abs(x), axis=-1, keepdims=True), 1e-05)
            xq = jnp.clip(jnp.round(x * scale), -128.0, 127.0) / scale
            return x + jax.lax.stop_gradient(xq - x)

        def _bitlinear(x, w):
            return jnp.einsum('bsi,oi->bso', _act_quant(x), _weight_quant(w))
        gate = jax.nn.silu(_bitlinear(x, w_gate))
        up = _bitlinear(x, w_up)
        return _bitlinear(gate * up, w_down)
    x = x + jnp.tanh(g_xattn[0]) * _L0_xattn_ref(ctx_1024, ctx_1024, _layernorm(x, axis=-1), mask_Bx1xSxS2_if1, L0_xattn_Wv, L0_xattn_Wk, L0_xattn_Wq, L0_xattn_Wo, L0_xattn_bo)
    x = x + jnp.tanh(g_ffn[0]) * _L0_ffn_ref(_layernorm(x, axis=-1), L0_ffn_gate_w, L0_ffn_sh_gate, L0_ffn_sh_up, L0_ffn_sh_down, L0_ffn_rt_gate, L0_ffn_rt_up, L0_ffn_rt_down)
    x = x + jnp.tanh(g_xattn[1]) * _L1_xattn_ref(_layernorm(x, axis=-1), ctx_1024, L1_xattn_Wq, L1_xattn_bq, L1_xattn_Wkv, L1_xattn_bkv, L1_xattn_Wo, L1_xattn_bo)
    x = x + jnp.tanh(g_ffn[1]) * _L1_ffn_ref(_layernorm(x, axis=-1), L1_ffn_w_gate, L1_ffn_w_up, L1_ffn_w_down)
    return x

_drawn_inputs = setup_inputs


def setup_inputs(seed=0):
    import zlib

    import numpy as np

    out = dict(_drawn_inputs(seed))
    spreads = {'g_ffn': (-1.0, 0.6),
     'L0_xattn_bo': (0.0, 0.1),
     'L1_xattn_bq': (0.0, 2.0),
     'L1_xattn_bkv': (0.0, 0.1),
     'L1_xattn_bo': (0.0, 0.1)}
    factors = {'L1_xattn_Wq': 49.419}
    for name, (base, spread) in spreads.items():
        noise = np.random.default_rng([zlib.crc32(name.encode()), seed]).standard_normal(out[name].shape)
        drawn = base * np.exp(spread * noise) if base else spread * noise
        out[name] = jnp.asarray(drawn.astype(out[name].dtype))
    for name, factor in factors.items():
        out[name] = (out[name] * factor).astype(out[name].dtype)
    return out
```

```python
import concourse.bass as bass
from concourse import mybir
from contextlib import ExitStack

F32 = mybir.dt.float32
F16 = mybir.dt.float16
BF16 = mybir.dt.bfloat16
I32 = mybir.dt.int32
ALU = mybir.AluOpType
ACT = mybir.ActivationFunctionType
AX = mybir.AxisListType


def wait(engine, semaphore, value):
    if not isinstance(value, int) or value > 0:
        engine.wait_ge(semaphore, value)


def flamingo_kernel(nc, x, ctx_in, mask, g_xattn, g_ffn,
                    wv0, wk0, wq0, wo0, bo0, gate_w, sh_gate, sh_up, sh_down, rt_gate, rt_up, rt_down,
                    wq1, bq1, wkv1, bkv1, wo1, bo1, w_gate, w_up, w_down, out):
    B, S, E = x.shape
    S2 = ctx_in.shape[1]
    H = 16
    D0 = E // H
    D1 = wq1.shape[0] // H
    KC = 12
    KP = S2 // KC
    ROWS = H * S
    NTOK = B * S
    TT = NTOK // 128
    HALF = NTOK // 2
    G = 4
    HG = H // G
    GC = HG * S
    T0 = 8
    R0 = 2 * S
    T1 = ROWS // 128
    UC = KC // 2
    NE = gate_w.shape[1]
    INNER0 = sh_gate.shape[1]
    IC = INNER0 // 128
    INNER1 = w_gate.shape[0]
    JC = INNER1 // 128
    EPS = 1e-5
    NEG = -1e20
    SCALE0 = float(E) ** -0.5
    SCALE1 = float(D1) ** -0.5
    PSCALE = 2.0 ** 14
    ROUND = 1.5 * 2.0 ** 23
    LAST = B // 2 - 1

    ctx = ExitStack()
    with ctx:
        def sb(name, shape, dt=F32):
            return ctx.enter_context(nc.sbuf_tensor(name, shape, dt))

        sems = {}

        def sem(name):
            if name not in sems:
                sems[name] = ctx.enter_context(nc.semaphore(name))
            return sems[name]

        ident = sb("ident", [128, 128])
        ident16 = sb("ident16", [128, 128], F16)
        ones_f = sb("ones_f", [128, 128])
        half_neg = sb("half_neg", [128, TT])
        head_of = sb("head_of", [128, H])
        expert_id = sb("expert_id", [128, NE])
        expert_row = sb("expert_row", [NE, NE, 128], F16)
        x_tok = sb("x_tok", [128, TT, E])
        x_norm = sb("x_norm", [128, TT, E])
        x_norm_t = sb("x_norm_t", [128, NTOK])
        stats = sb("stats", [128, TT, 6])
        mean_var = sb("mean_var", [128, TT, 2])
        rstd = sb("rstd", [128, TT])
        block_t = sb("block_t", [128, NTOK])
        gates = sb("gates", [128, 4])
        tanh_g = sb("tanh_g", [128, 4])
        bo0_col = sb("bo0_col", [128, 1])
        bo1_col = sb("bo1_col", [128, 1])

        w8 = sb("w8", [128, 3, D0])
        block_diag = sb("block_diag", [128, 3, E])
        wo0_sb = sb("wo0_sb", [128, E])
        wo0_t = sb("wo0_t", [128, E])

        gate_w_sb = sb("gate_w_sb", [128, NE])
        g_w = sb("g_w", [128, NE + 1, INNER0])
        u_w = sb("u_w", [128, NE + 1, INNER0])
        logits = sb("logits", [128, TT, NE])
        top = sb("top", [128, TT])
        is_top = sb("is_top", [128, TT, NE])
        first_top = sb("first_top", [128, TT])
        one_hot = sb("one_hot", [128, TT, NE])
        one_hot_t = sb("one_hot_t", [NE, NTOK], F16)
        score = sb("score", [128, TT])

        bq1_col = sb("bq1_col", [128, 8])
        bv1_col = sb("bv1_col", [128, 8])
        bias1 = sb("bias1", [128, 1])

        wg_sb = sb("wg_sb", [128, 3, JC, 128])
        abs_sum = sb("abs_sum", [128, 3])
        w_mean = sb("w_mean", [128, 3])
        w_scale = sb("w_scale", [128, 3])
        ident_b = sb("ident_b", [128, 128], BF16)
        x_amax = sb("x_amax", [128, TT])
        x_qscale = sb("x_qscale", [128, TT])
        x_deq = sb("x_deq", [128, TT, 2])
        h_amax = sb("h_amax", [128, TT])
        h_qscale = sb("h_qscale", [128, TT])
        h_deq = sb("h_deq", [128, TT])

        c_in = [sb(f"c_in{p}", [KP, KC, E]) for p in range(2)]
        e_row = [sb(f"e_row{p}", [128, S2]) for p in range(2)]
        neg_max = sb("neg_max", [128, T0])
        row_sum = sb("row_sum", [128, T0])
        row_inv = sb("row_inv", [128, T0])

        REGION = 34304
        region = sb("region", [128, REGION])
        at = [0]

        def carve(shape, dt=F32):
            size = 1
            for n in shape[1:]:
                size *= n
            words = size if dt in (F32, I32) else (size + 1) // 2
            t = region[0:shape[0], at[0]:at[0] + words]
            at[0] += words
            assert at[0] <= REGION, at[0]
            if dt is not F32:
                t = t.bitcast(dt)
            if len(shape) > 2:
                dims = [f"d{n}" for n in range(len(shape) - 1)]
                t = t.rearrange(f"p ({' '.join(dims)}) -> p {' '.join(dims)}", **dict(zip(dims, shape[1:])))
            return t

        q0 = carve([96, B, ROWS], F16)
        c_split0 = carve([128, KC, 2, E], F16)
        c_group = [carve([KP, KC, G, 64], F16) for _ in range(2)]
        c_t0 = carve([128, 2, KC, 128], F16)
        c_stack = [carve([96, G, KC, 128], F16) for _ in range(2)]
        mask_in = carve([R0, S2], I32)
        mask_bias = [carve([R0, KC, KP], BF16) for _ in range(2)]
        masked = [carve([R0, S2]) for _ in range(2)]
        inv_b = carve([128, GC])
        u0 = carve([128, G, GC])
        out0_w = carve([128, H, 128])
        before_p0 = at[0]
        p_high0 = [carve([KP, KC, GC], F16) for _ in range(2)]
        p_low0 = [carve([KP, KC, GC], F16) for _ in range(2)]
        at[0] = before_p0
        a_heads = carve([128, H, 3, 32])
        v_heads = carve([128, H, 4, 32])

        at[0] = 0
        x_score_t = carve([128, NTOK])
        x_exp = carve([128, 2, HALF])
        silu0 = carve([128, 2, HALF])
        act0 = carve([128, 2, HALF])
        d_w = carve([128, NE + 1, IC, 128])
        wq1_sb = carve([128, 8, 128])
        wo1_sb = carve([128, 8, 128])

        at[0] = 0
        q1 = carve([128, 2, B, ROWS], F16)
        out1_w = carve([128, H, 128])
        c_split1 = [carve([128, KC, 2, E], F16) for _ in range(2)]
        c_t1 = [carve([128, 2, KC, 128], F16) for _ in range(2)]
        GROUPS1 = [(0, 4), (4, T1)]
        before_p1 = at[0]
        p_high1 = [carve([KP, KC, 128 * (b - a)], F16) for a, b in GROUPS1]
        p_low1 = [carve([KP, KC, 128 * (b - a)], F16) for a, b in GROUPS1]
        u1 = carve([128, ROWS])
        at[0] = before_p1
        q1_proj = carve([128, 8, NTOK])
        wq1_t = carve([128, 8, 128])
        wk1_sb = carve([128, 8, 128])
        wv1_sb = carve([128, 8, 128])
        wo1_t = carve([128, 8, 128])

        at[0] = 0
        w_round = carve([128, 3, JC, 128])
        w_tern = carve([128, 3, JC, 128], BF16)
        w_tern_t = carve([128, 3, JC, 128], BF16)
        xq = carve([128, TT, E], BF16)
        xq_t = carve([128, TT, 128], BF16)
        hq = carve([128, 2, INNER1], BF16)
        hq_t = carve([128, 2, JC, 128], BF16)
        silu1 = carve([128, 2, INNER1])
        act1 = carve([128, 2, INNER1])

        bank = ctx.enter_context(nc.psum_tensor("bank", [128, 8, 512], F32))
        U_BANK = 7

        def pair(u):
            return bank[:, 3 + 2 * (u % 2):5 + 2 * (u % 2), :]

        def pair_flat(u, dt=F32):
            t = pair(u).rearrange("p a b -> p (a b)")
            return t if dt is F32 else t.bitcast(dt)

        def pair_chunks(u, cols):
            return pair_flat(u)[0:KP, 0:UC * 128].rearrange("p (c n) -> p c n", n=128)[:, :, 0:cols]

        block = ctx.enter_context(nc.Block())

        def order(tiles, proj_after, prep_after):
            units = []
            for t in range(tiles):
                units += [("turn", t, 0), ("turn", t, 1)]
                if t == proj_after:
                    units.append(("proj", 0, 0))
                if t == prep_after:
                    units += [("prep", 0, 0), ("prep", 1, 0)]
            return units

        PROJ_AT, PREP_AT = 3, 3
        UNITS = {0: order(T0, PROJ_AT, PREP_AT), 1: order(T1, 3, 4)}
        PREP1_AT = 4

        def unit_no(layer, par, what):
            return par + UNITS[layer].index(what)

        def consumed(layer, b, par, what):
            kind, n, u = what
            tiles = T0 if layer == 0 else T1
            if kind == "turn":
                return sem(f"low_done{layer}"), b * (2 * tiles) + 2 * n + u + 1
            if kind == "proj":
                return sem(f"block_done{layer}"), b + 0
            return sem(f"ct_done{layer}_{n}"), b + 2

        def wait_pair(engine, layer, b, par, what):
            units = UNITS[layer]
            k, back = units.index(what) - 2, 0
            while True:
                if k < 0:
                    k, back = k + len(units), back + 1
                before = units[k]
                first = isinstance(b, int) and b - back == 0
                last = isinstance(b, int) and b - back == B - 1
                if isinstance(b, int) and b - back < 0:
                    if before[0] == "prep" or back > 1:
                        pass
                    n = k - (len(units) - 2)
                    if n in (0, 1):
                        wait(engine, sem(f"ct_done{layer}_{n}"), 1)
                    return
                beyond = isinstance(b, int) and b - back == B
                if beyond or (before[0] == "proj" and first) or (before[0] == "prep" and last):
                    k -= 2
                    continue
                s, v = consumed(layer, b - back, par, before)
                wait(engine, s, v)
                return

        def wait_apart(engine, name, *waits):
            for semaphore, count in waits:
                wait(engine, semaphore, count)
            engine.sem_inc(sem(f"passed_{name}"), 1)

        def batches(engine, body):
            body(0, 0, True, False)
            body(1, 1, False, False)
            with engine.Fori(1, LAST) as i:
                body(i * 2, 0, False, False)
                body(i * 2 + 1, 1, False, False)
            body(B - 2, 0, False, False)
            body(B - 1, 1, False, True)

        def uses(b, par):
            return (b - par) // 2 + 1 if isinstance(b, int) else None

        def per_use(b, par, n):
            if isinstance(b, int):
                return ((b - par) // 2 + 1) * n
            return (b - par) * (n // 2) + n

        def load(engine, name, pairs):
            for dst, src in pairs:
                few = src.shape[-1] * src.shape[0] <= 1024 or len(src.shape) == 2 and src.shape[1] <= 8
                engine.dma_start(dst, src, allow_slow_non_contiguous=few).then_inc(sem(name), 16)

        def head_rows(w, two, rows):
            return w.rearrange("(k h) e -> h k e", h=2 * rows)[two * rows:(two + 1) * rows]

        def sync_load_context(sp, layer, b, par):
            wait_apart(sp, "sp", (sem(f"split_done{layer}"), b - 1))
            sp.dma_start(c_in[par][:], ctx_in[b].rearrange("(p c) e -> p c e", c=KC))\
                .then_inc(sem(f"ctx_in{layer}_{par}"), 16)

        def sync_load_mask(sp, b):
            wait_apart(sp, "sp", (sem("mask_done"), b))
            for two in range(2):
                sp.dma_start(mask_in[two * S:(two + 1) * S, :], mask[b, 0]).then_inc(sem("mask_in"), 16)

        def sync_stack(sp, b, par):
            for each in ((sem("ct_done0_0"), b + 1), (sem("ct_done0_1"), b + 1), (sem("scores0"), (b - 1) * T0)):
                wait_apart(sp, "sp", each)
            for g in range(G):
                for part, low in ((0, 0), (1, 1), (2, 0)):
                    sp.dma_start(c_stack[par][32 * part:32 * part + 32, g],
                                 c_t0[32 * g:32 * g + 32, low]).then_inc(sem(f"stack{par}"), 16)

        @block.sync
        def _(sp):
            load(sp, "in_x", [(x_tok[:], x.rearrange("b s e -> (b s) e").rearrange("(t p) e -> p t e", p=128))])
            for n, w in enumerate((wq0, wk0, wv0)):
                for h in range(H):
                    sp.dma_start(w8[D0 * h:D0 * (h + 1), n, :], w).then_inc(sem("in_w8"), 16)
            load(sp, "in_w0", [(wo0_sb[:], wo0), (bo0_col[:], bo0.rearrange("(e o) -> e o", o=1))])
            sync_load_context(sp, 0, 0, 0)
            sync_load_mask(sp, 0)

            def layer0(b, par, first, last):
                if not last:
                    sync_load_context(sp, 0, b + 1, 1 - par)
                    sync_load_mask(sp, b + 1)
                    sync_stack(sp, b + 1, 1 - par)
            sync_stack(sp, 0, 0)
            batches(sp, layer0)
            wait(sp, sem("split_done0"), B)
            sync_load_context(sp, 1, 0, 0)

            def layer1(b, par, first, last):
                if not last:
                    sync_load_context(sp, 1, b + 1, 1 - par)
            batches(sp, layer1)
            sp.wait_ge(sem("final"), TT)
            for t in range(TT):
                sp.dma_start(out.rearrange("b s e -> (b s) e")[128 * t:128 * (t + 1), :], x_tok[:, t, :])\
                    .then_inc(sem("stored"), 16)
            sp.wait_ge(sem("stored"), 16 * TT)

        def pool_rstd(pool, layer):
            pool.wait_ge(sem("ln_var"), TT * (layer + 1))
            pool.tensor_scalar(rstd[:], mean_var[:, :, 1], EPS, None, ALU.add).then_inc(sem("ln_eps"), 1)
            pool.wait_ge(sem("ln_eps"), layer + 1)
            pool.tensor_tensor(rstd[:], rstd[:], half_neg[:], ALU.pow).then_inc(sem("ln_rstd"), 1)

        @block.gpsimd
        def _(pool):
            for m in (ident, ident16, ident_b):
                pool.memset(m[:], 0.0).then_inc(sem("const_0"), 1)
            pool.memset(ones_f[:], 1.0).then_inc(sem("const_0"), 1)
            pool.memset(half_neg[:], -0.5).then_inc(sem("const_0"), 1)
            pool.memset(head_of[:], 1.0).then_inc(sem("const_0"), 1)
            pool.memset(expert_row[:], 0.0).then_inc(sem("const_0"), 1)
            pool.memset(a_heads[:], 0.0).then_inc(sem("const_0"), 1)
            pool.memset(v_heads[:], 0.0).then_inc(sem("const_0"), 1)
            pool.memset(c_split0[:], 0.0).then_inc(sem("const_0"), 1)
            pool.wait_ge(sem("const_0"), 10)
            for m in (ident, ident16, ident_b):
                pool.affine_select(out=m[:], in_=m[:], compare_op=ALU.not_equal, fill=1.0, base=0,
                                   pattern=[[-1, 128]], channel_multiplier=1).then_inc(sem("const"), 1)
            pool.affine_select(out=head_of[:], in_=head_of[:], compare_op=ALU.is_ge, fill=0.0, base=0,
                               pattern=[[-D0, H]], channel_multiplier=1).then_inc(sem("const"), 1)
            pool.wait_ge(sem("const"), 4)
            pool.affine_select(out=head_of[:], in_=head_of[:], compare_op=ALU.is_ge, fill=0.0, base=D0 - 1,
                               pattern=[[D0, H]], channel_multiplier=-1).then_inc(sem("const"), 1)
            pool.affine_select(out=expert_row[:], in_=expert_row[:], compare_op=ALU.not_equal, fill=1.0, base=0,
                               pattern=[[-1, NE], [0, 128]], channel_multiplier=1).then_inc(sem("const"), 1)
            for e in range(NE):
                pool.memset(expert_id[:, e:e + 1], float(e - NE)).then_inc(sem("const"), 1)
            pool_rstd(pool, 0)

            def split0(b, par):
                wait_apart(pool, "pool", (sem(f"ctx_in0_{par}"), per_use(b, par, 16)), (sem("ct_turned0"), 2 * b))
                high, low = c_split0[0:KP, :, 0, :], c_split0[0:KP, :, 1, :]
                pool.tensor_copy(high, c_in[par][:]).then_inc(sem("high0"), 1)
                pool.wait_ge(sem("high0"), b + 1)
                pool.tensor_tensor(low, c_in[par][:], high, ALU.subtract).then_inc(sem("low0"), 1)
                wait_apart(pool, "pool", (sem("pv_done0"), G * (b - 1)))
                grouped = c_group[par][:]
                for g in range(G):
                    pool.tensor_copy(grouped[:, :, g, 0:32], c_split0[0:KP, :, 0, 32 * g:32 * g + 32])\
                        .then_inc(sem("group_done"), 1)
                wait_apart(pool, "pool", (sem("low0"), b + 1))
                for g in range(G):
                    ins = pool.tensor_copy(grouped[:, :, g, 32:64], c_split0[0:KP, :, 1, 32 * g:32 * g + 32])
                    ins.then_inc(sem("group_done"), 1)
                wait(pool, sem("group_done"), (b + 1) * (2 * G))
                pool.sem_inc(sem("split_done0"), 1)

            def mask0(b, par):
                wait_apart(pool, "pool", (sem("mask_in"), (b + 1) * 32), (sem("max_done0"), (b - 1) * T0))
                pool.tensor_scalar(mask_bias[par][:], mask_in[:].rearrange("q (p c) -> q c p", c=KC),
                                   0.0, NEG, ALU.is_equal, ALU.mult).then_inc(sem("mask_done"), 1)

            split0(0, 0)
            mask0(0, 0)

            def layer0(b, par, first, last):
                if not last:
                    split0(b + 1, 1 - par)
                    mask0(b + 1, 1 - par)
            batches(pool, layer0)
            pool_rstd(pool, 1)
            pool_rstd(pool, 2)
            for p in range(2):
                pool.wait_ge(sem("residual"), TT)
                pool.memset(c_split1[p], 0.0).then_inc(sem("pad1"), 1)

            def layer1(b, par):
                pool.wait_ge(sem("high1"), b + 1)
                high = c_split1[par][0:KP, :, 0, :]
                pool.tensor_tensor(c_split1[par][0:KP, :, 1, :], c_in[par][:], high, ALU.subtract)\
                    .then_inc(sem("split_done1"), 1)
            layer1(0, 0)
            batches(pool, lambda b, par, first, last: None if last else layer1(b + 1, 1 - par))
            pool_rstd(pool, 3)

        def pe_norm_t(pe, layer):
            pe.wait_ge(sem("ln_norm"), TT * (layer + 1))
            wait(pe, sem("const"), 1)
            for t in range(TT):
                pe.transpose(bank[:, t // 4, 128 * (t % 4):128 * (t % 4 + 1)], x_norm[:, t, :], ident[:])\
                    .then_inc(sem("ln_turned"), 1)

        def pe_block_turn(pe, n):
            pe.wait_ge(sem("block_ready"), n + 1)
            for t in range(TT):
                pe.transpose(bank[:, 5 + t // 4, 128 * (t % 4):128 * (t % 4 + 1)],
                             block_t[:, 128 * t:128 * (t + 1)], ident[:]).then_inc(sem("block_turned"), 1)

        def pe_scores0(pe, b, par, t):
            if t == 0:
                pe.wait_ge(sem(f"stack{par}"), per_use(b, par, 12 * 16))
            wait(pe, sem("max_done0"), b * T0 + t)
            for k in range(3):
                last = pe.matmul(bank[0:R0, k, 0:4 * KP], q0[:, b, R0 * t:R0 * (t + 1)],
                                 c_stack[par][:, t // 2, 4 * k:4 * k + 4, 0:KP], start=True, stop=True)
            last.then_inc(sem("scores0"), 1)

        def pe_turn(pe, layer, b, par, t):
            rows, tiles = (R0, T0) if layer == 0 else (128, T1)
            pe.wait_ge(sem("exp_done0" if layer == 0 else "norm_done1"), b * tiles + t + 1)
            for u in range(2):
                wait_pair(pe, layer, b, par, ("turn", t, u))
                n = unit_no(layer, par, ("turn", t, u))
                for c in range(UC):
                    k = UC * u + c
                    last = pe.transpose(pair(n)[0:KP, c // 4, 128 * (c % 4):128 * (c % 4) + rows],
                                        e_row[(t + par * (tiles % 2)) % 2][0:rows, KP * k:KP * (k + 1)],
                                        ident[0:rows, 0:rows])
                last.then_inc(sem(f"turned{layer}"), 1)

        def pe_prep(pe, layer, b, par):
            src = c_split0 if layer == 0 else c_split1[par]
            for n in range(2):
                if isinstance(b, int) and b == 0:
                    if n == 0:
                        wait(pe, sem("const"), 3)
                else:
                    wait_pair(pe, layer, b - 1, 1 - par, ("prep", n, 0))
                if layer == 0:
                    pe.wait_ge(sem("low0" if n else "high0"), b + 1)
                else:
                    pe.wait_ge(sem("split_done1" if n else "high1"), b + 1)
                no = unit_no(layer, 1 - par, ("prep", n, 0)) if not (isinstance(b, int) and b == 0) else \
                    len(UNITS[layer]) + 1 - 2 + n
                for c in range(KC):
                    last = pe.transpose(pair_flat(no, F16)[:, 128 * c:128 * (c + 1)], src[:, c, n, :], ident16[:])
                last.then_inc(sem(f"ct_turned{layer}"), 1)

        def pe_pv0(pe, b, par, g, part):
            if part == 0:
                pe.wait_ge(sem("low_done0"), b * (2 * T0) + 4 * (g + 1))
                wait(pe, sem("u_done0"), b * G + g)
                pe.wait_ge(sem("group_done"), (b + 1) * (2 * G))
            for c in range(UC * part, UC * part + UC):
                for lo, p in ((0, p_high0), (64, p_low0)):
                    last = pe.matmul(bank[lo:lo + 64, U_BANK, 0:GC], c_group[par][:, c, g, :],
                                     p[g % 2][:, c, :], start=(c == 0), stop=(c == KC - 1))
            if part == 1:
                last.then_inc(sem("pv_done0"), 1)
                pe.wait_ge(sem("inv_done0"), b * G + g + 1)
                for n in range(2):
                    t = 2 * g + n
                    last = pe.matmul(bank[:, U_BANK, 256 + R0 * n:256 + R0 * (n + 1)],
                                     row_inv[0:R0, t:t + 1].broadcast_to((R0, 128)),
                                     ident[0:R0, 0:R0], start=True, stop=True)
                last.then_inc(sem("inv_spread"), 1)

        def pe_proj(pe, layer, b, par):
            pe.wait_ge(sem("u_done0"), b * G) if layer == 0 else pe.wait_ge(sem("u_done1"), b * 2)
            wait_pair(pe, layer, b, par, ("proj", 0, 0))
            n = unit_no(layer, par, ("proj", 0, 0))
            for h in range(H):
                rhs = u0[:, h // HG, S * (h % HG):S * (h % HG + 1)] if layer == 0 else u1[:, S * h:S * (h + 1)]
                last = pe.matmul(pair(n)[:, 0, 0:S], (out0_w if layer == 0 else out1_w)[:, h, :], rhs,
                                 start=(h == 0), stop=(h == H - 1))
            last.then_inc(sem(f"projected{layer}"), 1)

        def pe_scores1(pe, b, par, t):
            if t == 0:
                for n in range(2):
                    pe.wait_ge(sem(f"ct_done1_{n}"), b + 1)
            wait(pe, sem("exp_done1"), b * T1 + t)
            for ql, cls in ((0, (0, 1)), (1, (0,))):
                for cl in cls:
                    for k in range(3):
                        last = pe.matmul(bank[:, k, 0:4 * KP], q1[:, ql, b, 128 * t:128 * (t + 1)],
                                         c_t1[par][:, cl, 4 * k:4 * k + 4, 0:KP],
                                         start=(ql == 0 and cl == 0), stop=(ql == 1))
            last.then_inc(sem("scores1"), 1)

        def pe_pv1(pe, b, par, grp, part):
            a, z = GROUPS1[grp]
            cols = 128 * (z - a)
            if part == 0:
                pe.wait_ge(sem("low_done1"), b * (2 * T1) + 2 * z)
                wait(pe, sem("u_done1"), b * 2 + grp)
            for c in range(4 * part, 4 * part + 4):
                for cl, p in ((0, p_high1), (0, p_low1), (1, p_high1)):
                    last = pe.matmul(bank[:, U_BANK, 0:cols], c_split1[par][0:KP, c, cl, :], p[grp][:, c, :],
                                     start=(c == 0 and cl == 0 and p is p_high1),
                                     stop=(c == KC - 1 and cl == 1))
            if part == 2:
                last.then_inc(sem("pv_done1"), 1)

        @block.tensor
        def _(pe):
            pe_norm_t(pe, 0)
            pe.wait_ge(sem("diag"), 3)
            pe.matmul(bank[:, 2, 0:E], block_diag[:, 0, :], block_diag[:, 1, :], start=True, stop=True)\
                .then_inc(sem("w0_a"), 1)
            pe.wait_ge(sem("in_w0"), 32)
            pe.transpose(bank[:, 3, 0:E], wo0_sb[:], ident[:]).then_inc(sem("w0_wo"), 1)
            pe.wait_ge(sem("w0_sb"), 8)
            for h in range(H):
                last = pe.matmul(bank[:, 4 + h // 4, 128 * (h % 4):128 * (h % 4 + 1)],
                                 v_heads[:, h].rearrange("p a b -> p (a b)"), wo0_t[:], start=True, stop=True)
            last.then_inc(sem("w0_out"), 1)
            pe.wait_ge(sem("ln_t"), 2)
            for n in range(2 * H):
                h, half = n // 2, n % 2
                if n >= 4:
                    pe.wait_ge(sem("q0_low"), n - 3)
                pe.matmul(bank[0:96, n % 4, 0:HALF], a_heads[:, h].rearrange("p a b -> p (a b)"),
                          x_norm_t[:, HALF * half:HALF * (half + 1)], start=True, stop=True)\
                    .then_inc(sem("q0_made"), 1)
            pe.wait_ge(sem("q0_low"), 2 * H)
            pe.wait_ge(sem("w0_out_sb"), 1)
            pe_prep(pe, 0, 0, 0)
            pe_scores0(pe, 0, 0, 0)

            def layer0(b, par, first, last):
                for t in range(T0):
                    if t < T0 - 1:
                        pe_scores0(pe, b, par, t + 1)
                    elif not last:
                        pe_scores0(pe, b + 1, 1 - par, 0)
                    pe_turn(pe, 0, b, par, t)
                    g = t // 2 - 1
                    if g >= 0:
                        pe_pv0(pe, b, par, g, t % 2)
                    elif not first:
                        pe_pv0(pe, b - 1, 1 - par, G - 1, t % 2)
                    if t == PROJ_AT and not first:
                        pe_proj(pe, 0, b, par)
                    if t == PREP_AT and not last:
                        pe_prep(pe, 0, b + 1, 1 - par)
            batches(pe, layer0)
            for part in range(2):
                pe_pv0(pe, B - 1, 1, G - 1, part)
            pe_proj(pe, 0, B, 0)

            pe_block_turn(pe, 0)
            pe_norm_t(pe, 1)
            pe.wait_ge(sem("in_ffn0"), 16 * 5)
            pe.wait_ge(sem("in_down0"), 16 * 2)
            pe.wait_ge(sem("ln_t"), 4)
            for t in range(TT):
                last = pe.matmul(bank[:, 2, NE * t:NE * (t + 1)], x_norm_t[:, 128 * t:128 * (t + 1)],
                                 gate_w_sb[:], start=True, stop=True)
            last.then_inc(sem("logits"), 1)
            pe.wait_ge(sem("one_hot"), 1)
            for t in range(TT):
                last = pe.transpose(bank[0:NE, 3 + t // 4, 128 * (t % 4):128 * (t % 4 + 1)], one_hot[:, t, :], ident[:])
            last.then_inc(sem("hot_turned"), 1)
            pe.wait_ge(sem("x_scored"), 1)
            for t in range(TT):
                last = pe.transpose(bank[:, 5 + t // 4, 128 * (t % 4):128 * (t % 4 + 1)], x_norm[:, t, :], ident[:])
            last.then_inc(sem("xs_turned"), 1)
            pe.wait_ge(sem("hot_t"), 1)

            pe.wait_ge(sem("xs_t"), 1)

            def hot_rows(n):
                half, e = n // (NE + 1), n % (NE + 1)
                if e < NE:
                    r = half * NE + e
                    wait(pe, sem("x_exp"), r)
                    pe.matmul(bank[:, 0, 0:HALF], expert_row[:, e, :], one_hot_t[:, HALF * half:HALF * (half + 1)],
                              start=True, stop=True).then_inc(sem("hot_rows"), 1)

            def down(m):
                n, ic = m // IC, m % IC
                half, e = n // (NE + 1), n % (NE + 1)
                pe.wait_ge(sem("act0"), m + 1)
                last = pe.matmul(bank[:, 5 + half, 0:HALF], d_w[:, e, ic, :], act0[:, m % 2, :],
                                 start=(e == 0 and ic == 0), stop=(e == NE and ic == IC - 1))
                last.then_inc(sem("down0"), 1)

            hot_rows(0)
            for m in range(2 * (NE + 1) * IC):
                n, ic = m // IC, m % IC
                half, e = n // (NE + 1), n % (NE + 1)
                if ic == 0:
                    if n + 1 < 2 * (NE + 1):
                        hot_rows(n + 1)
                    if e < NE:
                        pe.wait_ge(sem("x_exp"), half * NE + e + 1)
                moving = x_exp[:, (half * NE + e) % 2, :] if e < NE else x_norm_t[:, HALF * half:HALF * (half + 1)]
                wait(pe, sem("act0"), m - 1)
                for w, at in ((g_w, 0), (u_w, 1)):
                    pe.matmul(bank[:, 1 + 2 * (m % 2) + at, 0:HALF], w[:, e, 128 * ic:128 * (ic + 1)], moving,
                              start=True, stop=True).then_inc(sem("up0"), 1)
                if m >= 1:
                    down(m - 1)
            down(2 * (NE + 1) * IC - 1)
            pe.wait_ge(sem("block_out"), 2)
            pe_block_turn(pe, 1)

            pe.wait_ge(sem("in_w1"), 16 * 8)
            pe.wait_ge(sem("in_bv"), 16 * 2)
            for n in range(16):
                src = (wq1_sb if n < 8 else wo1_sb)[:, n % 8, :]
                pe.transpose(bank[:, n // 4, 128 * (n % 4):128 * (n % 4 + 1)], src, ident[:])\
                    .then_inc(sem("w1_turned"), 1)
            pe.wait_ge(sem("w1_t"), 4)
            for h in range(H):
                lo, k = 64 * (h % 2), h // 2
                last = pe.matmul(bank[:, 2 * (h % 2) + k // 4, 128 * (k % 4):128 * (k % 4 + 1)], wv1_sb[lo:lo + 64, h // 2, :],
                                 wo1_t[lo:lo + 64, h // 2, :], start=True, stop=True)
            last.then_inc(sem("w1_out"), 1)
            for k in range(8):
                last = pe.matmul(bank[:, 4, 0:1], wo1_t[:, k, :], bv1_col[:, k:k + 1], start=(k == 0), stop=(k == 7))
            last.then_inc(sem("w1_bias"), 1)
            pe.wait_ge(sem("w1_out_sb"), 4)
            pe_norm_t(pe, 2)
            pe.wait_ge(sem("ln_t"), 6)
            for n in range(16):
                k, half = n // 2, n % 2
                if n >= 4:
                    pe.wait_ge(sem("q1_proj"), n - 3)
                pe.matmul(bank[:, n % 4, 0:HALF], wq1_t[:, k, :], x_norm_t[:, HALF * half:HALF * (half + 1)],
                          start=True, stop=True).then_inc(sem("q1_made"), 1)
            for n in range(2 * H):
                h, half = n // 2, n % 2
                lo = 64 * (h % 2)
                pe.wait_ge(sem("q1_proj"), 16 if n < 4 else 16)
                if n >= 4:
                    pe.wait_ge(sem("q1_low"), n - 3)
                pe.matmul(bank[:, n % 4, 0:HALF], wk1_sb[lo:lo + 64, h // 2, :],
                          q1_proj[lo:lo + 64, h // 2, HALF * half:HALF * (half + 1)], start=True, stop=True)\
                    .then_inc(sem("qk1_made"), 1)
            pe.wait_ge(sem("q1_low"), 2 * H)
            pe_prep(pe, 1, 0, 0)
            pe_scores1(pe, 0, 0, 0)

            def layer1(b, par, first, last):
                for t in range(T1):
                    if t < T1 - 1:
                        pe_scores1(pe, b, par, t + 1)
                    elif not last:
                        pe_scores1(pe, b + 1, 1 - par, 0)
                    pe_turn(pe, 1, b, par, t)
                    if t < 3 and not first:
                        pe_pv1(pe, b - 1, 1 - par, 1, t)
                    if t >= 4:
                        pe_pv1(pe, b, par, 0, t - 4)
                    if t == 3 and not first:
                        pe_proj(pe, 1, b, par)
                    if t == PREP1_AT and not last:
                        pe_prep(pe, 1, b + 1, 1 - par)
            batches(pe, layer1)
            for part in range(3):
                pe_pv1(pe, B - 1, 1, 1, part)
            pe_proj(pe, 1, B, 0)

            pe_block_turn(pe, 2)
            pe.wait_ge(sem("w_abs"), 3)
            pe.matmul(bank[:, 0, 0:3], ones_f[:], abs_sum[:], start=True, stop=True).then_inc(sem("w_abs_all"), 1)
            pe.wait_ge(sem("w_tern"), 3)
            for n in range(3):
                for j in range(JC):
                    last = pe.transpose(bank[:, 1 + n, 0:256].bitcast(BF16)[:, 128 * j:128 * (j + 1)],
                                        w_tern[:, n, j, :], ident_b[:])
                last.then_inc(sem("w_turned"), 1)
            pe.wait_ge(sem("xq"), 1)
            for t in range(TT):
                last = pe.transpose(bank[:, 4, :].bitcast(BF16)[:, 128 * t:128 * (t + 1)], xq[:, t, :], ident_b[:])
            last.then_inc(sem("xq_turned"), 1)
            pe.wait_ge(sem("w_t"), 3)
            pe.wait_ge(sem("xq_t"), 1)

            def up1(t):
                wait(pe, sem("act1"), t - 1)
                for n in range(2):
                    pe.matmul(bank[:, 2 * (t % 2) + n, :], xq_t[:, t, :],
                              w_tern_t[:, n].rearrange("p a b -> p (a b)"), start=True, stop=True)\
                        .then_inc(sem("up1"), 1)

            def down1(t):
                pe.wait_ge(sem("hq"), t + 1)
                for j in range(JC):
                    last = pe.transpose(bank[:, 4 + t % 2, :].bitcast(BF16)[:, 128 * j:128 * (j + 1)],
                                        hq[:, t % 2, 128 * j:128 * (j + 1)], ident_b[:])
                last.then_inc(sem("hq_turned"), 1)
                pe.wait_ge(sem("hq_t"), t + 1)
                wait(pe, sem("final"), t - 1)
                for j in range(JC):
                    last = pe.matmul(bank[:, 6 + t % 2, 0:128], hq_t[:, t % 2, j, :], w_tern_t[:, 2, j, :],
                                     start=(j == 0), stop=(j == JC - 1))
                last.then_inc(sem("down1"), 1)

            up1(0)
            for t in range(TT):
                if t + 1 < TT:
                    up1(t + 1)
                down1(t)

        def act_norm_t(act, layer):
            for n in range(2):
                act.wait_ge(sem("ln_turned"), TT * layer + (4 if n == 0 else TT))
                cols = 512 if n == 0 else NTOK - 512
                act.copy(x_norm_t[:, 512 * n:512 * n + cols], bank[:, n, 0:cols]).then_inc(sem("ln_t"), 1)

        def act_exp0(act, b, par, t):
            act.wait_ge(sem("max_done0"), b * T0 + t + 1)
            wait(act, sem("turned0"), (b * T0 + t - 1) * 2)
            act.activation(e_row[t % 2][0:R0, :], masked[t % 2][:], ACT.Exp, bias=neg_max[0:R0, t:t + 1],
                           scale=-1.0, accum_out=row_sum[0:R0, t:t + 1]).then_inc(sem("exp_done0"), 1)

        def act_high0(act, b, par, t):
            g = t // 2
            for u in range(2):
                act.wait_ge(sem("turned0"), (b * T0 + t) * 2 + u + 1)
                if t % 2 == 0 and u == 0:
                    wait(act, sem("pv_done0"), b * G + g - 1)
                act.activation(p_high0[g % 2][:, UC * u:UC * (u + 1), R0 * (t % 2):R0 * (t % 2 + 1)],
                               pair_chunks(unit_no(0, par, ("turn", t, u)), R0), ACT.Copy, scale=PSCALE)\
                    .then_inc(sem("high_done0"), 1)

        def act_inv0(act, b, par, g):
            act.wait_ge(sem("inv_spread"), b * G + g + 1)
            wait(act, sem("u_done0"), b * G + g)
            act.copy(inv_b[:], bank[:, U_BANK, 256:256 + GC]).then_inc(sem("inv_sb"), 1)

        def act_block(act, layer, b, par):
            act.wait_ge(sem(f"projected{layer}"), b)
            act.activation(block_t[:, bass.ds((b - 1) * S, S)], pair(unit_no(layer, par, ("proj", 0, 0)))[:, 0, 0:S],
                           ACT.Identity, bias=(bo0_col if layer == 0 else bias1)[:]).then_inc(sem(f"block_done{layer}"), 1)

        def act_exp1(act, b, par, t):
            act.wait_ge(sem("max_done1"), b * T1 + t + 1)
            wait(act, sem("turned1"), (b * T1 + t - 1) * 2)
            act.activation(e_row[(t + par) % 2][:], bank[:, 0:3, 0:4 * KP], ACT.Exp, bias=neg_max[:, t:t + 1],
                           accum_out=row_sum[:, t:t + 1]).then_inc(sem("exp_done1"), 1)

        def act_high1(act, b, par, t):
            grp = 0 if t < 4 else 1
            at = t - GROUPS1[grp][0]
            for u in range(2):
                act.wait_ge(sem("turned1"), (b * T1 + t) * 2 + u + 1)
                if at == 0 and u == 0:
                    wait(act, sem("pv_done1"), (b - 1) * 2 + grp + 1)
                act.copy(p_high1[grp][:, UC * u:UC * (u + 1), 128 * at:128 * (at + 1)],
                         pair_chunks(unit_no(1, par, ("turn", t, u)), 128)).then_inc(sem("high_done1"), 1)

        def act_u1(act, b, par, grp):
            a, z = GROUPS1[grp]
            act.wait_ge(sem("pv_done1"), b * 2 + grp + 1)
            if grp == 0:
                wait(act, sem("projected1"), b)
            act.activation(u1[:, 128 * a:128 * z], bank[:, U_BANK, 0:128 * (z - a)], ACT.Copy, scale=1.0 / PSCALE)\
                .then_inc(sem("u_done1"), 1)

        def act_split1(act, b, par):
            act.wait_ge(sem(f"ctx_in1_{par}"), per_use(b, par, 16))
            wait(act, sem("pv_done1"), (b - 1) * 2)
            act.copy(c_split1[par][0:KP, :, 0, :], c_in[par][:]).then_inc(sem("high1"), 1)

        @block.scalar
        def _(act):
            load(act, "in_gates", [(gates[:, 0:2], g_xattn.rearrange("(o n) -> o n", o=1).broadcast_to((128, 2))),
                                   (gates[:, 2:4], g_ffn.rearrange("(o n) -> o n", o=1).broadcast_to((128, 2)))])
            load(act, "in_ffn0", [
                (gate_w_sb[:], gate_w),
                (g_w[:, 0:NE, :], rt_gate.rearrange("e h i -> h e i")), (g_w[:, NE, :], sh_gate),
                (u_w[:, 0:NE, :], rt_up.rearrange("e h i -> h e i")), (u_w[:, NE, :], sh_up)])
            bkv = bkv1.rearrange("(k two part d) -> two part d k", two=2, part=2, d=D1)
            load(act, "in_w1", [(bq1_col[:], bq1.rearrange("(k p) -> p k", p=128)),
                                (bo1_col[:], bo1.rearrange("(e o) -> e o", o=1))])
            for two in range(2):
                load(act, "in_bv", [(bv1_col[64 * two:64 * two + 64], bkv[two, 1])])
            load(act, "in_wf", [(wg_sb[:, 0], w_gate.rearrange("(j p) h -> p j h", p=128)),
                                (wg_sb[:, 1], w_up.rearrange("(j p) h -> p j h", p=128)),
                                (wg_sb[:, 2], w_down.rearrange("h (j p) -> h j p", p=128))])
            act.wait_ge(sem("in_gates"), 32)
            act.activation(tanh_g[:], gates[:], ACT.Tanh).then_inc(sem("tanh_g"), 1)
            act_norm_t(act, 0)
            act.wait_ge(sem("w0_wo"), 1)
            act.copy(wo0_t[:], bank[:, 3, 0:E]).then_inc(sem("w0_sb"), 1)
            act.wait_ge(sem("w0_out"), 1)
            act.copy(out0_w[:].rearrange("p (a h) e -> p a (h e)", a=4), bank[:, 4:8, :]).then_inc(sem("w0_out_sb"), 1)
            for n in range(2 * H):
                h, half = n // 2, n % 2
                act.wait_ge(sem("q0_made"), n + 1)
                act.copy(q0[:, 8 * half:8 * half + 8, S * h:S * (h + 1)],
                         bank[0:96, n % 4, 0:HALF].rearrange("p (b s) -> p b s", s=S)).then_inc(sem("q0_high"), 1)

            def layer0(b, par, first, last):
                for t in range(T0):
                    if t % 2 == 0 and t >= 4:
                        act_inv0(act, b, par, t // 2 - 2)
                    elif t % 2 == 0 and not first:
                        act_inv0(act, b - 1, 1 - par, t // 2 + 2)
                    act_high0(act, b, par, t)
                    if t < T0 - 1:
                        act_exp0(act, b, par, t + 1)
                    elif not last:
                        act_exp0(act, b + 1, 1 - par, 0)
                    if t == PROJ_AT and not first:
                        act_block(act, 0, b, par)
            act_exp0(act, 0, 0, 0)
            batches(act, layer0)
            act_inv0(act, B - 1, 1, 2)
            act_inv0(act, B - 1, 1, 3)
            act.wait_ge(sem("projected0"), B)
            act.activation(block_t[:, (B - 1) * S:B * S], pair(unit_no(0, 0, ("proj", 0, 0)))[:, 0, 0:S],
                           ACT.Identity, bias=bo0_col[:]).then_inc(sem("block_ready"), 1)

            act.wait_ge(sem("block_ready"), 1)
            load(act, "in_down0", [
                (d_w[:, 0:NE].rearrange("p e c h -> p (e c) h"), rt_down.rearrange("e (c p) h -> p (e c) h", p=128)),
                (d_w[:, NE], sh_down.rearrange("(c p) h -> p c h", p=128))])
            load(act, "in_w1", [
                (wq1_sb[:], wq1.rearrange("(k p) e -> p k e", p=128)),
                (wo1_sb[:], wo1.rearrange("e (k p) -> e k p", p=128))])
            kv = wkv1.rearrange("(k two part d) e -> two part d k e", two=2, part=2, d=D1)
            for two in range(2):
                load(act, "in_w1", [(wk1_sb[64 * two:64 * two + 64], kv[two, 0]), (wv1_sb[64 * two:64 * two + 64], kv[two, 1])])

            act_norm_t(act, 1)
            act.wait_ge(sem("top"), 1)
            act.activation(score[:], top[:], ACT.Exp, scale=-1.0).then_inc(sem("score_exp"), 1)
            act.wait_ge(sem("hot_turned"), 1)
            for n in range(2):
                cols = 512 if n == 0 else NTOK - 512
                last = act.copy(one_hot_t[:, 512 * n:512 * n + cols], bank[0:NE, 3 + n, 0:cols])
            last.then_inc(sem("hot_t"), 1)
            act.wait_ge(sem("xs_turned"), 1)
            for n in range(2):
                cols = 512 if n == 0 else NTOK - 512
                last = act.copy(x_score_t[:, 512 * n:512 * n + cols], bank[:, 5 + n, 0:cols])
            last.then_inc(sem("xs_t"), 1)
            for m in range(2 * (NE + 1) * IC):
                act.wait_ge(sem("up0"), 2 * m + 1)
                wait(act, sem("act0"), m - 1)
                act.activation(silu0[:, m % 2, :], bank[:, 1 + 2 * (m % 2), 0:HALF], ACT.Silu).then_inc(sem("silu0"), 1)
            act.wait_ge(sem("down0"), 2 * (NE + 1) * IC)
            for half in range(2):
                last = act.copy(block_t[:, HALF * half:HALF * (half + 1)], bank[:, 5 + half, 0:HALF])
                last.then_inc(sem("block_out"), 1)
            act.wait_ge(sem("block_out"), 2)
            act.sem_inc(sem("block_ready"), 1)

            act.wait_ge(sem("w1_turned"), 16)
            for n in range(4):
                dst = (wq1_t if n < 2 else wo1_t)[:, 4 * (n % 2):4 * (n % 2) + 4, :]
                act.copy(dst.rearrange("p a b -> p (a b)"), bank[:, n, :]).then_inc(sem("w1_t"), 1)
            act.wait_ge(sem("w1_out"), 1)
            for n in range(4):
                act.copy(out1_w[:].rearrange("p (k two) e -> p two k e", two=2)[:, n // 2, 4 * (n % 2):4 * (n % 2) + 4, :],
                         bank[:, n, :].rearrange("p (k e) -> p k e", k=4))\
                    .then_inc(sem("w1_out_sb"), 1)
            act.wait_ge(sem("w1_bias"), 1)
            act.activation(bias1[:], bank[:, 4, 0:1], ACT.Identity, bias=bo1_col[:]).then_inc(sem("bias1"), 1)
            act_norm_t(act, 2)
            for n in range(16):
                k, half = n // 2, n % 2
                act.wait_ge(sem("q1_made"), n + 1)
                act.activation(q1_proj[:, k, HALF * half:HALF * (half + 1)], bank[:, n % 4, 0:HALF], ACT.Identity,
                               bias=bq1_col[:, k:k + 1]).then_inc(sem("q1_proj"), 1)
            for n in range(2 * H):
                h, half = n // 2, n % 2
                act.wait_ge(sem("qk1_made"), n + 1)
                act.activation(q1[:, 0, 8 * half:8 * half + 8, S * h:S * (h + 1)],
                               bank[:, n % 4, 0:HALF].rearrange("p (b s) -> p b s", s=S), ACT.Copy, scale=SCALE1)\
                    .then_inc(sem("q1_high"), 1)
            act.wait_ge(sem("pad1"), 2)
            act_split1(act, 0, 0)

            def layer1(b, par, first, last):
                for t in range(T1):
                    if t == 0 and not first:
                        act_u1(act, b - 1, 1 - par, 0)
                    if t == 3 and not first:
                        act_u1(act, b - 1, 1 - par, 1)
                    if t == 4 and not first:
                        act_block(act, 1, b, par)
                    act_high1(act, b, par, t)
                    if t < T1 - 1:
                        act_exp1(act, b, par, t + 1)
                    elif not last:
                        act_exp1(act, b + 1, 1 - par, 0)
                    if t == 3 and not last:
                        act_split1(act, b + 1, 1 - par)
            act_exp1(act, 0, 0, 0)
            batches(act, layer1)
            act_u1(act, B - 1, 1, 0)
            act_u1(act, B - 1, 1, 1)
            act.wait_ge(sem("projected1"), B)
            act.activation(block_t[:, (B - 1) * S:B * S], pair(unit_no(1, 0, ("proj", 0, 0)))[:, 0, 0:S],
                           ACT.Identity, bias=bias1[:]).then_inc(sem("block_ready"), 1)

            act.wait_ge(sem("w_turned"), 3)
            for n in range(3):
                act.copy(w_tern_t[:, n].rearrange("p a b -> p (a b)"), bank[:, 1 + n, 0:256].bitcast(BF16))\
                    .then_inc(sem("w_t"), 1)
            act.wait_ge(sem("xq_turned"), 1)
            act.copy(xq_t[:].rearrange("p a b -> p (a b)"), bank[:, 4, 0:448].bitcast(BF16)).then_inc(sem("xq_t"), 1)

            def turned_h(t):
                act.wait_ge(sem("hq_turned"), t + 1)
                wait(act, sem("down1"), t - 1)
                act.copy(hq_t[:, t % 2].rearrange("p a b -> p (a b)"), bank[:, 4 + t % 2, 0:256].bitcast(BF16))\
                    .then_inc(sem("hq_t"), 1)
            for t in range(TT):
                act.wait_ge(sem("up1"), 2 * t + 1)
                wait(act, sem("act1"), t - 1)
                act.activation(silu1[:, t % 2, :], bank[:, 2 * (t % 2), :], ACT.Silu, scale=x_deq[:, t, 0:1])\
                    .then_inc(sem("silu1"), 1)
                if t >= 1:
                    turned_h(t - 1)
            turned_h(TT - 1)

        def dve_norm(dve, layer):
            for t in range(TT):
                if layer == 0:
                    dve.wait_ge(sem("in_x"), 16)
                else:
                    dve.wait_ge(sem("residual"), TT * (layer - 1) + t + 1)
                dve.bn_stats(stats[:, t, :], x_tok[:, t, :]).then_inc(sem("ln_stats"), 1)
            for t in range(TT):
                dve.wait_ge(sem("ln_stats"), TT * layer + t + 1)
                dve.bn_aggr(mean_var[:, t, :], stats[:, t, :]).then_inc(sem("ln_var"), 1)
            dve.wait_ge(sem("ln_rstd"), layer + 1)
            if layer == 2:
                dve.wait_ge(sem("xs_turned"), 1)
            for t in range(TT):
                dve.tensor_scalar(x_norm[:, t, :], x_tok[:, t, :], mean_var[:, t, 0:1], rstd[:, t:t + 1],
                                  ALU.subtract, ALU.mult).then_inc(sem("ln_norm"), 1)

        def dve_residual(dve, n, gate):
            for t in range(TT):
                dve.wait_ge(sem("block_turned"), TT * n + TT)
                dve.scalar_tensor_tensor(x_tok[:, t, :], bank[:, 5 + t // 4, 128 * (t % 4):128 * (t % 4 + 1)],
                                         tanh_g[:, gate:gate + 1], x_tok[:, t, :], ALU.mult, ALU.add)\
                    .then_inc(sem("residual"), 1)

        def dve_max0(dve, b, par, t):
            if t == 0:
                dve.wait_ge(sem("mask_done"), b + 1)
            wait_apart(dve, "dve", (sem("scores0"), b * T0 + t + 1), (sem("exp_done0"), b * T0 + t - 1))
            dve.tensor_tensor_reduce(out=masked[t % 2][:].rearrange("p (a k) -> p a k", a=3),
                                     in0=bank[0:R0, 0:3, 0:4 * KP],
                                     in1=mask_bias[par][:].rearrange("p (a c) k -> p a (c k)", a=3),
                                     scale=-SCALE0, scalar=3.0e38, op0=ALU.add, op1=ALU.min,
                                     accum_out=neg_max[0:R0, t:t + 1]).then_inc(sem("max_done0"), 1)

        def dve_low0(dve, b, par, t):
            g = t // 2
            for u in range(2):
                dve.wait_ge(sem("high_done0"), (b * T0 + t) * 2 + u + 1)
                cols = slice(R0 * (t % 2), R0 * (t % 2 + 1))
                dve.scalar_tensor_tensor(p_low0[g % 2][:, UC * u:UC * (u + 1), cols],
                                         pair_chunks(unit_no(0, par, ("turn", t, u)), R0), PSCALE,
                                         p_high0[g % 2][:, UC * u:UC * (u + 1), cols], ALU.mult, ALU.subtract)\
                    .then_inc(sem("low_done0"), 1)

        def dve_inv0(dve, b, par, g):
            dve.wait_ge(sem("exp_done0"), b * T0 + 2 * g + 2)
            wait(dve, sem("inv_spread"), (b - 1) * G + g + 1)
            dve.tensor_scalar(row_sum[0:R0, 2 * g:2 * g + 2], row_sum[0:R0, 2 * g:2 * g + 2], PSCALE, None, ALU.mult)\
                .then_inc(sem("sum_scaled"), 1)
            dve.wait_ge(sem("sum_scaled"), b * G + g + 1)
            dve.reciprocal(row_inv[0:R0, 2 * g:2 * g + 2], row_sum[0:R0, 2 * g:2 * g + 2]).then_inc(sem("inv_done0"), 1)

        def dve_u0(dve, b, par, g):
            dve.wait_ge(sem("inv_sb"), b * G + g + 1)
            if g == 0:
                wait(dve, sem("projected0"), b)
            dve.tensor_tensor(u0[:, g, :], bank[:, U_BANK, 0:GC], inv_b[:], ALU.mult).then_inc(sem("u_done0"), 1)

        def dve_context(dve, layer, b, par):
            dst = c_t0 if layer == 0 else c_t1[par]
            first = isinstance(b, int) and b == 0
            for n in range(2):
                dve.wait_ge(sem(f"ct_turned{layer}"), 2 * b + n + 1)
                if layer == 0 and n == 0 and not first:
                    dve.wait_ge(sem(f"stack{1 - par}"), per_use(b - 1, 1 - par, 12 * 16))
                if layer == 1 and n == 0:
                    wait(dve, sem("scores1"), (b - 1) * T1)
                no = unit_no(layer, 1 - par, ("prep", n, 0)) if not first else len(UNITS[layer]) - 1 + n
                dve.tensor_copy(dst[:, n].rearrange("p c k -> p (c k)"), pair_flat(no, F16)[:, 0:KC * 128])\
                    .then_inc(sem(f"ct_done{layer}_{n}"), 1)

        def dve_max1(dve, b, par, t):
            dve.wait_ge(sem("scores1"), b * T1 + t + 1)
            wait(dve, sem("exp_done1"), (b - 1) * T1 + t + 1)
            dve.tensor_reduce(neg_max[:, t:t + 1], bank[:, 0:3, 0:4 * KP], AX.XY, ALU.max, negate=True)\
                .then_inc(sem("max_done1"), 1)

        def dve_norm1(dve, b, par, t):
            dve.wait_ge(sem("exp_done1"), b * T1 + t + 1)
            dve.reciprocal(row_inv[:, t:t + 1], row_sum[:, t:t + 1]).then_inc(sem("inv_done1"), 1)
            dve.wait_ge(sem("inv_done1"), b * T1 + t + 1)
            e = e_row[(t + par) % 2][:]
            dve.tensor_scalar(e, e, row_inv[:, t:t + 1], PSCALE, ALU.mult, ALU.mult).then_inc(sem("norm_done1"), 1)

        def dve_low1(dve, b, par, t):
            grp = 0 if t < 4 else 1
            at = t - GROUPS1[grp][0]
            for u in range(2):
                dve.wait_ge(sem("high_done1"), (b * T1 + t) * 2 + u + 1)
                part = (slice(None), slice(UC * u, UC * (u + 1)), slice(128 * at, 128 * (at + 1)))
                dve.tensor_tensor(p_low1[grp][part], pair_chunks(unit_no(1, par, ("turn", t, u)), 128),
                                  p_high1[grp][part], ALU.subtract).then_inc(sem("low_done1"), 1)

        @block.vector
        def _(dve):
            dve_norm(dve, 0)
            dve.wait_ge(sem("in_w8"), 16 * 3 * H)
            dve.wait_ge(sem("const"), 6 + NE)
            for n in range(3):
                dve.tensor_tensor(block_diag[:, n, :].rearrange("p (h d) -> p h d", d=D0),
                                  w8[:, n, :].unsqueeze(1).broadcast_to((128, H, D0)),
                                  head_of[:].unsqueeze(2).broadcast_to((128, H, D0)), ALU.mult).then_inc(sem("diag"), 1)
            dve.wait_ge(sem("diag"), 3)
            dve.wait_ge(sem("w0_a"), 1)
            for heads, parts, src in ((a_heads, 3, bank[:, 2, 0:E]), (v_heads, 4, block_diag[:, 2, :])):
                for part in range(parts):
                    for g in range(G):
                        base = heads[:, HG * g:HG * (g + 1), part, :].rearrange("p h k -> p h k")
                        dst = diagonal(base)
                        dve.tensor_copy(dst, src.rearrange("p (g h d) -> p g h d", g=G, d=D0)[:, g])\
                            .then_inc(sem("w0_place"), 1)
            dve.wait_ge(sem("w0_place"), 7 * G)
            for _ in range(7):
                dve.sem_inc(sem("w0_sb"), 1)
            for n in range(2 * H):
                h, half = n // 2, n % 2
                dve.wait_ge(sem("q0_high"), n + 1)
                low = q0[64:96, 8 * half:8 * half + 8, S * h:S * (h + 1)]
                dve.tensor_tensor(low, bank[64:96, n % 4, 0:HALF].rearrange("p (b s) -> p b s", s=S), low,
                                  ALU.subtract).then_inc(sem("q0_low"), 1)
            dve_context(dve, 0, 0, 0)
            dve_max0(dve, 0, 0, 0)

            def layer0(b, par, first, last):
                for t in range(T0):
                    if t < T0 - 1:
                        dve_max0(dve, b, par, t + 1)
                    elif not last:
                        dve_max0(dve, b + 1, 1 - par, 0)
                    if t % 2 == 0 and t >= 4:
                        dve_u0(dve, b, par, t // 2 - 2)
                    elif t % 2 == 0 and not first:
                        dve_u0(dve, b - 1, 1 - par, t // 2 + 2)
                    if t == PREP_AT + 1 and not last:
                        dve_context(dve, 0, b + 1, 1 - par)
                    dve_low0(dve, b, par, t)
                    if t % 2 == 1:
                        dve_inv0(dve, b, par, t // 2)
            batches(dve, layer0)
            dve_u0(dve, B - 1, 1, 2)
            dve_u0(dve, B - 1, 1, 3)
            dve.wait_ge(sem("tanh_g"), 1)
            dve_residual(dve, 0, 0)

            dve_norm(dve, 1)
            dve.wait_ge(sem("logits"), 1)
            dve.tensor_copy(logits[:].rearrange("p t e -> p (t e)"), bank[:, 2, 0:TT * NE]).then_inc(sem("route"), 1)
            dve.wait_ge(sem("route"), 1)
            dve.tensor_reduce(top[:], logits[:], AX.X, ALU.max).then_inc(sem("top"), 1)
            dve.wait_ge(sem("top"), 1)
            top_b = top[:].unsqueeze(2).broadcast_to((128, TT, NE))
            id_b = expert_id[:].unsqueeze(1).broadcast_to((128, TT, NE))
            dve.tensor_tensor(is_top[:], logits[:], top_b, ALU.is_equal).then_inc(sem("route"), 1)
            dve.wait_ge(sem("route"), 2)
            dve.tensor_tensor(is_top[:], is_top[:], id_b, ALU.mult).then_inc(sem("route"), 1)
            dve.wait_ge(sem("route"), 3)
            dve.tensor_reduce(first_top[:], is_top[:], AX.X, ALU.min).then_inc(sem("route"), 1)
            dve.wait_ge(sem("route"), 4)
            dve.tensor_tensor(one_hot[:], id_b, first_top[:].unsqueeze(2).broadcast_to((128, TT, NE)),
                              ALU.is_equal).then_inc(sem("one_hot"), 1)
            dve.wait_ge(sem("score_exp"), 1)
            dve.tensor_scalar(score[:], score[:], 1.0, None, ALU.add).then_inc(sem("route"), 1)
            dve.wait_ge(sem("route"), 5)
            dve.reciprocal(score[:], score[:]).then_inc(sem("route"), 1)
            dve.wait_ge(sem("route"), 6)
            dve.wait_ge(sem("ln_turned"), 2 * TT)
            dve.tensor_tensor(x_norm[:], x_norm[:], score[:].unsqueeze(2).broadcast_to((128, TT, E)), ALU.mult)\
                .then_inc(sem("x_scored"), 1)

            dve.wait_ge(sem("xs_t"), 1)

            def expert_tokens(n):
                half, e = n // (NE + 1), n % (NE + 1)
                if e < NE:
                    r = half * NE + e
                    dve.wait_ge(sem("hot_rows"), r + 1)
                    before = n - 2 if (n - 2) % (NE + 1) < NE else n - 3
                    wait(dve, sem("up0"), 2 * IC * (n - 1) if n >= 2 else 0)
                    dve.tensor_tensor(x_exp[:, r % 2, :], bank[:, 0, 0:HALF],
                                      x_score_t[:, HALF * half:HALF * (half + 1)], ALU.mult).then_inc(sem("x_exp"), 1)
            expert_tokens(0)
            for m in range(2 * (NE + 1) * IC):
                if m % IC == 0 and m // IC + 1 < 2 * (NE + 1):
                    expert_tokens(m // IC + 1)
                dve.wait_ge(sem("silu0"), m + 1)
                dve.wait_ge(sem("up0"), 2 * m + 2)
                wait(dve, sem("down0"), m - 1)
                dve.tensor_tensor(act0[:, m % 2, :], bank[:, 2 + 2 * (m % 2), 0:HALF], silu0[:, m % 2, :], ALU.mult)\
                    .then_inc(sem("act0"), 1)
            dve_residual(dve, 1, 2)
            dve_norm(dve, 2)
            for n in range(2 * H):
                h, half = n // 2, n % 2
                dve.wait_ge(sem("q1_high"), n + 1)
                part = (slice(None), slice(8 * half, 8 * half + 8), slice(S * h, S * (h + 1)))
                dve.scalar_tensor_tensor(q1[:, 1][part], bank[:, n % 4, 0:HALF].rearrange("p (b s) -> p b s", s=S), SCALE1,
                                         q1[:, 0][part], ALU.mult, ALU.subtract).then_inc(sem("q1_low"), 1)
            dve_context(dve, 1, 0, 0)
            dve_max1(dve, 0, 0, 0)
            dve_norm1(dve, 0, 0, 0)

            def layer1(b, par, first, last):
                for t in range(T1):
                    nxt = (b, par, t + 1) if t < T1 - 1 else (b + 1, 1 - par, 0)
                    if not (last and t == T1 - 1):
                        dve_max1(dve, *nxt)
                    if t == PREP1_AT + 1 and not last:
                        dve_context(dve, 1, b + 1, 1 - par)
                    dve_low1(dve, b, par, t)
                    if not (last and t == T1 - 1):
                        dve_norm1(dve, *nxt)
            batches(dve, layer1)

            dve.wait_ge(sem("in_wf"), 48)
            for n in range(3):
                dve.tensor_reduce(abs_sum[:, n:n + 1], wg_sb[:, n].rearrange("p a b -> p (a b)"), AX.X, ALU.add,
                                  apply_absolute_value=True).then_inc(sem("w_abs"), 1)
            dve_residual(dve, 2, 1)
            dve.wait_ge(sem("w_abs_all"), 1)
            dve.tensor_scalar(w_mean[:], bank[:, 0, 0:3], 1.0 / (INNER1 * E), 1e-5, ALU.mult, ALU.max)\
                .then_inc(sem("w_stat"), 1)
            dve.wait_ge(sem("w_stat"), 1)
            dve.reciprocal(w_scale[:], w_mean[:]).then_inc(sem("w_stat"), 1)
            dve.wait_ge(sem("w_stat"), 2)
            for n in range(3):
                w, r = wg_sb[:, n], w_round[:, n]
                dve.tensor_scalar(r, w, w_scale[:, n:n + 1], ROUND, ALU.mult, ALU.add).then_inc(sem("w_q"), 1)
                dve.wait_ge(sem("w_q"), 2 * n + 1)
                dve.tensor_scalar(r, r, -ROUND, 1.0, ALU.add, ALU.min).then_inc(sem("w_q"), 1)
                dve.wait_ge(sem("w_q"), 2 * n + 2)
                dve.tensor_scalar(w_tern[:, n], r, -1.0, None, ALU.max).then_inc(sem("w_tern"), 1)
            dve_norm(dve, 3)
            dve.wait_ge(sem("ln_norm"), 4 * TT)
            dve.tensor_reduce(x_amax[:], x_norm[:], AX.X, ALU.max, apply_absolute_value=True).then_inc(sem("xq_s"), 1)
            dve.wait_ge(sem("xq_s"), 1)
            dve.tensor_scalar(x_amax[:], x_amax[:], 1e-5, None, ALU.max).then_inc(sem("xq_s"), 1)
            dve.wait_ge(sem("xq_s"), 2)
            dve.reciprocal(x_qscale[:], x_amax[:]).then_inc(sem("xq_s"), 1)
            dve.wait_ge(sem("xq_s"), 3)
            dve.tensor_scalar(x_qscale[:], x_qscale[:], 127.0, None, ALU.mult).then_inc(sem("xq_s"), 1)
            for n in range(2):
                dve.tensor_scalar(x_deq[:, :, n], x_amax[:], 1.0 / 127.0, w_mean[:, n:n + 1], ALU.mult, ALU.mult)\
                    .then_inc(sem("xq_s"), 1)
            dve.wait_ge(sem("xq_s"), 6)
            dve.tensor_tensor(x_norm[:], x_norm[:], x_qscale[:].unsqueeze(2).broadcast_to((128, TT, E)), ALU.mult)\
                .then_inc(sem("xq_s"), 1)
            dve.wait_ge(sem("xq_s"), 7)
            dve.tensor_scalar(x_norm[:], x_norm[:], ROUND, None, ALU.add).then_inc(sem("xq_s"), 1)
            dve.wait_ge(sem("xq_s"), 8)
            dve.tensor_scalar(x_norm[:], x_norm[:], -ROUND, 127.0, ALU.add, ALU.min).then_inc(sem("xq_s"), 1)
            dve.wait_ge(sem("xq_s"), 9)
            dve.tensor_scalar(xq[:], x_norm[:], -128.0, None, ALU.max).then_inc(sem("xq"), 1)

            def finish(t):
                dve.wait_ge(sem("down1"), t + 1)
                dve.scalar_tensor_tensor(x_tok[:, t, :], bank[:, 6 + t % 2, 0:128], h_deq[:, t:t + 1], x_tok[:, t, :],
                                         ALU.mult, ALU.add).then_inc(sem("final"), 1)
            for t in range(TT):
                dve.wait_ge(sem("up1"), 2 * t + 2)
                dve.wait_ge(sem("silu1"), t + 1)
                a = act1[:, t % 2, :]
                dve.scalar_tensor_tensor(a, bank[:, 2 * (t % 2) + 1, :], x_deq[:, t, 1:2], silu1[:, t % 2, :],
                                         ALU.mult, ALU.mult).then_inc(sem("act1"), 1)
                dve.wait_ge(sem("act1"), t + 1)
                dve.tensor_reduce(h_amax[:, t:t + 1], a, AX.X, ALU.max, apply_absolute_value=True).then_inc(sem("hq_s"), 1)
                dve.wait_ge(sem("hq_s"), 7 * t + 1)
                dve.tensor_scalar(h_amax[:, t:t + 1], h_amax[:, t:t + 1], 1e-5, None, ALU.max).then_inc(sem("hq_s"), 1)
                dve.wait_ge(sem("hq_s"), 7 * t + 2)
                dve.reciprocal(h_qscale[:, t:t + 1], h_amax[:, t:t + 1]).then_inc(sem("hq_s"), 1)
                dve.tensor_scalar(h_deq[:, t:t + 1], h_amax[:, t:t + 1], 1.0 / 127.0, w_mean[:, 2:3], ALU.mult, ALU.mult)\
                    .then_inc(sem("hq_s"), 1)
                dve.wait_ge(sem("hq_s"), 7 * t + 4)
                dve.tensor_scalar(h_deq[:, t:t + 1], h_deq[:, t:t + 1], tanh_g[:, 3:4], None, ALU.mult).then_inc(sem("hq_s"), 1)
                dve.tensor_scalar(h_qscale[:, t:t + 1], h_qscale[:, t:t + 1], 127.0, None, ALU.mult).then_inc(sem("hq_s"), 1)
                dve.wait_ge(sem("hq_s"), 7 * t + 6)
                dve.tensor_scalar(a, a, h_qscale[:, t:t + 1], ROUND, ALU.mult, ALU.add).then_inc(sem("hq_s"), 1)
                dve.wait_ge(sem("hq_s"), 7 * t + 7)
                dve.tensor_scalar(a, a, -ROUND, 127.0, ALU.add, ALU.min).then_inc(sem("hq_r"), 1)
                dve.wait_ge(sem("hq_r"), t + 1)
                wait(dve, sem("hq_turned"), t - 1)
                dve.tensor_scalar(hq[:, t % 2, :], a, -128.0, None, ALU.max).then_inc(sem("hq"), 1)
                if t >= 1:
                    finish(t - 1)
            finish(TT - 1)


def diagonal(t):
    dims = [list(d) for d in t.ap]
    step = dims[1][0]
    return bass.AP(tensor=t.tensor, offset=t.offset, ap=[dims[0], [step + 8, dims[1][1]], [1, 8]])


_INS = ['x', 'ctx_1024', 'mask_Bx1xSxS2_if1', 'g_xattn', 'g_ffn', 'L0_xattn_Wv', 'L0_xattn_Wk', 'L0_xattn_Wq',
        'L0_xattn_Wo', 'L0_xattn_bo', 'L0_ffn_gate_w', 'L0_ffn_sh_gate', 'L0_ffn_sh_up', 'L0_ffn_sh_down',
        'L0_ffn_rt_gate', 'L0_ffn_rt_up', 'L0_ffn_rt_down', 'L1_xattn_Wq', 'L1_xattn_bq', 'L1_xattn_Wkv',
        'L1_xattn_bkv', 'L1_xattn_Wo', 'L1_xattn_bo', 'L1_ffn_w_gate', 'L1_ffn_w_up', 'L1_ffn_w_down']


def build(nc, arrays_of):
    args = [nc.dram_tensor(f"in_{n}", a.shape, mybir.dt.from_np(a.dtype), kind="ExternalInput").ap()
            for n, a in arrays_of.items()]
    out = nc.dram_tensor("out_x", arrays_of['x'].shape, F32, kind="ExternalOutput").ap()
    flamingo_kernel(nc, *args, out)


def kernel(**inputs):
    import numpy as np
    import concourse.bacc as bacc
    from concourse.bass_utils import run_bass_kernel_spmd

    nc = bacc.Bacc("TRN2", target_bir_lowering=False, num_devices=1)
    arrays = {n: np.ascontiguousarray(inputs[n]) for n in _INS}
    build(nc, arrays)
    r = run_bass_kernel_spmd(nc, [{f"in_{n}": a for n, a in arrays.items()}], core_ids=[0])
    return r.results[0]["out_x"]
```

```python
import concourse.bass as bass
from concourse import mybir
from contextlib import ExitStack

F32 = mybir.dt.float32
F16 = mybir.dt.float16
BF16 = mybir.dt.bfloat16
I32 = mybir.dt.int32
ALU = mybir.AluOpType
ACT = mybir.ActivationFunctionType
AX = mybir.AxisListType


def wait(engine, semaphore, value):
    if not isinstance(value, int) or value > 0:
        engine.wait_ge(semaphore, value)


def flamingo_kernel(nc, x, ctx_in, mask, g_xattn, g_ffn,
                    wv0, wk0, wq0, wo0, bo0, gate_w, sh_gate, sh_up, sh_down, rt_gate, rt_up, rt_down,
                    wq1, bq1, wkv1, bkv1, wo1, bo1, w_gate, w_up, w_down, out):
    B, S, E = x.shape
    S2 = ctx_in.shape[1]
    H = 16
    D0 = E // H
    D1 = wq1.shape[0] // H
    KC = 12
    KP = S2 // KC
    ROWS = H * S
    NTOK = B * S
    TT = NTOK // 128
    HALF = NTOK // 2
    G = 4
    HG = H // G
    GC = HG * S
    T0 = 8
    R0 = 2 * S
    T1 = ROWS // 128
    UC = KC // 2
    NE = gate_w.shape[1]
    INNER0 = sh_gate.shape[1]
    IC = INNER0 // 128
    INNER1 = w_gate.shape[0]
    JC = INNER1 // 128
    EPS = 1e-5
    NEG = -1e20
    SCALE0 = float(E) ** -0.5
    SCALE1 = float(D1) ** -0.5
    PSCALE = 2.0 ** 14
    ROUND = 1.5 * 2.0 ** 23
    LAST = B // 2 - 1

    ctx = ExitStack()
    with ctx:
        def sb(name, shape, dt=F32):
            return ctx.enter_context(nc.sbuf_tensor(name, shape, dt))

        sems = {}

        def sem(name):
            if name not in sems:
                sems[name] = ctx.enter_context(nc.semaphore(name))
            return sems[name]

        ident = sb("ident", [128, 128])
        ident16 = sb("ident16", [128, 128], F16)
        ones_f = sb("ones_f", [128, 128])
        half_neg = sb("half_neg", [128, TT])
        head_of = sb("head_of", [128, H])
        expert_id = sb("expert_id", [128, NE])
        expert_row = sb("expert_row", [NE, NE, 128], F16)
        x_tok = sb("x_tok", [128, TT, E])
        x_norm = sb("x_norm", [128, TT, E])
        x_norm_t = sb("x_norm_t", [128, NTOK])
        stats = sb("stats", [128, TT, 6])
        mean_var = sb("mean_var", [128, TT, 2])
        rstd = sb("rstd", [128, TT])
        block_t = sb("block_t", [128, NTOK])
        gates = sb("gates", [128, 4])
        tanh_g = sb("tanh_g", [128, 4])
        bo0_col = sb("bo0_col", [128, 1])
        bo1_col = sb("bo1_col", [128, 1])

        gate_w_sb = sb("gate_w_sb", [128, NE])
        g_w = sb("g_w", [128, NE + 1, INNER0])
        u_w = sb("u_w", [128, NE + 1, INNER0])
        logits = sb("logits", [128, TT, NE])
        top = sb("top", [128, TT])
        is_top = sb("is_top", [128, TT, NE])
        first_top = sb("first_top", [128, TT])
        one_hot = sb("one_hot", [128, TT, NE])
        one_hot_t = sb("one_hot_t", [NE, NTOK], F16)
        score = sb("score", [128, TT])

        bq1_col = sb("bq1_col", [128, 8])
        bv1_col = sb("bv1_col", [128, 8])
        bias1 = sb("bias1", [128, 1])

        wg_sb = sb("wg_sb", [128, 3, JC, 128])
        abs_sum = sb("abs_sum", [128, 3])
        w_mean = sb("w_mean", [128, 3])
        w_scale = sb("w_scale", [128, 3])
        ident_b = sb("ident_b", [128, 128], BF16)
        x_amax = sb("x_amax", [128, TT])
        x_qscale = sb("x_qscale", [128, TT])
        x_deq = sb("x_deq", [128, TT, 2])
        h_amax = sb("h_amax", [128, TT])
        h_qscale = sb("h_qscale", [128, TT])
        h_deq = sb("h_deq", [128, TT])

        c_in = [sb(f"c_in{p}", [KP, KC, E]) for p in range(2)]
        e_row = [sb(f"e_row{p}", [128, S2]) for p in range(2)]
        neg_max = sb("neg_max", [128, T0])
        bank_max = sb("bank_max", [128, T1, 3])
        row_sum = sb("row_sum", [128, T0])
        row_inv = sb("row_inv", [128, T0])

        REGION = 35072
        region = sb("region", [128, REGION])
        at = [0]

        def carve(shape, dt=F32):
            size = 1
            for n in shape[1:]:
                size *= n
            words = size if dt in (F32, I32) else (size + 1) // 2
            t = region[0:shape[0], at[0]:at[0] + words]
            at[0] += words
            assert at[0] <= REGION, at[0]
            if dt is not F32:
                t = t.bitcast(dt)
            if len(shape) > 2:
                dims = [f"d{n}" for n in range(len(shape) - 1)]
                t = t.rearrange(f"p ({' '.join(dims)}) -> p {' '.join(dims)}", **dict(zip(dims, shape[1:])))
            return t

        q0 = carve([96, B, ROWS], F16)
        c_split0 = carve([128, KC, G, 2, 32], F16)
        c_group = [carve([KP, KC, G, 64], F16) for _ in range(2)]
        c_t0 = carve([128, 2, KC, 128], F16)
        c_stack = [carve([96, G, KC, 128], F16) for _ in range(2)]
        mask_in = carve([R0, S2], I32)
        mask_bias = [carve([R0, KC, KP], BF16) for _ in range(2)]
        masked = [carve([R0, S2]) for _ in range(2)]
        inv_b = carve([128, GC])
        u0 = carve([128, 2, G, GC])
        out0_w = carve([128, H, 128])
        before_p0 = at[0]
        p_high0 = [carve([KP, KC, GC], F16) for _ in range(2)]
        p_low0 = [carve([KP, KC, GC], F16) for _ in range(2)]
        at[0] = before_p0
        a_heads = carve([128, H, 3, 32])
        v_heads = carve([128, H, 4, 32])
        w8 = carve([128, 3, D0])
        block_diag = carve([128, 3, E])
        wo0_sb = carve([128, E])
        wo0_t = carve([128, E])

        at[0] = 0
        x_score_t = carve([128, NTOK])
        x_exp = carve([128, 2, HALF])
        silu0 = carve([128, 2, HALF])
        act0 = carve([128, 2, HALF])
        d_w = carve([128, NE + 1, IC, 128])
        wq1_sb = carve([128, 8, 128])
        wo1_sb = carve([128, 8, 128])

        at[0] = 0
        q1 = carve([128, 2, B, ROWS], F16)
        out1_w = carve([128, H, 128])
        c_split1 = [carve([128, KC, 2, E], F16) for _ in range(2)]
        c_t1 = [carve([128, 2, KC, 128], F16) for _ in range(2)]
        GROUPS1 = [(0, 4), (4, T1)]
        before_p1 = at[0]
        p_high1 = [carve([KP, KC, 128 * (b - a)], F16) for a, b in GROUPS1]
        p_low1 = [carve([KP, KC, 128 * (b - a)], F16) for a, b in GROUPS1]
        u1 = carve([128, 2, ROWS])
        at[0] = before_p1
        q1_proj = carve([128, 8, NTOK])
        wq1_t = carve([128, 8, 128])
        wk1_sb = carve([128, 8, 128])
        wv1_sb = carve([128, 8, 128])
        wo1_t = carve([128, 8, 128])

        at[0] = 0
        w_round = carve([128, 3, JC, 128])
        w_tern = carve([128, 3, JC, 128], BF16)
        w_tern_t = carve([128, 3, JC, 128], BF16)
        xq = carve([128, TT, E], BF16)
        xq_t = carve([128, TT, 128], BF16)
        hq = carve([128, 2, INNER1], BF16)
        hq_t = carve([128, 2, JC, 128], BF16)
        silu1 = carve([128, 2, INNER1])
        act1 = carve([128, 2, INNER1])

        bank = ctx.enter_context(nc.psum_tensor("bank", [128, 8, 512], F32))
        U_BANK = 7

        def pair(u):
            return bank[:, 3 + 2 * (u % 2):5 + 2 * (u % 2), :]

        def pair_flat(u, dt=F32):
            t = pair(u).rearrange("p a b -> p (a b)")
            return t if dt is F32 else t.bitcast(dt)

        def pair_chunks(u, cols):
            return pair_flat(u)[0:KP, 0:UC * 128].rearrange("p (c n) -> p c n", n=128)[:, :, 0:cols]

        block = ctx.enter_context(nc.Block())

        turns = {layer: [[("turn", t, 0), ("turn", t, 1)] for t in range(tiles)] for layer, tiles in ((0, T0), (1, T1))}
        PROJ, NONE, PREP_0, PREP_1 = ("proj", 0, 0), ("none", 0, 0), ("prep", 0, 0), ("prep", 1, 0)
        PROJ_AT, PREP_AT = 3, {0: (4, 5), 1: (3, 4)}
        UNITS = {(0, par): sum(turns[0][:3], []) + [[PROJ, NONE], []][par] + turns[0][3] + [PREP_0] + turns[0][4]
                 + [PREP_1] + sum(turns[0][5:], []) for par in range(2)}
        UNITS.update({(1, par): sum(turns[1][:4], []) + [PREP_0] + turns[1][4] + [PREP_1] + sum(turns[1][5:], [])
                      for par in range(2)})

        def unit_no(layer, par, what):
            return UNITS[layer, par].index(what)

        def consumed(layer, b, what):
            kind, n, u = what
            tiles = T0 if layer == 0 else T1
            if kind == "turn":
                return sem(f"low_done{layer}"), b * (2 * tiles) + 2 * n + u + 1
            if kind == "proj":
                return sem(f"block_done{layer}"), b
            return sem(f"ct_done{layer}_{n}"), b + 2

        def wait_pair(engine, layer, b, par, what):
            units = UNITS[layer, par]
            k, back = units.index(what) - 2, 0
            while True:
                if k < 0:
                    back, par = back + 1, 1 - par
                    units = UNITS[layer, par]
                    k += len(units)
                before = units[k]
                fixed = isinstance(b, int)
                if fixed and b - back < 0:
                    n = k - (len(units) - 2)
                    if n in (0, 1):
                        wait(engine, sem(f"ct_done{layer}_{n}"), 1)
                    return
                absent = fixed and (b - back == B or (before[0] == "proj" and b - back == 0)
                                    or (before[0] == "prep" and b - back == B - 1))
                if absent or before[0] == "none":
                    k -= 2
                    continue
                s, v = consumed(layer, b - back, before)
                wait(engine, s, v)
                return

        def wait_apart(engine, name, *waits):
            for semaphore, count in waits:
                wait(engine, semaphore, count)
            engine.sem_inc(sem(f"passed_{name}"), 1)

        def batches(engine, body):
            body(0, 0, True, False)
            body(1, 1, False, False)
            with engine.Fori(1, LAST) as i:
                body(i * 2, 0, False, False)
                body(i * 2 + 1, 1, False, False)
            body(B - 2, 0, False, False)
            body(B - 1, 1, False, True)

        def per_use(b, par, n):
            if isinstance(b, int):
                return ((b - par) // 2 + 1) * n
            return (b - par) * (n // 2) + n

        def load(engine, name, pairs):
            for dst, src in pairs:
                few = src.shape[-1] * src.shape[0] <= 1024 or len(src.shape) == 2 and src.shape[1] <= 8
                engine.dma_start(dst, src, allow_slow_non_contiguous=few).then_inc(sem(name), 16)

        def head_rows(w, two, rows):
            return w.rearrange("(k h) e -> h k e", h=2 * rows)[two * rows:(two + 1) * rows]

        def sync_load_context(sp, layer, b, par):
            wait_apart(sp, "sp", (sem("low0" if layer == 0 else "split_done1"), b - 1))
            sp.dma_start(c_in[par][:], ctx_in[b].rearrange("(p c) e -> p c e", c=KC))\
                .then_inc(sem(f"ctx_in{layer}_{par}"), 16)

        def sync_load_mask(sp, b):
            wait_apart(sp, "sp", (sem("mask_done"), b))
            for two in range(2):
                sp.dma_start(mask_in[two * S:(two + 1) * S, :], mask[b, 0]).then_inc(sem("mask_in"), 16)

        def sync_stack(sp, b, par):
            wait_apart(sp, "sp", (sem("scores0"), (b - 1) * T0))
            for g in range(G):
                if g % 2 == 0:
                    wait_apart(sp, "sp", (sem(f"ct_done0_{g // 2}"), b + 1))
                rows = 64 * (g % 2)
                sp.dma_start(c_stack[par][0:64, g], c_t0[rows:rows + 64, g // 2]).then_inc(sem(f"stack{par}_{g}"), 16)
                sp.dma_start(c_stack[par][64:96, g], c_t0[rows:rows + 32, g // 2]).then_inc(sem(f"stack{par}_{g}"), 16)

        def sync_keep(sp, b, par):
            wait_apart(sp, "sp", (sem("low0"), b + 1))
            wait_apart(sp, "sp", (sem("pv_done0"), G * (b - 1)))
            sp.dma_start(c_group[par], c_split0[0:KP].rearrange("p c g two d -> p c g (two d)"))\
                .then_inc(sem("kept"), 16)

        @block.sync
        def _(sp):
            load(sp, "in_x", [(x_tok[:], x.rearrange("b s e -> (b s) e").rearrange("(t p) e -> p t e", p=128))])
            for n, w in enumerate((wq0, wk0, wv0)):
                for h in range(H):
                    sp.dma_start(w8[D0 * h:D0 * (h + 1), n, :], w).then_inc(sem("in_w8"), 16)
            load(sp, "in_w0", [(wo0_sb[:], wo0), (bo0_col[:], bo0.rearrange("(e o) -> e o", o=1))])
            sync_load_context(sp, 0, 0, 0)
            sync_load_mask(sp, 0)

            def layer0(b, par, first, last):
                if not last:
                    sync_load_context(sp, 0, b + 1, 1 - par)
                    sync_load_mask(sp, b + 1)
                    sync_stack(sp, b + 1, 1 - par)
                    sync_keep(sp, b + 1, 1 - par)
            sync_stack(sp, 0, 0)
            sync_keep(sp, 0, 0)
            batches(sp, layer0)
            sync_load_context(sp, 1, 0, 0)

            def layer1(b, par, first, last):
                if not last:
                    sync_load_context(sp, 1, b + 1, 1 - par)
            batches(sp, layer1)
            sp.wait_ge(sem("final"), TT)
            for t in range(TT):
                sp.dma_start(out.rearrange("b s e -> (b s) e")[128 * t:128 * (t + 1), :], x_tok[:, t, :])\
                    .then_inc(sem("stored"), 16)
            sp.wait_ge(sem("stored"), 16 * TT)

        def pool_rstd(pool, layer):
            pool.wait_ge(sem("ln_var"), TT * (layer + 1))
            pool.tensor_scalar(rstd[:], mean_var[:, :, 1], EPS, None, ALU.add).then_inc(sem("ln_eps"), 1)
            pool.wait_ge(sem("ln_eps"), layer + 1)
            pool.tensor_tensor(rstd[:], rstd[:], half_neg[:], ALU.pow).then_inc(sem("ln_rstd"), 1)

        @block.gpsimd
        def _(pool):
            for m in (ident, ident16, ident_b):
                pool.memset(m[:], 0.0).then_inc(sem("const_0"), 1)
            pool.memset(ones_f[:], 1.0).then_inc(sem("const_0"), 1)
            pool.memset(half_neg[:], -0.5).then_inc(sem("const_0"), 1)
            pool.memset(head_of[:], 1.0).then_inc(sem("const_0"), 1)
            pool.memset(expert_row[:], 0.0).then_inc(sem("const_0"), 1)
            pool.memset(a_heads[:], 0.0).then_inc(sem("const_0"), 1)
            pool.memset(v_heads[:], 0.0).then_inc(sem("const_0"), 1)
            pool.memset(c_split0[:], 0.0).then_inc(sem("const_0"), 1)
            pool.wait_ge(sem("const_0"), 10)
            for m in (ident, ident16, ident_b):
                pool.affine_select(out=m[:], in_=m[:], compare_op=ALU.not_equal, fill=1.0, base=0,
                                   pattern=[[-1, 128]], channel_multiplier=1).then_inc(sem("const"), 1)
            pool.affine_select(out=head_of[:], in_=head_of[:], compare_op=ALU.is_ge, fill=0.0, base=0,
                               pattern=[[-D0, H]], channel_multiplier=1).then_inc(sem("const"), 1)
            pool.wait_ge(sem("const"), 4)
            pool.affine_select(out=head_of[:], in_=head_of[:], compare_op=ALU.is_ge, fill=0.0, base=D0 - 1,
                               pattern=[[D0, H]], channel_multiplier=-1).then_inc(sem("const"), 1)
            pool.affine_select(out=expert_row[:], in_=expert_row[:], compare_op=ALU.not_equal, fill=1.0, base=0,
                               pattern=[[-1, NE], [0, 128]], channel_multiplier=1).then_inc(sem("const"), 1)
            for e in range(NE):
                pool.memset(expert_id[:, e:e + 1], float(e - NE)).then_inc(sem("const"), 1)
            pool_rstd(pool, 0)

            def split0(b, par):
                wait_apart(pool, "pool", (sem(f"ctx_in0_{par}"), per_use(b, par, 16)), (sem("ct_turned0"), 2 * b),
                           (sem("kept"), 16 * b))
                source = c_in[par][:].rearrange("p c (g d) -> p c g d", g=G)
                high, low = c_split0[0:KP, :, :, 0, :], c_split0[0:KP, :, :, 1, :]
                pool.tensor_copy(high, source).then_inc(sem("high0"), 1)
                pool.wait_ge(sem("high0"), b + 1)
                pool.tensor_tensor(low, source, high, ALU.subtract).then_inc(sem("low0"), 1)

            def mask0(b, par):
                wait_apart(pool, "pool", (sem("mask_in"), (b + 1) * 32), (sem("max_done0"), (b - 1) * T0))
                pool.tensor_scalar(mask_bias[par][:], mask_in[:].rearrange("q (p c) -> q c p", c=KC),
                                   0.0, NEG, ALU.is_equal, ALU.mult).then_inc(sem("mask_done"), 1)

            split0(0, 0)
            mask0(0, 0)

            def layer0(b, par, first, last):
                if not last:
                    split0(b + 1, 1 - par)
                    mask0(b + 1, 1 - par)
            batches(pool, layer0)
            pool_rstd(pool, 1)
            pool_rstd(pool, 2)
            for p in range(2):
                pool.wait_ge(sem("residual"), TT)
                pool.memset(c_split1[p], 0.0).then_inc(sem("pad1"), 1)

            def layer1(b, par):
                pool.wait_ge(sem("high1"), b + 1)
                high = c_split1[par][0:KP, :, 0, :]
                pool.tensor_tensor(c_split1[par][0:KP, :, 1, :], c_in[par][:], high, ALU.subtract)\
                    .then_inc(sem("split_done1"), 1)
            layer1(0, 0)
            batches(pool, lambda b, par, first, last: None if last else layer1(b + 1, 1 - par))
            pool_rstd(pool, 3)

        def pe_norm_t(pe, layer):
            pe.wait_ge(sem("ln_norm"), TT * (layer + 1))
            wait(pe, sem("const"), 1)
            for t in range(TT):
                pe.transpose(bank[:, t // 4, 128 * (t % 4):128 * (t % 4 + 1)], x_norm[:, t, :], ident[:])\
                    .then_inc(sem("ln_turned"), 1)

        def pe_block_turn(pe, n):
            pe.wait_ge(sem("block_ready"), n + 1)
            for t in range(TT):
                pe.transpose(bank[:, 5 + t // 4, 128 * (t % 4):128 * (t % 4 + 1)],
                             block_t[:, 128 * t:128 * (t + 1)], ident[:]).then_inc(sem("block_turned"), 1)

        def pe_scores0(pe, b, par, t):
            if t % 2 == 0:
                pe.wait_ge(sem(f"stack{par}_{t // 2}"), per_use(b, par, 32))
            wait(pe, sem("max_done0"), b * T0 + t)
            for k in range(3):
                last = pe.matmul(bank[0:R0, k, 0:4 * KP], q0[:, b, R0 * t:R0 * (t + 1)],
                                 c_stack[par][:, t // 2, 4 * k:4 * k + 4, 0:KP], start=True, stop=True)
            last.then_inc(sem("scores0"), 1)

        def pe_turn(pe, layer, b, par, t):
            rows, tiles = (R0, T0) if layer == 0 else (128, T1)
            pe.wait_ge(sem("exp_done0" if layer == 0 else "norm_done1"), b * tiles + t + 1)
            for u in range(2):
                wait_pair(pe, layer, b, par, ("turn", t, u))
                n = unit_no(layer, par, ("turn", t, u))
                for c in range(UC):
                    k = UC * u + c
                    last = pe.transpose(pair(n)[0:KP, c // 4, 128 * (c % 4):128 * (c % 4) + rows],
                                        e_row[(t + par * (tiles % 2)) % 2][0:rows, KP * k:KP * (k + 1)],
                                        ident[0:rows, 0:rows])
                last.then_inc(sem(f"turned{layer}"), 1)

        def pe_prep(pe, layer, b, par, halves):
            for n in halves:
                if isinstance(b, int) and b == 0:
                    if n == 0:
                        wait(pe, sem("const"), 3)
                else:
                    wait_pair(pe, layer, b - 1, 1 - par, ("prep", n, 0))
                if layer == 0:
                    pe.wait_ge(sem("low0"), b + 1)
                else:
                    pe.wait_ge(sem("split_done1" if n else "high1"), b + 1)
                no = unit_no(layer, 1 - par, ("prep", n, 0)) if not (isinstance(b, int) and b == 0) else \
                    n
                for c in range(KC):
                    src = c_split0[:, c, 2 * n:2 * n + 2].rearrange("p g two d -> p (g two d)") if layer == 0 \
                        else c_split1[par][:, c, n, :]
                    last = pe.transpose(pair_flat(no, F16)[:, 128 * c:128 * (c + 1)], src, ident16[:])
                last.then_inc(sem(f"ct_turned{layer}"), 1)

        def pe_pv0(pe, b, par, g, part):
            if part == 0:
                pe.wait_ge(sem("low_done0"), b * (2 * T0) + 4 * (g + 1))
                wait(pe, sem("u_done0"), b * G + g)
                pe.wait_ge(sem("kept"), (b + 1) * 16)
            for c in range(UC * part, UC * part + UC):
                for lo, p in ((0, p_high0), (64, p_low0)):
                    last = pe.matmul(bank[lo:lo + 64, U_BANK, 0:GC], c_group[par][:, c, g, :],
                                     p[g % 2][:, c, :], start=(c == 0), stop=(c == KC - 1))
            if part == 1:
                last.then_inc(sem("pv_done0"), 1)
                pe.wait_ge(sem("inv_done0"), b * G + g + 1)
                for n in range(2):
                    t = 2 * g + n
                    last = pe.matmul(bank[:, U_BANK, 256 + R0 * n:256 + R0 * (n + 1)],
                                     row_inv[0:R0, t:t + 1].broadcast_to((R0, 128)),
                                     ident[0:R0, 0:R0], start=True, stop=True)
                last.then_inc(sem("inv_spread"), 1)

        def projected(layer):
            return bank[:, U_BANK, 0:2 * S] if layer == 1 else pair(unit_no(0, 0, PROJ))[:, 0, 0:2 * S]

        def pe_proj(pe, layer, b):
            pe.wait_ge(sem("u_done0"), b * G) if layer == 0 else pe.wait_ge(sem("u_done1"), b * 2)
            if layer == 0:
                wait_pair(pe, 0, b, 0, PROJ)
            for h in range(H):
                rhs = u0[:, :, h // HG, S * (h % HG):S * (h % HG + 1)] if layer == 0 else u1[:, :, S * h:S * (h + 1)]
                last = pe.matmul(projected(layer).rearrange("p (b s) -> p b s", b=2),
                                 (out0_w if layer == 0 else out1_w)[:, h, :], rhs, start=(h == 0), stop=(h == H - 1))
            last.then_inc(sem(f"projected{layer}"), 2)

        def pe_scores1(pe, b, par, t):
            if t == 0:
                for n in range(2):
                    pe.wait_ge(sem(f"ct_done1_{n}"), b + 1)
            wait(pe, sem("exp_done1"), b * T1 + t)
            for k in range(3):
                for ql, cl in ((0, 0), (0, 1), (1, 0)):
                    last = pe.matmul(bank[:, k, 0:4 * KP], q1[:, ql, b, 128 * t:128 * (t + 1)],
                                     c_t1[par][:, cl, 4 * k:4 * k + 4, 0:KP],
                                     start=(ql == 0 and cl == 0), stop=(ql == 1))
                last.then_inc(sem("scores1"), 1)

        def pe_pv1(pe, b, par, grp, first, end):
            a, z = GROUPS1[grp]
            cols = 128 * (z - a)
            if first == 0:
                pe.wait_ge(sem("low_done1"), b * (2 * T1) + 2 * z)
                wait(pe, sem("u_done1"), b * 2 + grp)
                if grp == 0 and par == 0:
                    wait(pe, sem("block_done1"), b)
            for c in range(first, end):
                for cl, p in ((0, p_high1), (0, p_low1), (1, p_high1)):
                    last = pe.matmul(bank[:, U_BANK, 0:cols], c_split1[par][0:KP, c, cl, :], p[grp][:, c, :],
                                     start=(c == 0 and cl == 0 and p is p_high1),
                                     stop=(c == KC - 1 and cl == 1))
            if end == KC:
                last.then_inc(sem("pv_done1"), 1)

        @block.tensor
        def _(pe):
            pe_norm_t(pe, 0)
            pe.wait_ge(sem("diag"), 3)
            pe.matmul(bank[:, 2, 0:E], block_diag[:, 0, :], block_diag[:, 1, :], start=True, stop=True)\
                .then_inc(sem("w0_a"), 1)
            pe.wait_ge(sem("in_w0"), 32)
            pe.transpose(bank[:, 3, 0:E], wo0_sb[:], ident[:]).then_inc(sem("w0_wo"), 1)
            pe.wait_ge(sem("w0_sb"), 8)
            for h in range(H):
                last = pe.matmul(bank[:, 4 + h // 4, 128 * (h % 4):128 * (h % 4 + 1)],
                                 v_heads[:, h].rearrange("p a b -> p (a b)"), wo0_t[:], start=True, stop=True)
            last.then_inc(sem("w0_out"), 1)
            pe.wait_ge(sem("ln_t"), 2)
            for n in range(2 * H):
                h, half = n // 2, n % 2
                if n >= 4:
                    pe.wait_ge(sem("q0_low"), n - 3)
                pe.matmul(bank[0:96, n % 4, 0:HALF], a_heads[:, h].rearrange("p a b -> p (a b)"),
                          x_norm_t[:, HALF * half:HALF * (half + 1)], start=True, stop=True)\
                    .then_inc(sem("q0_made"), 1)
            pe.wait_ge(sem("q0_low"), 2 * H)
            pe.wait_ge(sem("w0_out_sb"), 1)
            pe_prep(pe, 0, 0, 0, (0, 1))
            pe_scores0(pe, 0, 0, 0)

            def layer0(b, par, first, last):
                for t in range(T0):
                    if t < T0 - 1:
                        pe_scores0(pe, b, par, t + 1)
                    elif not last:
                        pe_scores0(pe, b + 1, 1 - par, 0)
                    if t >= 3:
                        pe_pv0(pe, b, par, (t - 3) // 2, (t - 3) % 2)
                    elif not first:
                        pe_pv0(pe, b - 1, 1 - par, (t + T0 - 3) // 2, (t + T0 - 3) % 2)
                    if t == PROJ_AT and par == 0 and not first:
                        pe_proj(pe, 0, b)
                    if t in PREP_AT[0] and not last:
                        pe_prep(pe, 0, b + 1, 1 - par, (PREP_AT[0].index(t),))
                    pe_turn(pe, 0, b, par, t)
            batches(pe, layer0)
            for k in range(T0 - 3, T0):
                pe_pv0(pe, B - 1, 1, k // 2, k % 2)
            pe_proj(pe, 0, B)

            pe_block_turn(pe, 0)
            pe_norm_t(pe, 1)
            pe.wait_ge(sem("in_ffn0"), 16 * 5)
            pe.wait_ge(sem("in_down0"), 16 * 2)
            pe.wait_ge(sem("ln_t"), 4)
            for t in range(TT):
                last = pe.matmul(bank[:, 2, NE * t:NE * (t + 1)], x_norm_t[:, 128 * t:128 * (t + 1)],
                                 gate_w_sb[:], start=True, stop=True)
            last.then_inc(sem("logits"), 1)
            pe.wait_ge(sem("one_hot"), 1)
            for t in range(TT):
                last = pe.transpose(bank[0:NE, 3 + t // 4, 128 * (t % 4):128 * (t % 4 + 1)], one_hot[:, t, :], ident[:])
            last.then_inc(sem("hot_turned"), 1)
            pe.wait_ge(sem("x_scored"), 1)
            for t in range(TT):
                last = pe.transpose(bank[:, 5 + t // 4, 128 * (t % 4):128 * (t % 4 + 1)], x_norm[:, t, :], ident[:])
            last.then_inc(sem("xs_turned"), 1)
            pe.wait_ge(sem("hot_t"), 1)

            pe.wait_ge(sem("xs_t"), 1)

            def hot_rows(n):
                half, e = n // (NE + 1), n % (NE + 1)
                if e < NE:
                    r = half * NE + e
                    wait(pe, sem("x_exp"), r)
                    pe.matmul(bank[:, 0, 0:HALF], expert_row[:, e, :], one_hot_t[:, HALF * half:HALF * (half + 1)],
                              start=True, stop=True).then_inc(sem("hot_rows"), 1)

            def down(m):
                n, ic = m // IC, m % IC
                half, e = n // (NE + 1), n % (NE + 1)
                pe.wait_ge(sem("act0"), m + 1)
                last = pe.matmul(bank[:, 5 + half, 0:HALF], d_w[:, e, ic, :], act0[:, m % 2, :],
                                 start=(e == 0 and ic == 0), stop=(e == NE and ic == IC - 1))
                last.then_inc(sem("down0"), 1)

            hot_rows(0)
            for m in range(2 * (NE + 1) * IC):
                n, ic = m // IC, m % IC
                half, e = n // (NE + 1), n % (NE + 1)
                if ic == 0:
                    if n + 1 < 2 * (NE + 1):
                        hot_rows(n + 1)
                    if e < NE:
                        pe.wait_ge(sem("x_exp"), half * NE + e + 1)
                moving = x_exp[:, (half * NE + e) % 2, :] if e < NE else x_norm_t[:, HALF * half:HALF * (half + 1)]
                wait(pe, sem("act0"), m - 1)
                for w, at in ((g_w, 0), (u_w, 1)):
                    pe.matmul(bank[:, 1 + 2 * (m % 2) + at, 0:HALF], w[:, e, 128 * ic:128 * (ic + 1)], moving,
                              start=True, stop=True).then_inc(sem("up0"), 1)
                if m >= 1:
                    down(m - 1)
            down(2 * (NE + 1) * IC - 1)
            pe.wait_ge(sem("block_out"), 2)
            pe_block_turn(pe, 1)

            pe.wait_ge(sem("in_w1"), 16 * 8)
            pe.wait_ge(sem("in_bv"), 16 * 2)
            for n in range(16):
                src = (wq1_sb if n < 8 else wo1_sb)[:, n % 8, :]
                pe.transpose(bank[:, n // 4, 128 * (n % 4):128 * (n % 4 + 1)], src, ident[:])\
                    .then_inc(sem("w1_turned"), 1)
            pe.wait_ge(sem("w1_t"), 4)
            for h in range(H):
                lo, k = 64 * (h % 2), h // 2
                last = pe.matmul(bank[:, 2 * (h % 2) + k // 4, 128 * (k % 4):128 * (k % 4 + 1)], wv1_sb[lo:lo + 64, h // 2, :],
                                 wo1_t[lo:lo + 64, h // 2, :], start=True, stop=True)
            last.then_inc(sem("w1_out"), 1)
            for k in range(8):
                last = pe.matmul(bank[:, 4, 0:1], wo1_t[:, k, :], bv1_col[:, k:k + 1], start=(k == 0), stop=(k == 7))
            last.then_inc(sem("w1_bias"), 1)
            pe.wait_ge(sem("w1_out_sb"), 4)
            pe_norm_t(pe, 2)
            pe.wait_ge(sem("ln_t"), 6)
            for n in range(16):
                k, half = n // 2, n % 2
                if n >= 4:
                    pe.wait_ge(sem("q1_proj"), n - 3)
                pe.matmul(bank[:, n % 4, 0:HALF], wq1_t[:, k, :], x_norm_t[:, HALF * half:HALF * (half + 1)],
                          start=True, stop=True).then_inc(sem("q1_made"), 1)
            for n in range(2 * H):
                h, half = n // 2, n % 2
                lo = 64 * (h % 2)
                pe.wait_ge(sem("q1_proj"), 16)
                if n >= 4:
                    pe.wait_ge(sem("q1_low"), n - 3)
                pe.matmul(bank[:, n % 4, 0:HALF], wk1_sb[lo:lo + 64, h // 2, :],
                          q1_proj[lo:lo + 64, h // 2, HALF * half:HALF * (half + 1)], start=True, stop=True)\
                    .then_inc(sem("qk1_made"), 1)
            pe.wait_ge(sem("q1_low"), 2 * H)
            pe_prep(pe, 1, 0, 0, (0, 1))
            pe_scores1(pe, 0, 0, 0)

            def layer1(b, par, first, last):
                for t in range(T1):
                    if t < T1 - 1:
                        pe_scores1(pe, b, par, t + 1)
                    elif not last:
                        pe_scores1(pe, b + 1, 1 - par, 0)
                    pe_turn(pe, 1, b, par, t)
                    if t < 3 and not first:
                        pe_pv1(pe, b - 1, 1 - par, 1, 4 * t, 4 * t + 4)
                    if t == PROJ_AT and par == 0 and not first:
                        pe_proj(pe, 1, b)
                    if t in PREP_AT[1] and not last:
                        pe_prep(pe, 1, b + 1, 1 - par, (PREP_AT[1].index(t),))
                    if t >= 4:
                        pe_pv1(pe, b, par, 0, *((0, 3), (3, 7), (7, KC))[t - 4])
            batches(pe, layer1)
            pe_pv1(pe, B - 1, 1, 1, 0, KC)
            pe_proj(pe, 1, B)

            pe_block_turn(pe, 2)
            pe.wait_ge(sem("w_abs"), 3)
            pe.matmul(bank[:, 0, 0:3], ones_f[:], abs_sum[:], start=True, stop=True).then_inc(sem("w_abs_all"), 1)
            pe.wait_ge(sem("w_tern"), 3)
            for n in range(3):
                for j in range(JC):
                    last = pe.transpose(bank[:, 1 + n, 0:256].bitcast(BF16)[:, 128 * j:128 * (j + 1)],
                                        w_tern[:, n, j, :], ident_b[:])
                last.then_inc(sem("w_turned"), 1)
            pe.wait_ge(sem("xq"), 1)
            for t in range(TT):
                last = pe.transpose(bank[:, 4, :].bitcast(BF16)[:, 128 * t:128 * (t + 1)], xq[:, t, :], ident_b[:])
            last.then_inc(sem("xq_turned"), 1)
            pe.wait_ge(sem("w_t"), 3)
            pe.wait_ge(sem("xq_t"), 1)

            def up1(t):
                wait(pe, sem("act1"), t - 1)
                for n in range(2):
                    pe.matmul(bank[:, 2 * (t % 2) + n, :], xq_t[:, t, :],
                              w_tern_t[:, n].rearrange("p a b -> p (a b)"), start=True, stop=True)\
                        .then_inc(sem("up1"), 1)

            def down1(t):
                pe.wait_ge(sem("hq"), t + 1)
                for j in range(JC):
                    last = pe.transpose(bank[:, 4 + t % 2, :].bitcast(BF16)[:, 128 * j:128 * (j + 1)],
                                        hq[:, t % 2, 128 * j:128 * (j + 1)], ident_b[:])
                last.then_inc(sem("hq_turned"), 1)
                pe.wait_ge(sem("hq_t"), t + 1)
                wait(pe, sem("final"), t - 1)
                for j in range(JC):
                    last = pe.matmul(bank[:, 6 + t % 2, 0:128], hq_t[:, t % 2, j, :], w_tern_t[:, 2, j, :],
                                     start=(j == 0), stop=(j == JC - 1))
                last.then_inc(sem("down1"), 1)

            up1(0)
            for t in range(TT):
                if t + 1 < TT:
                    up1(t + 1)
                down1(t)

        def act_norm_t(act, layer):
            for n in range(2):
                act.wait_ge(sem("ln_turned"), TT * layer + (4 if n == 0 else TT))
                cols = 512 if n == 0 else NTOK - 512
                act.copy(x_norm_t[:, 512 * n:512 * n + cols], bank[:, n, 0:cols]).then_inc(sem("ln_t"), 1)

        def act_exp0(act, b, par, t):
            act.wait_ge(sem("max_done0"), b * T0 + t + 1)
            wait(act, sem("turned0"), (b * T0 + t - 1) * 2)
            act.activation(e_row[t % 2][0:R0, :], masked[t % 2][:], ACT.Exp, bias=neg_max[0:R0, t:t + 1],
                           scale=-1.0, accum_out=row_sum[0:R0, t:t + 1]).then_inc(sem("exp_done0"), 1)

        def act_high0(act, b, par, t):
            g = t // 2
            for u in range(2):
                act.wait_ge(sem("turned0"), (b * T0 + t) * 2 + u + 1)
                if t % 2 == 0 and u == 0:
                    wait(act, sem("pv_done0"), b * G + g - 1)
                act.activation(p_high0[g % 2][:, UC * u:UC * (u + 1), R0 * (t % 2):R0 * (t % 2 + 1)],
                               pair_chunks(unit_no(0, par, ("turn", t, u)), R0), ACT.Copy, scale=PSCALE)\
                    .then_inc(sem("high_done0"), 1)

        def act_inv0(act, b, par, g):
            act.wait_ge(sem("inv_spread"), b * G + g + 1)
            wait(act, sem("u_done0"), b * G + g)
            act.copy(inv_b[:], bank[:, U_BANK, 256:256 + GC]).then_inc(sem("inv_sb"), 1)

        def act_block(act, layer, b):
            act.wait_ge(sem(f"projected{layer}"), b)
            act.activation(block_t[:, bass.ds((b - 2) * S, 2 * S)], projected(layer),
                           ACT.Identity, bias=(bo0_col if layer == 0 else bias1)[:]).then_inc(sem(f"block_done{layer}"), 2)

        def act_exp1(act, b, par, t):
            act.wait_ge(sem("max_done1"), b * T1 + t + 1)
            wait(act, sem("turned1"), (b * T1 + t - 1) * 2)
            act.activation(e_row[(t + par) % 2][:], bank[:, 0:3, 0:4 * KP], ACT.Exp, bias=neg_max[:, t:t + 1],
                           accum_out=row_sum[:, t:t + 1]).then_inc(sem("exp_done1"), 1)

        def act_high1(act, b, par, t, u):
            grp = 0 if t < 4 else 1
            at = t - GROUPS1[grp][0]
            act.wait_ge(sem("turned1"), (b * T1 + t) * 2 + u + 1)
            if at == 0 and u == 0:
                wait(act, sem("pv_done1"), (b - 1) * 2 + grp + 1)
            act.copy(p_high1[grp][:, UC * u:UC * (u + 1), 128 * at:128 * (at + 1)],
                     pair_chunks(unit_no(1, par, ("turn", t, u)), 128)).then_inc(sem("high_done1"), 1)

        def act_u1(act, b, par, grp):
            a, z = GROUPS1[grp]
            act.wait_ge(sem("pv_done1"), b * 2 + grp + 1)
            if grp == 0 and par == 0:
                wait(act, sem("projected1"), b)
            act.activation(u1[:, par, 128 * a:128 * z], bank[:, U_BANK, 0:128 * (z - a)], ACT.Copy, scale=1.0 / PSCALE)\
                .then_inc(sem("u_done1"), 1)

        def act_split1(act, b, par):
            act.wait_ge(sem(f"ctx_in1_{par}"), per_use(b, par, 16))
            wait(act, sem("pv_done1"), (b - 1) * 2)
            act.copy(c_split1[par][0:KP, :, 0, :], c_in[par][:]).then_inc(sem("high1"), 1)

        @block.scalar
        def _(act):
            load(act, "in_gates", [(gates[:, 0:2], g_xattn.rearrange("(o n) -> o n", o=1).broadcast_to((128, 2))),
                                   (gates[:, 2:4], g_ffn.rearrange("(o n) -> o n", o=1).broadcast_to((128, 2)))])
            load(act, "in_ffn0", [
                (gate_w_sb[:], gate_w),
                (g_w[:, 0:NE, :], rt_gate.rearrange("e h i -> h e i")), (g_w[:, NE, :], sh_gate),
                (u_w[:, 0:NE, :], rt_up.rearrange("e h i -> h e i")), (u_w[:, NE, :], sh_up)])
            bkv = bkv1.rearrange("(k two part d) -> two part d k", two=2, part=2, d=D1)
            load(act, "in_w1", [(bq1_col[:], bq1.rearrange("(k p) -> p k", p=128)),
                                (bo1_col[:], bo1.rearrange("(e o) -> e o", o=1))])
            for two in range(2):
                load(act, "in_bv", [(bv1_col[64 * two:64 * two + 64], bkv[two, 1])])
            load(act, "in_wf", [(wg_sb[:, 0], w_gate.rearrange("(j p) h -> p j h", p=128)),
                                (wg_sb[:, 1], w_up.rearrange("(j p) h -> p j h", p=128)),
                                (wg_sb[:, 2], w_down.rearrange("h (j p) -> h j p", p=128))])
            act.wait_ge(sem("in_gates"), 32)
            act.activation(tanh_g[:], gates[:], ACT.Tanh).then_inc(sem("tanh_g"), 1)
            act_norm_t(act, 0)
            act.wait_ge(sem("w0_wo"), 1)
            act.copy(wo0_t[:], bank[:, 3, 0:E]).then_inc(sem("w0_sb"), 1)
            act.wait_ge(sem("w0_out"), 1)
            act.copy(out0_w[:].rearrange("p (a h) e -> p a (h e)", a=4), bank[:, 4:8, :]).then_inc(sem("w0_out_sb"), 1)
            for n in range(2 * H):
                h, half = n // 2, n % 2
                act.wait_ge(sem("q0_made"), n + 1)
                act.copy(q0[:, 8 * half:8 * half + 8, S * h:S * (h + 1)],
                         bank[0:96, n % 4, 0:HALF].rearrange("p (b s) -> p b s", s=S)).then_inc(sem("q0_high"), 1)

            def layer0(b, par, first, last):
                for t in range(T0):
                    if t % 2 == 0 and t >= 4:
                        act_inv0(act, b, par, t // 2 - 2)
                    elif t % 2 == 0 and not first:
                        act_inv0(act, b - 1, 1 - par, t // 2 + 2)
                    if t == PROJ_AT and par == 0 and not first:
                        act_block(act, 0, b)
                    act_high0(act, b, par, t)
                    if t < T0 - 1:
                        act_exp0(act, b, par, t + 1)
                    elif not last:
                        act_exp0(act, b + 1, 1 - par, 0)
            act_exp0(act, 0, 0, 0)
            batches(act, layer0)
            act_inv0(act, B - 1, 1, 2)
            act_inv0(act, B - 1, 1, 3)
            act_block(act, 0, B)
            act.wait_ge(sem("block_done0"), B)
            act.sem_inc(sem("block_ready"), 1)

            act.wait_ge(sem("block_ready"), 1)
            load(act, "in_down0", [
                (d_w[:, 0:NE].rearrange("p e c h -> p (e c) h"), rt_down.rearrange("e (c p) h -> p (e c) h", p=128)),
                (d_w[:, NE], sh_down.rearrange("(c p) h -> p c h", p=128))])
            load(act, "in_w1", [
                (wq1_sb[:], wq1.rearrange("(k p) e -> p k e", p=128)),
                (wo1_sb[:], wo1.rearrange("e (k p) -> e k p", p=128))])
            kv = wkv1.rearrange("(k two part d) e -> two part d k e", two=2, part=2, d=D1)
            for two in range(2):
                load(act, "in_w1", [(wk1_sb[64 * two:64 * two + 64], kv[two, 0]), (wv1_sb[64 * two:64 * two + 64], kv[two, 1])])

            act_norm_t(act, 1)
            act.wait_ge(sem("top"), 1)
            act.activation(score[:], top[:], ACT.Exp, scale=-1.0).then_inc(sem("score_exp"), 1)
            act.wait_ge(sem("hot_turned"), 1)
            for n in range(2):
                cols = 512 if n == 0 else NTOK - 512
                last = act.copy(one_hot_t[:, 512 * n:512 * n + cols], bank[0:NE, 3 + n, 0:cols])
            last.then_inc(sem("hot_t"), 1)
            act.wait_ge(sem("xs_turned"), 1)
            for n in range(2):
                cols = 512 if n == 0 else NTOK - 512
                last = act.copy(x_score_t[:, 512 * n:512 * n + cols], bank[:, 5 + n, 0:cols])
            last.then_inc(sem("xs_t"), 1)
            for m in range(2 * (NE + 1) * IC):
                act.wait_ge(sem("up0"), 2 * m + 1)
                wait(act, sem("act0"), m - 1)
                act.activation(silu0[:, m % 2, :], bank[:, 1 + 2 * (m % 2), 0:HALF], ACT.Silu).then_inc(sem("silu0"), 1)
            act.wait_ge(sem("down0"), 2 * (NE + 1) * IC)
            for half in range(2):
                last = act.copy(block_t[:, HALF * half:HALF * (half + 1)], bank[:, 5 + half, 0:HALF])
                last.then_inc(sem("block_out"), 1)
            act.wait_ge(sem("block_out"), 2)
            act.sem_inc(sem("block_ready"), 1)

            act.wait_ge(sem("w1_turned"), 16)
            for n in range(4):
                dst = (wq1_t if n < 2 else wo1_t)[:, 4 * (n % 2):4 * (n % 2) + 4, :]
                act.copy(dst.rearrange("p a b -> p (a b)"), bank[:, n, :]).then_inc(sem("w1_t"), 1)
            act.wait_ge(sem("w1_out"), 1)
            for n in range(4):
                act.copy(out1_w[:].rearrange("p (k two) e -> p two k e", two=2)[:, n // 2, 4 * (n % 2):4 * (n % 2) + 4, :],
                         bank[:, n, :].rearrange("p (k e) -> p k e", k=4))\
                    .then_inc(sem("w1_out_sb"), 1)
            act.wait_ge(sem("w1_bias"), 1)
            act.activation(bias1[:], bank[:, 4, 0:1], ACT.Identity, bias=bo1_col[:]).then_inc(sem("bias1"), 1)
            act_norm_t(act, 2)
            for n in range(16):
                k, half = n // 2, n % 2
                act.wait_ge(sem("q1_made"), n + 1)
                act.activation(q1_proj[:, k, HALF * half:HALF * (half + 1)], bank[:, n % 4, 0:HALF], ACT.Identity,
                               bias=bq1_col[:, k:k + 1]).then_inc(sem("q1_proj"), 1)
            for n in range(2 * H):
                h, half = n // 2, n % 2
                act.wait_ge(sem("qk1_made"), n + 1)
                act.activation(q1[:, 0, 8 * half:8 * half + 8, S * h:S * (h + 1)],
                               bank[:, n % 4, 0:HALF].rearrange("p (b s) -> p b s", s=S), ACT.Copy, scale=SCALE1)\
                    .then_inc(sem("q1_high"), 1)
            act.wait_ge(sem("pad1"), 2)
            act_split1(act, 0, 0)

            def layer1(b, par, first, last):
                for t in range(T1):
                    if t == 0 and not first:
                        act_u1(act, b - 1, 1 - par, 0)
                    if t == 3 and not first:
                        act_u1(act, b - 1, 1 - par, 1)
                    if t == 3 and not last:
                        act_split1(act, b + 1, 1 - par)
                    if t == PROJ_AT + 1 and par == 0 and not first:
                        act_block(act, 1, b)
                    act_high1(act, b, par, t, 0)
                    if t < T1 - 1:
                        act_exp1(act, b, par, t + 1)
                    elif not last:
                        act_exp1(act, b + 1, 1 - par, 0)
                    act_high1(act, b, par, t, 1)
            act_exp1(act, 0, 0, 0)
            batches(act, layer1)
            act_u1(act, B - 1, 1, 0)
            act_u1(act, B - 1, 1, 1)
            act_block(act, 1, B)
            act.wait_ge(sem("block_done1"), B)
            act.sem_inc(sem("block_ready"), 1)

            act.wait_ge(sem("w_turned"), 3)
            for n in range(3):
                act.copy(w_tern_t[:, n].rearrange("p a b -> p (a b)"), bank[:, 1 + n, 0:256].bitcast(BF16))\
                    .then_inc(sem("w_t"), 1)
            act.wait_ge(sem("xq_turned"), 1)
            act.copy(xq_t[:].rearrange("p a b -> p (a b)"), bank[:, 4, 0:448].bitcast(BF16)).then_inc(sem("xq_t"), 1)

            def turned_h(t):
                act.wait_ge(sem("hq_turned"), t + 1)
                wait(act, sem("down1"), t - 1)
                act.copy(hq_t[:, t % 2].rearrange("p a b -> p (a b)"), bank[:, 4 + t % 2, 0:256].bitcast(BF16))\
                    .then_inc(sem("hq_t"), 1)
            for t in range(TT):
                act.wait_ge(sem("up1"), 2 * t + 1)
                wait(act, sem("act1"), t - 1)
                act.activation(silu1[:, t % 2, :], bank[:, 2 * (t % 2), :], ACT.Silu, scale=x_deq[:, t, 0:1])\
                    .then_inc(sem("silu1"), 1)
                if t >= 1:
                    turned_h(t - 1)
            turned_h(TT - 1)

        def dve_norm(dve, layer):
            for t in range(TT):
                if layer == 0:
                    dve.wait_ge(sem("in_x"), 16)
                else:
                    dve.wait_ge(sem("residual"), TT * (layer - 1) + t + 1)
                dve.bn_stats(stats[:, t, :], x_tok[:, t, :]).then_inc(sem("ln_stats"), 1)
            for t in range(TT):
                dve.wait_ge(sem("ln_stats"), TT * layer + t + 1)
                dve.bn_aggr(mean_var[:, t, :], stats[:, t, :]).then_inc(sem("ln_var"), 1)
            dve.wait_ge(sem("ln_rstd"), layer + 1)
            if layer == 2:
                dve.wait_ge(sem("xs_turned"), 1)
            for t in range(TT):
                dve.tensor_scalar(x_norm[:, t, :], x_tok[:, t, :], mean_var[:, t, 0:1], rstd[:, t:t + 1],
                                  ALU.subtract, ALU.mult).then_inc(sem("ln_norm"), 1)

        def dve_residual(dve, n, gate):
            for t in range(TT):
                dve.wait_ge(sem("block_turned"), TT * n + TT)
                dve.scalar_tensor_tensor(x_tok[:, t, :], bank[:, 5 + t // 4, 128 * (t % 4):128 * (t % 4 + 1)],
                                         tanh_g[:, gate:gate + 1], x_tok[:, t, :], ALU.mult, ALU.add)\
                    .then_inc(sem("residual"), 1)

        def dve_max0(dve, b, par, t):
            if t == 0:
                dve.wait_ge(sem("mask_done"), b + 1)
            wait_apart(dve, "dve", (sem("scores0"), b * T0 + t + 1), (sem("exp_done0"), b * T0 + t - 1))
            dve.tensor_tensor_reduce(out=masked[t % 2][:].rearrange("p (a k) -> p a k", a=3),
                                     in0=bank[0:R0, 0:3, 0:4 * KP],
                                     in1=mask_bias[par][:].rearrange("p (a c) k -> p a (c k)", a=3),
                                     scale=-SCALE0, scalar=3.0e38, op0=ALU.add, op1=ALU.min,
                                     accum_out=neg_max[0:R0, t:t + 1]).then_inc(sem("max_done0"), 1)

        def dve_low0(dve, b, par, t):
            g = t // 2
            for u in range(2):
                dve.wait_ge(sem("high_done0"), (b * T0 + t) * 2 + u + 1)
                cols = slice(R0 * (t % 2), R0 * (t % 2 + 1))
                dve.scalar_tensor_tensor(p_low0[g % 2][:, UC * u:UC * (u + 1), cols],
                                         pair_chunks(unit_no(0, par, ("turn", t, u)), R0), PSCALE,
                                         p_high0[g % 2][:, UC * u:UC * (u + 1), cols], ALU.mult, ALU.subtract)\
                    .then_inc(sem("low_done0"), 1)

        def dve_inv0(dve, b, par, g):
            dve.wait_ge(sem("exp_done0"), b * T0 + 2 * g + 2)
            wait(dve, sem("inv_spread"), (b - 1) * G + g + 1)
            dve.tensor_scalar(row_sum[0:R0, 2 * g:2 * g + 2], row_sum[0:R0, 2 * g:2 * g + 2], PSCALE, None, ALU.mult)\
                .then_inc(sem("sum_scaled"), 1)
            dve.wait_ge(sem("sum_scaled"), b * G + g + 1)
            dve.reciprocal(row_inv[0:R0, 2 * g:2 * g + 2], row_sum[0:R0, 2 * g:2 * g + 2]).then_inc(sem("inv_done0"), 1)

        def dve_u0(dve, b, par, g):
            dve.wait_ge(sem("inv_sb"), b * G + g + 1)
            if g == 0 and par == 0:
                wait(dve, sem("projected0"), b)
            dve.tensor_tensor(u0[:, par, g, :], bank[:, U_BANK, 0:GC], inv_b[:], ALU.mult).then_inc(sem("u_done0"), 1)

        def dve_context(dve, layer, b, par, halves):
            dst = c_t0 if layer == 0 else c_t1[par]
            first = isinstance(b, int) and b == 0
            for n in halves:
                dve.wait_ge(sem(f"ct_turned{layer}"), 2 * b + n + 1)
                if layer == 0 and not first:
                    for g in (2 * n, 2 * n + 1):
                        dve.wait_ge(sem(f"stack{1 - par}_{g}"), per_use(b - 1, 1 - par, 32))
                if layer == 1 and n == 0:
                    wait(dve, sem("scores1"), (b - 1) * (3 * T1))
                no = unit_no(layer, 1 - par, ("prep", n, 0)) if not first else n
                dve.tensor_copy(dst[:, n].rearrange("p c k -> p (c k)"), pair_flat(no, F16)[:, 0:KC * 128])\
                    .then_inc(sem(f"ct_done{layer}_{n}"), 1)

        def dve_max1(dve, b, par, t):
            for k in range(3):
                dve.wait_ge(sem("scores1"), (b * T1 + t) * 3 + k + 1)
                dve.tensor_reduce(bank_max[:, t, k:k + 1], bank[:, k, 0:4 * KP], AX.X, ALU.max, negate=True)\
                    .then_inc(sem("bank_max"), 1)
            dve.wait_ge(sem("bank_max"), (b * T1 + t) * 3 + 3)
            wait(dve, sem("exp_done1"), (b - 1) * T1 + t + 1)
            dve.tensor_reduce(neg_max[:, t:t + 1], bank_max[:, t, :], AX.X, ALU.min).then_inc(sem("max_done1"), 1)

        def dve_norm1(dve, b, par, t):
            dve.wait_ge(sem("exp_done1"), b * T1 + t + 1)
            dve.reciprocal(row_inv[:, t:t + 1], row_sum[:, t:t + 1]).then_inc(sem("inv_done1"), 1)
            dve.wait_ge(sem("inv_done1"), b * T1 + t + 1)
            e = e_row[(t + par) % 2][:]
            dve.tensor_scalar(e, e, row_inv[:, t:t + 1], PSCALE, ALU.mult, ALU.mult).then_inc(sem("norm_done1"), 1)

        def dve_low1(dve, b, par, t, u):
            grp = 0 if t < 4 else 1
            at = t - GROUPS1[grp][0]
            dve.wait_ge(sem("high_done1"), (b * T1 + t) * 2 + u + 1)
            part = (slice(None), slice(UC * u, UC * (u + 1)), slice(128 * at, 128 * (at + 1)))
            dve.tensor_tensor(p_low1[grp][part], pair_chunks(unit_no(1, par, ("turn", t, u)), 128),
                              p_high1[grp][part], ALU.subtract).then_inc(sem("low_done1"), 1)

        @block.vector
        def _(dve):
            dve_norm(dve, 0)
            dve.wait_ge(sem("in_w8"), 16 * 3 * H)
            dve.wait_ge(sem("const"), 6 + NE)
            for n in range(3):
                dve.tensor_tensor(block_diag[:, n, :].rearrange("p (h d) -> p h d", d=D0),
                                  w8[:, n, :].unsqueeze(1).broadcast_to((128, H, D0)),
                                  head_of[:].unsqueeze(2).broadcast_to((128, H, D0)), ALU.mult).then_inc(sem("diag"), 1)
            dve.wait_ge(sem("diag"), 3)
            dve.wait_ge(sem("w0_a"), 1)
            for heads, parts, src in ((a_heads, 3, bank[:, 2, 0:E]), (v_heads, 4, block_diag[:, 2, :])):
                for part in range(parts):
                    for g in range(G):
                        base = heads[:, HG * g:HG * (g + 1), part, :].rearrange("p h k -> p h k")
                        dst = diagonal(base)
                        dve.tensor_copy(dst, src.rearrange("p (g h d) -> p g h d", g=G, d=D0)[:, g])\
                            .then_inc(sem("w0_place"), 1)
            dve.wait_ge(sem("w0_place"), 7 * G)
            for _ in range(7):
                dve.sem_inc(sem("w0_sb"), 1)
            for n in range(2 * H):
                h, half = n // 2, n % 2
                dve.wait_ge(sem("q0_high"), n + 1)
                low = q0[64:96, 8 * half:8 * half + 8, S * h:S * (h + 1)]
                dve.tensor_tensor(low, bank[64:96, n % 4, 0:HALF].rearrange("p (b s) -> p b s", s=S), low,
                                  ALU.subtract).then_inc(sem("q0_low"), 1)
            dve_context(dve, 0, 0, 0, (0, 1))
            dve_max0(dve, 0, 0, 0)

            def layer0(b, par, first, last):
                for t in range(T0):
                    if t < T0 - 1:
                        dve_max0(dve, b, par, t + 1)
                    elif not last:
                        dve_max0(dve, b + 1, 1 - par, 0)
                    if t % 2 == 0 and t >= 4:
                        dve_u0(dve, b, par, t // 2 - 2)
                    elif t % 2 == 0 and not first:
                        dve_u0(dve, b - 1, 1 - par, t // 2 + 2)
                    if t in PREP_AT[0] and not last:
                        dve_context(dve, 0, b + 1, 1 - par, (PREP_AT[0].index(t),))
                    dve_low0(dve, b, par, t)
                    if t % 2 == 1:
                        dve_inv0(dve, b, par, t // 2)
            batches(dve, layer0)
            dve_u0(dve, B - 1, 1, 2)
            dve_u0(dve, B - 1, 1, 3)
            dve.wait_ge(sem("tanh_g"), 1)
            dve_residual(dve, 0, 0)

            dve_norm(dve, 1)
            dve.wait_ge(sem("logits"), 1)
            dve.tensor_copy(logits[:].rearrange("p t e -> p (t e)"), bank[:, 2, 0:TT * NE]).then_inc(sem("route"), 1)
            dve.wait_ge(sem("route"), 1)
            dve.tensor_reduce(top[:], logits[:], AX.X, ALU.max).then_inc(sem("top"), 1)
            dve.wait_ge(sem("top"), 1)
            top_b = top[:].unsqueeze(2).broadcast_to((128, TT, NE))
            id_b = expert_id[:].unsqueeze(1).broadcast_to((128, TT, NE))
            dve.tensor_tensor(is_top[:], logits[:], top_b, ALU.is_equal).then_inc(sem("route"), 1)
            dve.wait_ge(sem("route"), 2)
            dve.tensor_tensor(is_top[:], is_top[:], id_b, ALU.mult).then_inc(sem("route"), 1)
            dve.wait_ge(sem("route"), 3)
            dve.tensor_reduce(first_top[:], is_top[:], AX.X, ALU.min).then_inc(sem("route"), 1)
            dve.wait_ge(sem("route"), 4)
            dve.tensor_tensor(one_hot[:], id_b, first_top[:].unsqueeze(2).broadcast_to((128, TT, NE)),
                              ALU.is_equal).then_inc(sem("one_hot"), 1)
            dve.wait_ge(sem("score_exp"), 1)
            dve.tensor_scalar(score[:], score[:], 1.0, None, ALU.add).then_inc(sem("route"), 1)
            dve.wait_ge(sem("route"), 5)
            dve.reciprocal(score[:], score[:]).then_inc(sem("route"), 1)
            dve.wait_ge(sem("route"), 6)
            dve.wait_ge(sem("ln_turned"), 2 * TT)
            dve.tensor_tensor(x_norm[:], x_norm[:], score[:].unsqueeze(2).broadcast_to((128, TT, E)), ALU.mult)\
                .then_inc(sem("x_scored"), 1)

            dve.wait_ge(sem("xs_t"), 1)

            def expert_tokens(n):
                half, e = n // (NE + 1), n % (NE + 1)
                if e < NE:
                    r = half * NE + e
                    dve.wait_ge(sem("hot_rows"), r + 1)
                    before = n - 2 if (n - 2) % (NE + 1) < NE else n - 3
                    wait(dve, sem("up0"), 2 * IC * (n - 1) if n >= 2 else 0)
                    dve.tensor_tensor(x_exp[:, r % 2, :], bank[:, 0, 0:HALF],
                                      x_score_t[:, HALF * half:HALF * (half + 1)], ALU.mult).then_inc(sem("x_exp"), 1)
            expert_tokens(0)
            for m in range(2 * (NE + 1) * IC):
                if m % IC == 0 and m // IC + 1 < 2 * (NE + 1):
                    expert_tokens(m // IC + 1)
                dve.wait_ge(sem("silu0"), m + 1)
                dve.wait_ge(sem("up0"), 2 * m + 2)
                wait(dve, sem("down0"), m - 1)
                dve.tensor_tensor(act0[:, m % 2, :], bank[:, 2 + 2 * (m % 2), 0:HALF], silu0[:, m % 2, :], ALU.mult)\
                    .then_inc(sem("act0"), 1)
            dve_residual(dve, 1, 2)
            dve_norm(dve, 2)
            for n in range(2 * H):
                h, half = n // 2, n % 2
                dve.wait_ge(sem("q1_high"), n + 1)
                part = (slice(None), slice(8 * half, 8 * half + 8), slice(S * h, S * (h + 1)))
                dve.scalar_tensor_tensor(q1[:, 1][part], bank[:, n % 4, 0:HALF].rearrange("p (b s) -> p b s", s=S), SCALE1,
                                         q1[:, 0][part], ALU.mult, ALU.subtract).then_inc(sem("q1_low"), 1)
            dve_context(dve, 1, 0, 0, (0, 1))
            dve_max1(dve, 0, 0, 0)
            dve_norm1(dve, 0, 0, 0)

            def layer1(b, par, first, last):
                for t in range(T1):
                    nxt = (b, par, t + 1) if t < T1 - 1 else (b + 1, 1 - par, 0)
                    if t - 1 in PREP_AT[1] and not last:
                        dve_context(dve, 1, b + 1, 1 - par, (PREP_AT[1].index(t - 1),))
                    if not (last and t == T1 - 1):
                        dve_max1(dve, *nxt)
                    dve_low1(dve, b, par, t, 0)
                    if not (last and t == T1 - 1):
                        dve_norm1(dve, *nxt)
                    dve_low1(dve, b, par, t, 1)
            batches(dve, layer1)

            dve.wait_ge(sem("in_wf"), 48)
            for n in range(3):
                dve.tensor_reduce(abs_sum[:, n:n + 1], wg_sb[:, n].rearrange("p a b -> p (a b)"), AX.X, ALU.add,
                                  apply_absolute_value=True).then_inc(sem("w_abs"), 1)
            dve_residual(dve, 2, 1)
            dve.wait_ge(sem("w_abs_all"), 1)
            dve.tensor_scalar(w_mean[:], bank[:, 0, 0:3], 1.0 / (INNER1 * E), 1e-5, ALU.mult, ALU.max)\
                .then_inc(sem("w_stat"), 1)
            dve.wait_ge(sem("w_stat"), 1)
            dve.reciprocal(w_scale[:], w_mean[:]).then_inc(sem("w_stat"), 1)
            dve.wait_ge(sem("w_stat"), 2)
            for n in range(3):
                w, r = wg_sb[:, n], w_round[:, n]
                dve.tensor_scalar(r, w, w_scale[:, n:n + 1], ROUND, ALU.mult, ALU.add).then_inc(sem("w_q"), 1)
                dve.wait_ge(sem("w_q"), 2 * n + 1)
                dve.tensor_scalar(r, r, -ROUND, 1.0, ALU.add, ALU.min).then_inc(sem("w_q"), 1)
                dve.wait_ge(sem("w_q"), 2 * n + 2)
                dve.tensor_scalar(w_tern[:, n], r, -1.0, None, ALU.max).then_inc(sem("w_tern"), 1)
            dve_norm(dve, 3)
            dve.wait_ge(sem("ln_norm"), 4 * TT)
            dve.tensor_reduce(x_amax[:], x_norm[:], AX.X, ALU.max, apply_absolute_value=True).then_inc(sem("xq_s"), 1)
            dve.wait_ge(sem("xq_s"), 1)
            dve.tensor_scalar(x_amax[:], x_amax[:], 1e-5, None, ALU.max).then_inc(sem("xq_s"), 1)
            dve.wait_ge(sem("xq_s"), 2)
            dve.reciprocal(x_qscale[:], x_amax[:]).then_inc(sem("xq_s"), 1)
            dve.wait_ge(sem("xq_s"), 3)
            dve.tensor_scalar(x_qscale[:], x_qscale[:], 127.0, None, ALU.mult).then_inc(sem("xq_s"), 1)
            for n in range(2):
                dve.tensor_scalar(x_deq[:, :, n], x_amax[:], 1.0 / 127.0, w_mean[:, n:n + 1], ALU.mult, ALU.mult)\
                    .then_inc(sem("xq_s"), 1)
            dve.wait_ge(sem("xq_s"), 6)
            dve.tensor_tensor(x_norm[:], x_norm[:], x_qscale[:].unsqueeze(2).broadcast_to((128, TT, E)), ALU.mult)\
                .then_inc(sem("xq_s"), 1)
            dve.wait_ge(sem("xq_s"), 7)
            dve.tensor_scalar(x_norm[:], x_norm[:], ROUND, None, ALU.add).then_inc(sem("xq_s"), 1)
            dve.wait_ge(sem("xq_s"), 8)
            dve.tensor_scalar(x_norm[:], x_norm[:], -ROUND, 127.0, ALU.add, ALU.min).then_inc(sem("xq_s"), 1)
            dve.wait_ge(sem("xq_s"), 9)
            dve.tensor_scalar(xq[:], x_norm[:], -128.0, None, ALU.max).then_inc(sem("xq"), 1)

            def finish(t):
                dve.wait_ge(sem("down1"), t + 1)
                dve.scalar_tensor_tensor(x_tok[:, t, :], bank[:, 6 + t % 2, 0:128], h_deq[:, t:t + 1], x_tok[:, t, :],
                                         ALU.mult, ALU.add).then_inc(sem("final"), 1)
            for t in range(TT):
                dve.wait_ge(sem("up1"), 2 * t + 2)
                dve.wait_ge(sem("silu1"), t + 1)
                a = act1[:, t % 2, :]
                dve.scalar_tensor_tensor(a, bank[:, 2 * (t % 2) + 1, :], x_deq[:, t, 1:2], silu1[:, t % 2, :],
                                         ALU.mult, ALU.mult).then_inc(sem("act1"), 1)
                dve.wait_ge(sem("act1"), t + 1)
                dve.tensor_reduce(h_amax[:, t:t + 1], a, AX.X, ALU.max, apply_absolute_value=True).then_inc(sem("hq_s"), 1)
                dve.wait_ge(sem("hq_s"), 7 * t + 1)
                dve.tensor_scalar(h_amax[:, t:t + 1], h_amax[:, t:t + 1], 1e-5, None, ALU.max).then_inc(sem("hq_s"), 1)
                dve.wait_ge(sem("hq_s"), 7 * t + 2)
                dve.reciprocal(h_qscale[:, t:t + 1], h_amax[:, t:t + 1]).then_inc(sem("hq_s"), 1)
                dve.tensor_scalar(h_deq[:, t:t + 1], h_amax[:, t:t + 1], 1.0 / 127.0, w_mean[:, 2:3], ALU.mult, ALU.mult)\
                    .then_inc(sem("hq_s"), 1)
                dve.wait_ge(sem("hq_s"), 7 * t + 4)
                dve.tensor_scalar(h_deq[:, t:t + 1], h_deq[:, t:t + 1], tanh_g[:, 3:4], None, ALU.mult).then_inc(sem("hq_s"), 1)
                dve.tensor_scalar(h_qscale[:, t:t + 1], h_qscale[:, t:t + 1], 127.0, None, ALU.mult).then_inc(sem("hq_s"), 1)
                dve.wait_ge(sem("hq_s"), 7 * t + 6)
                dve.tensor_scalar(a, a, h_qscale[:, t:t + 1], ROUND, ALU.mult, ALU.add).then_inc(sem("hq_s"), 1)
                dve.wait_ge(sem("hq_s"), 7 * t + 7)
                dve.tensor_scalar(a, a, -ROUND, 127.0, ALU.add, ALU.min).then_inc(sem("hq_r"), 1)
                dve.wait_ge(sem("hq_r"), t + 1)
                wait(dve, sem("hq_turned"), t - 1)
                dve.tensor_scalar(hq[:, t % 2, :], a, -128.0, None, ALU.max).then_inc(sem("hq"), 1)
                if t >= 1:
                    finish(t - 1)
            finish(TT - 1)


def diagonal(t):
    dims = [list(d) for d in t.ap]
    step = dims[1][0]
    return bass.AP(tensor=t.tensor, offset=t.offset, ap=[dims[0], [step + 8, dims[1][1]], [1, 8]])


_INS = ['x', 'ctx_1024', 'mask_Bx1xSxS2_if1', 'g_xattn', 'g_ffn', 'L0_xattn_Wv', 'L0_xattn_Wk', 'L0_xattn_Wq',
        'L0_xattn_Wo', 'L0_xattn_bo', 'L0_ffn_gate_w', 'L0_ffn_sh_gate', 'L0_ffn_sh_up', 'L0_ffn_sh_down',
        'L0_ffn_rt_gate', 'L0_ffn_rt_up', 'L0_ffn_rt_down', 'L1_xattn_Wq', 'L1_xattn_bq', 'L1_xattn_Wkv',
        'L1_xattn_bkv', 'L1_xattn_Wo', 'L1_xattn_bo', 'L1_ffn_w_gate', 'L1_ffn_w_up', 'L1_ffn_w_down']


def build(nc, arrays_of):
    args = [nc.dram_tensor(f"in_{n}", a.shape, mybir.dt.from_np(a.dtype), kind="ExternalInput").ap()
            for n, a in arrays_of.items()]
    out = nc.dram_tensor("out_x", arrays_of['x'].shape, F32, kind="ExternalOutput").ap()
    flamingo_kernel(nc, *args, out)


def kernel(**inputs):
    import numpy as np
    import concourse.bacc as bacc
    from concourse.bass_utils import run_bass_kernel_spmd

    nc = bacc.Bacc("TRN2", target_bir_lowering=False, num_devices=1)
    arrays = {n: np.ascontiguousarray(inputs[n]) for n in _INS}
    build(nc, arrays)
    r = run_bass_kernel_spmd(nc, [{f"in_{n}": a for n, a in arrays.items()}], core_ids=[0])
    return r.results[0]["out_x"]
```

```python
import concourse.bass as bass
from concourse import mybir
from contextlib import ExitStack

F32 = mybir.dt.float32
F16 = mybir.dt.float16
BF16 = mybir.dt.bfloat16
I32 = mybir.dt.int32
ALU = mybir.AluOpType
ACT = mybir.ActivationFunctionType
AX = mybir.AxisListType


def wait(engine, semaphore, value):
    if not isinstance(value, int) or value > 0:
        engine.wait_ge(semaphore, value)


def flamingo_kernel(nc, x, ctx_in, mask, g_xattn, g_ffn,
                    wv0, wk0, wq0, wo0, bo0, gate_w, sh_gate, sh_up, sh_down, rt_gate, rt_up, rt_down,
                    wq1, bq1, wkv1, bkv1, wo1, bo1, w_gate, w_up, w_down, out):
    B, S, E = x.shape
    S2 = ctx_in.shape[1]
    H = 16
    D0 = E // H
    D1 = wq1.shape[0] // H
    KC = 12
    KP = S2 // KC
    ROWS = H * S
    NTOK = B * S
    TT = NTOK // 128
    HALF = NTOK // 2
    G = 4
    HG = H // G
    GC = HG * S
    T0 = 8
    R0 = 2 * S
    T1 = ROWS // 128
    UC = KC // 2
    NE = gate_w.shape[1]
    INNER0 = sh_gate.shape[1]
    IC = INNER0 // 128
    INNER1 = w_gate.shape[0]
    JC = INNER1 // 128
    EPS = 1e-5
    NEG = -1e20
    SCALE0 = float(E) ** -0.5
    SCALE1 = float(D1) ** -0.5
    PSCALE = 2.0 ** 14
    W_SCALE = 2.0 ** 8
    ROUND = 1.5 * 2.0 ** 23
    LAST = B // 2 - 1
    EARLY = (B - 2) * S // 128

    ctx = ExitStack()
    with ctx:
        def sb(name, shape, dt=F32):
            return ctx.enter_context(nc.sbuf_tensor(name, shape, dt))

        sems = {}

        def sem(name):
            if name not in sems:
                sems[name] = ctx.enter_context(nc.semaphore(name))
            return sems[name]

        ident = sb("ident", [128, 128])
        ident16 = sb("ident16", [128, 128], F16)
        ones_f = sb("ones_f", [128, 128])
        half_neg = sb("half_neg", [128, TT])
        head_of = sb("head_of", [128, H])
        place = sb("place", [128, HG, 32])
        expert_id = sb("expert_id", [128, NE])
        expert_row = sb("expert_row", [NE, NE, 128], F16)
        x_tok = sb("x_tok", [128, TT, E])
        x_norm = sb("x_norm", [128, TT, E])
        x_norm_t = sb("x_norm_t", [128, NTOK])
        stats = sb("stats", [128, TT, 6])
        mean_var = sb("mean_var", [128, TT, 2])
        rstd = sb("rstd", [128, TT])
        block_t = sb("block_t", [128, NTOK])
        gates = sb("gates", [128, 4])
        tanh_g = sb("tanh_g", [128, 4])
        bo0_col = sb("bo0_col", [128, 1])
        bo1_col = sb("bo1_col", [128, 1])

        gate_w_sb = sb("gate_w_sb", [128, NE])
        g_w = sb("g_w", [128, NE + 1, INNER0])
        u_w = sb("u_w", [128, NE + 1, INNER0])
        warm = sb("warm", [128, 1])
        q_bias = sb("q_bias", [128, H])
        logits = sb("logits", [128, TT, NE])
        top = sb("top", [128, TT])
        is_top = sb("is_top", [128, TT, NE])
        first_top = sb("first_top", [128, TT])
        one_hot = sb("one_hot", [128, TT, NE])
        one_hot_t = sb("one_hot_t", [NE, NTOK], F16)
        score = sb("score", [128, TT])

        bq1_pad = sb("bq1_pad", [128, 8, 2])
        bv1_col = sb("bv1_col", [128, 8])
        bias1 = sb("bias1", [128, 1])

        wg_sb = sb("wg_sb", [128, 3, JC, 128])
        abs_sum = sb("abs_sum", [128, 3])
        w_mean = sb("w_mean", [128, 3])
        down_scale = sb("down_scale", [128, 1])
        w_scale = sb("w_scale", [128, 3])
        ident_b = sb("ident_b", [128, 128], BF16)
        x_amax = sb("x_amax", [128, TT])
        x_qscale = sb("x_qscale", [128, TT])
        x_deq = sb("x_deq", [128, TT, 2])
        h_amax = sb("h_amax", [128, TT])
        h_qscale = sb("h_qscale", [128, TT])
        h_deq = sb("h_deq", [128, TT])

        c_in = [sb(f"c_in{p}", [KP, KC, E]) for p in range(2)]
        e_row = [sb(f"e_row{p}", [128, S2]) for p in range(2)]
        neg_max = sb("neg_max", [128, T0])
        bank_max = sb("bank_max", [128, T1, 3])
        row_sum = sb("row_sum", [128, T0])
        row_inv = sb("row_inv", [128, T0])

        REGION = 35072
        region = sb("region", [128, REGION])
        at = [0]

        def carve(shape, dt=F32):
            size = 1
            for n in shape[1:]:
                size *= n
            words = size if dt in (F32, I32) else (size + 1) // 2
            t = region[0:shape[0], at[0]:at[0] + words]
            at[0] += words
            assert at[0] <= REGION, at[0]
            if dt is not F32:
                t = t.bitcast(dt)
            if len(shape) > 2:
                dims = [f"d{n}" for n in range(len(shape) - 1)]
                t = t.rearrange(f"p ({' '.join(dims)}) -> p {' '.join(dims)}", **dict(zip(dims, shape[1:])))
            return t

        q0 = carve([96, B, ROWS], F16)
        c_stack = [carve([96, G, KC, 128], F16) for _ in range(2)]
        c_group = [carve([KP, KC, G, 64], F16) for _ in range(2)]
        group_at = at[0] - KC * G * 64
        split_at = at[0]
        c_split0 = carve([128, KC, G, 2, 32], F16)
        c_t0 = carve([128, 2, KC, 128], F16)
        mask_in = carve([R0, S2], I32)
        mask_bias = [carve([R0, KC, KP], BF16) for _ in range(2)]
        masked = [carve([R0, S2]) for _ in range(2)]
        inv_b = carve([128, GC])
        u0 = carve([128, 2, G, GC])
        out0_w = carve([128, H, 128])
        before_p0 = at[0]
        p_high0 = [carve([KP, KC, GC], F16) for _ in range(2)]
        p_low0 = [carve([KP, KC, GC], F16) for _ in range(2)]
        at[0] = before_p0
        a_heads = carve([128, H, 3, 32])
        v_heads = carve([128, H, 4, 32])
        w8 = carve([128, 3, D0])
        block_diag = carve([128, 3, E])
        wo0_sb = carve([128, E])
        wo0_t = carve([128, E])

        at[0] = 0
        wo1_sb = carve([128, 8, 128])
        wq1_sb = carve([128, 8, 128])
        wk1_sb = carve([128, 8, 128])
        wv1_sb = carve([128, 8, 128])
        wo1_t = carve([128, 8, 128])
        queries_dead = at[0]
        d_w = carve([128, NE + 1, IC, 128])
        g_split = carve([128, NE + 1, 2, INNER0], F16)
        u_split = carve([128, NE + 1, 2, INNER0], F16)
        scores_dead = at[0]
        d_split = carve([128, NE + 1, 2, IC, 128], F16)

        at[0] = 0
        q1 = carve([128, 2, B, ROWS], F16)
        out1_w = carve([128, H, 128])
        assert queries_dead <= (B - 3) * ROWS // 2 and scores_dead <= group_at
        assert at[0] == split_at
        c_split1 = carve([128, KC, 2, E], F16)
        c_keep1 = [carve([128, KC, 2, E], F16)[0:KP],
                   g_w[:].rearrange("p e i -> p (e i)")[0:KP, 0:KC * E].bitcast(F16)
                   .rearrange("p (c n e) -> p c n e", c=KC, n=2)]
        c_t1 = [carve([128, 2, KC, 128], F16) for _ in range(2)]
        GROUPS1 = [(0, 4), (4, T1)]
        before_p1 = at[0]
        p_high1 = [carve([KP, KC, 128 * (b - a)], F16) for a, b in GROUPS1]
        p_low1 = [carve([KP, KC, 128 * (b - a)], F16) for a, b in GROUPS1]
        u1 = carve([128, 2, ROWS])
        at[0] = before_p1
        a1_w = carve([128, H, 128])
        xs_split = carve([128, 2, NTOK], F16)
        xn_split = carve([128, 2, NTOK], F16)
        x_exp = [carve([128, 2, 512], F16) for _ in range(2)]
        hot_mask = [carve([128, 512], F16) for _ in range(2)]
        silu0 = carve([128, 2, 512])
        act0 = carve([128, 2, 512])
        act_split = [carve([128, 2, 512], F16) for _ in range(3)]

        g_flat, u_flat = (w[:].rearrange("p e i -> p (e i)") for w in (g_w, u_w))
        words = 3 * JC * 128
        w_round = g_flat[:, 0:words].rearrange("p (n j h) -> p n j h", n=3, j=JC)
        w_tern, w_tern_t = (t.bitcast(BF16).rearrange("p (n j h) -> p n j h", n=3, j=JC)
                            for t in (g_flat[:, words:words + words // 2], u_flat[:, 0:words // 2]))
        at[0] = 0
        xq = carve([128, TT, E], BF16)
        xq_t = carve([128, TT, 128], BF16)
        hq = carve([128, 2, INNER1], BF16)
        hq_t = carve([128, 2, JC, 128], BF16)
        silu1 = carve([128, 2, INNER1])
        act1 = carve([128, 2, INNER1])

        bank = ctx.enter_context(nc.psum_tensor("bank", [128, 8, 512], F32))
        U_BANK = 7

        def pair(u):
            return bank[:, 3 + 2 * (u % 2):5 + 2 * (u % 2), :]

        def pair_flat(u, dt=F32):
            t = pair(u).rearrange("p a b -> p (a b)")
            return t if dt is F32 else t.bitcast(dt)

        def pair_chunks(u, cols):
            return pair_flat(u)[0:KP, 0:UC * 128].rearrange("p (c n) -> p c n", n=128)[:, :, 0:cols]

        block = ctx.enter_context(nc.Block())

        turns = {layer: [[("turn", t, 0), ("turn", t, 1)] for t in range(tiles)] for layer, tiles in ((0, T0), (1, T1))}
        PROJ, NONE, PREP_0, PREP_1 = ("proj", 0, 0), ("none", 0, 0), ("prep", 0, 0), ("prep", 1, 0)
        PROJ_AT, PREP_AT = 3, {0: (2, 4), 1: (3, 4)}
        UNITS = {(0, par): sum(([PROJ] * (t == PROJ_AT and par == 0) + [PREP_0] * (t == PREP_AT[0][0])
                                + [PREP_1] * (t == PREP_AT[0][1]) + turns[0][t - 1][1:] * (t > 0) + turns[0][t][:1]
                                + [NONE] * (t == 6 and par == 0) for t in range(T0)), []) + turns[0][T0 - 1][1:]
                 for par in range(2)}
        UNITS.update({(1, par): sum(turns[1][:4], []) + [PREP_0] + turns[1][4] + [PREP_1] + sum(turns[1][5:], [])
                      for par in range(2)})

        def unit_no(layer, par, what):
            return UNITS[layer, par].index(what)

        def consumed(layer, b, what):
            kind, n, u = what
            tiles = T0 if layer == 0 else T1
            if kind == "turn":
                return sem(f"low_done{layer}"), b * (2 * tiles) + 2 * n + u + 1
            if kind == "proj":
                return sem(f"block_done{layer}"), b
            if isinstance(b, int) and b == B - 1:
                return sem("residual"), 2 * TT + EARLY
            return sem(f"ct_done{layer}_{n}"), b + 2

        def wait_pair(engine, layer, b, par, what):
            units = UNITS[layer, par]
            k, back = units.index(what) - 2, 0
            while True:
                if k < 0:
                    back, par = back + 1, 1 - par
                    units = UNITS[layer, par]
                    k += len(units)
                before = units[k]
                fixed = isinstance(b, int)
                if fixed and b - back < 0:
                    n = k - (len(units) - 2)
                    if n in (0, 1):
                        wait(engine, sem(f"ct_done{layer}_{n}"), 1)
                    return
                absent = fixed and (b - back == B or (before[0] == "proj" and b - back == 0)
                                    or (before[0] == "prep" and b - back == B - 1 and (layer, before) != (1, PREP_0)))
                if absent or before[0] == "none":
                    k -= 2
                    continue
                s, v = consumed(layer, b - back, before)
                wait(engine, s, v)
                return

        def wait_apart(engine, name, *waits):
            for semaphore, count in waits:
                wait(engine, semaphore, count)
            engine.sem_inc(sem(f"passed_{name}"), 1)

        def batches(engine, body):
            body(0, 0, True, False)
            body(1, 1, False, False)
            with engine.Fori(1, LAST) as i:
                body(i * 2, 0, False, False)
                body(i * 2 + 1, 1, False, False)
            body(B - 2, 0, False, False)
            body(B - 1, 1, False, True)

        def per_use(b, par, n):
            if isinstance(b, int):
                return ((b - par) // 2 + 1) * n
            return (b - par) * (n // 2) + n

        def tern_turned(n):
            return bank[:, 7, :].bitcast(BF16)[:, 512 * (n % 2):512 * (n % 2 + 1)]

        UNITS0 = 2 * (NE + 1) * IC
        FFN_HALVES = [(0, 512), (512, NTOK)]

        def in_banks_56(t):
            return bank[:, 5 + t // 4, 128 * (t % 4):128 * (t % 4 + 1)]

        def early_turned(t):
            return pair_flat(unit_no(1, 1, PREP_0))[:, 128 * t:128 * (t + 1)]

        def late_turned(t):
            return bank[:, 7, 128:256]

        LATE_AT = 3
        assert EARLY == TT - 1

        def in_bank_7(t):
            return bank[:, 7, 128 * (t % 4):128 * (t % 4 + 1)]

        def load(engine, name, pairs):
            for dst, src in pairs:
                few = src.shape[-1] * src.shape[0] <= 1024 or len(src.shape) == 2 and src.shape[1] <= 8
                engine.dma_start(dst, src, allow_slow_non_contiguous=few).then_inc(sem(name), 16)

        def sync_load_context(sp, layer, b, par):
            wait_apart(sp, "sp", (sem("low0" if layer == 0 else "split_done1"), b - 1))
            sp.dma_start(c_in[par][:], ctx_in[b].rearrange("(p c) e -> p c e", c=KC))\
                .then_inc(sem(f"ctx_in{layer}_{par}"), 16)

        def sync_load_mask(sp, b):
            wait_apart(sp, "sp", (sem("mask_done"), b))
            for two in range(2):
                sp.dma_start(mask_in[two * S:(two + 1) * S, :], mask[b, 0]).then_inc(sem("mask_in"), 16)

        def sync_stack(sp, b, par):
            wait_apart(sp, "sp", (sem("scores0"), (b - 1) * T0))
            for g in range(G):
                if g % 2 == 0:
                    wait_apart(sp, "sp", (sem(f"ct_done0_{g // 2}"), b + 1))
                rows = 64 * (g % 2)
                sp.dma_start(c_stack[par][0:64, g], c_t0[rows:rows + 64, g // 2]).then_inc(sem(f"stack{par}_{g}"), 16)
                sp.dma_start(c_stack[par][64:96, g], c_t0[rows:rows + 32, g // 2]).then_inc(sem(f"stack{par}_{g}"), 16)

        def sync_keep(sp, layer, b, par):
            split, done = ("low0", G) if layer == 0 else ("split_done1", 2)
            wait_apart(sp, "sp", (sem(split), b + 1))
            wait_apart(sp, "sp", (sem(f"pv_done{layer}"), done * (b - 1)))
            source = c_split0[0:KP].rearrange("p c g two d -> p c g (two d)") if layer == 0 else c_split1[0:KP]
            sp.dma_start(c_group[par] if layer == 0 else c_keep1[par], source).then_inc(sem(f"kept{layer}"), 16)

        @block.sync
        def _(sp):
            load(sp, "in_x", [(x_tok[:], x.rearrange("b s e -> (b s) e").rearrange("(t p) e -> p t e", p=128))])
            for n, w in enumerate((wq0, wk0, wv0)):
                sp.dma_start(w8[:, n, :], w.unsqueeze(0).broadcast_to((H, D0, D0))).then_inc(sem("in_w8"), 16)
            load(sp, "in_w0", [(wo0_sb[:], wo0), (bo0_col[:], bo0.rearrange("(e o) -> e o", o=1))])
            sync_load_context(sp, 0, 0, 0)
            sync_load_mask(sp, 0)

            def layer0(b, par, first, last):
                if last:
                    sp.wait_ge(sem("scores0"), (B - 3) * T0)
                    load(sp, "in_w1", [(wo1_sb[:], wo1.rearrange("e (k p) -> e k p", p=128)),
                                       (wq1_sb[:], wq1.rearrange("(k p) e -> p k e", p=128))])
                    kv = wkv1.rearrange("(k two part d) e -> two part d k e", two=2, part=2, d=D1)
                    for two in range(2):
                        load(sp, "in_w1", [(wk1_sb[64 * two:64 * two + 64], kv[two, 0]),
                                           (wv1_sb[64 * two:64 * two + 64], kv[two, 1])])
                else:
                    sync_load_context(sp, 0, b + 1, 1 - par)
                    sync_load_mask(sp, b + 1)
                    sync_stack(sp, b + 1, 1 - par)
                    sync_keep(sp, 0, b + 1, 1 - par)
            sync_stack(sp, 0, 0)
            sync_keep(sp, 0, 0, 0)
            batches(sp, layer0)
            sync_load_context(sp, 1, 0, 0)
            sp.wait_ge(sem("scores0"), B * T0)
            load(sp, "in_down0", [
                (d_w[:, 0:NE].rearrange("p e c h -> p (e c) h"), rt_down.rearrange("e (c p) h -> p (e c) h", p=128)),
                (d_w[:, NE], sh_down.rearrange("(c p) h -> p c h", p=128))])

            sp.wait_ge(sem("w_tern"), 3)
            sync_keep(sp, 1, 0, 0)

            def layer1(b, par, first, last):
                if not last:
                    sync_load_context(sp, 1, b + 1, 1 - par)
                    sync_keep(sp, 1, b + 1, 1 - par)
            batches(sp, layer1)
            for t in range(TT):
                sp.wait_ge(sem("final"), t + 1)
                sp.dma_start(out.rearrange("b s e -> (b s) e")[128 * t:128 * (t + 1), :], x_tok[:, t, :])\
                    .then_inc(sem("stored"), 16)
            sp.wait_ge(sem("stored"), 16 * TT)

        def pool_rstd(pool, number, tiles_before, tiles):
            a, z = tiles
            pool.wait_ge(sem("ln_var"), tiles_before + z - a)
            pool.tensor_scalar(rstd[:, a:z], mean_var[:, a:z, 1], EPS, None, ALU.add).then_inc(sem("ln_eps"), 1)
            pool.wait_ge(sem("ln_eps"), number + 1)
            pool.tensor_tensor(rstd[:, a:z], rstd[:, a:z], half_neg[:, a:z], ALU.pow).then_inc(sem("ln_rstd"), 1)

        def pool_context1(pool, b, par):
            pool.wait_ge(sem("high1"), b + 1)
            pool.tensor_tensor(c_split1[0:KP, :, 1, :], c_in[par][:], c_split1[0:KP, :, 0, :], ALU.subtract)\
                .then_inc(sem("split_done1"), 1)

        @block.gpsimd
        def _(pool):
            for m in (bq1_pad, ident, ident16, ident_b, expert_row):
                pool.memset(m[:], 0.0).then_inc(sem("const_0"), 1)
            for m in (ones_f, head_of, place):
                pool.memset(m[:], 1.0).then_inc(sem("const_0"), 1)
            pool.memset(half_neg[:], -0.5).then_inc(sem("const_0"), 1)
            pool.wait_ge(sem("const_0"), 9)
            for m in (ident, ident16, ident_b):
                pool.affine_select(out=m[:], in_=m[:], compare_op=ALU.not_equal, fill=1.0, base=0,
                                   pattern=[[-1, 128]], channel_multiplier=1).then_inc(sem("const"), 1)
            pool.affine_select(out=head_of[:], in_=head_of[:], compare_op=ALU.is_ge, fill=0.0, base=0,
                               pattern=[[-D0, H]], channel_multiplier=1).then_inc(sem("const"), 1)
            pool.affine_select(out=place[:], in_=place[:], compare_op=ALU.is_ge, fill=0.0, base=0,
                               pattern=[[-D0, HG], [1, 32]], channel_multiplier=0).then_inc(sem("const"), 1)
            pool.wait_ge(sem("const"), 5)
            pool.affine_select(out=head_of[:], in_=head_of[:], compare_op=ALU.is_ge, fill=0.0, base=D0 - 1,
                               pattern=[[D0, H]], channel_multiplier=-1).then_inc(sem("const"), 1)
            pool.affine_select(out=place[:], in_=place[:], compare_op=ALU.is_ge, fill=0.0, base=D0 - 1,
                               pattern=[[D0, HG], [-1, 32]], channel_multiplier=0).then_inc(sem("const"), 1)
            pool.affine_select(out=expert_row[:], in_=expert_row[:], compare_op=ALU.not_equal, fill=1.0, base=0,
                               pattern=[[-1, NE], [0, 128]], channel_multiplier=1).then_inc(sem("const"), 1)
            pool_rstd(pool, 0, 0, (0, TT))
            pool.memset(c_split0[:], 0.0).then_inc(sem("pad0"), 1)
            for e in range(NE):
                pool.memset(expert_id[:, e:e + 1], float(e - NE)).then_inc(sem("const"), 1)
            pool.wait_ge(sem("pad0"), 1)

            def split0(b, par):
                wait_apart(pool, "pool", (sem(f"ctx_in0_{par}"), per_use(b, par, 16)), (sem("ct_turned0"), 2 * b),
                           (sem("kept0"), 16 * b))
                source = c_in[par][:].rearrange("p c (g d) -> p c g d", g=G)
                high, low = c_split0[0:KP, :, :, 0, :], c_split0[0:KP, :, :, 1, :]
                pool.tensor_copy(high, source).then_inc(sem("high0"), 1)
                pool.wait_ge(sem("high0"), b + 1)
                pool.tensor_tensor(low, source, high, ALU.subtract).then_inc(sem("low0"), 1)

            def mask0(b, par):
                wait_apart(pool, "pool", (sem("mask_in"), (b + 1) * 32), (sem("max_done0"), (b - 1) * T0))
                pool.tensor_scalar(mask_bias[par][:], mask_in[:].rearrange("q (p c) -> q c p", c=KC),
                                   0.0, NEG, ALU.is_equal, ALU.mult).then_inc(sem("mask_done"), 1)

            split0(0, 0)
            mask0(0, 0)

            def layer0(b, par, first, last):
                if not last:
                    split0(b + 1, 1 - par)
                    mask0(b + 1, 1 - par)
                if isinstance(b, int) and b < 2:
                    pool.wait_ge(sem("in_ffn0"), 16 * 5)
                    w = (g_w, u_w)[b]
                    pool.tensor_scalar(w[:], w[:], W_SCALE, None, ALU.mult).then_inc(sem("gu_scaled"), 1)
            batches(pool, layer0)

            def low_weights(third):
                part = slice(3 * third, 3 * third + 3)
                for n, (w, split) in enumerate(((g_w, g_split), (u_w, u_split))):
                    pool.wait_ge(sem("gu_high"), 2 * third + n + 1)
                    pool.tensor_tensor(split[:, part, 1, :], w[:, part, :], split[:, part, 0, :], ALU.subtract)\
                        .then_inc(sem("gu_low"), 1)
            low_weights(0)
            low_weights(1)
            pool_rstd(pool, 1, TT, (0, TT))
            pool_context1(pool, 0, 0)
            low_weights(2)

            def expert_tokens(r):
                a, z = FFN_HALVES[r // NE]
                pool.wait_ge(sem("hot_mask"), r + 1)
                if r >= 2:
                    n = (r - 2) + (r - 2) // NE
                    pool.wait_ge(sem("up0"), 2 * IC * (n + 1))
                pool.tensor_tensor(x_exp[r % 2][:, :, 0:z - a], xs_split[:, :, a:z],
                                   hot_mask[r % 2][:, 0:z - a].unsqueeze(1).broadcast_to((128, 2, z - a)), ALU.mult)\
                    .then_inc(sem("x_exp"), 1)
            pool.wait_ge(sem("xs_t"), 4)
            for r in range(2 * NE):
                if r == NE + 6:
                    pool_rstd(pool, 2, 2 * TT, (0, 4))
                expert_tokens(r)
            pool_rstd(pool, 3, 2 * TT + 4, (4, TT))

            batches(pool, lambda b, par, first, last: None if last else pool_context1(pool, b + 1, 1 - par))
            pool_rstd(pool, 4, 3 * TT, (0, EARLY))
            pool_rstd(pool, 5, 3 * TT + EARLY, (EARLY, TT))

        def pe_norm_t(pe, layer):
            pe.wait_ge(sem("ln_norm"), TT * (layer + 1))
            wait(pe, sem("const"), 1)
            for t in range(TT):
                pe.transpose(bank[:, t // 4, 128 * (t % 4):128 * (t % 4 + 1)], x_norm[:, t, :], ident[:])\
                    .then_inc(sem("ln_turned"), 1)

        def pe_block_turn(pe, ready, tiles, where, name="block_ready"):
            pe.wait_ge(sem(name), ready)
            for t in tiles:
                pe.transpose(where(t), block_t[:, 128 * t:128 * (t + 1)], ident[:]).then_inc(sem("block_turned"), 1)

        def pe_norm_half(pe, tiles):
            pe.wait_ge(sem("ln_norm"), TT * 2 + tiles[-1] + 1)
            for t in tiles:
                pe.transpose(in_bank_7(t), x_norm[:, t, :], ident[:]).then_inc(sem("ln_turned"), 1)

        def pe_scores0(pe, b, par, t):
            if t % 2 == 0:
                pe.wait_ge(sem(f"stack{par}_{t // 2}"), per_use(b, par, 32))
            wait(pe, sem("max_done0"), b * T0 + t)
            for k in range(3):
                last = pe.matmul(bank[0:R0, k, 0:4 * KP], q0[:, b, R0 * t:R0 * (t + 1)],
                                 c_stack[par][:, t // 2, 4 * k:4 * k + 4, 0:KP], start=True, stop=True)
            last.then_inc(sem("scores0"), 1)

        def pe_turn(pe, layer, b, par, t, parts=(0, 1)):
            rows, tiles = (R0, T0) if layer == 0 else (128, T1)
            if 0 in parts:
                pe.wait_ge(sem("exp_done0" if layer == 0 else "norm_done1"), b * tiles + t + 1)
            for u in parts:
                wait_pair(pe, layer, b, par, ("turn", t, u))
                n = unit_no(layer, par, ("turn", t, u))
                for c in range(UC):
                    k = UC * u + c
                    last = pe.transpose(pair(n)[0:KP, c // 4, 128 * (c % 4):128 * (c % 4) + rows],
                                        e_row[(t + par * (tiles % 2)) % 2][0:rows, KP * k:KP * (k + 1)],
                                        ident[0:rows, 0:rows])
                last.then_inc(sem(f"turned{layer}"), 1)

        def pe_prep(pe, layer, b, par, halves):
            for n in halves:
                if isinstance(b, int) and b == 0:
                    if n == 0:
                        wait(pe, sem("const"), 3)
                else:
                    wait_pair(pe, layer, b - 1, 1 - par, ("prep", n, 0))
                if layer == 0:
                    pe.wait_ge(sem("low0"), b + 1)
                else:
                    pe.wait_ge(sem("split_done1" if n else "high1"), b + 1)
                no = unit_no(layer, 1 - par, ("prep", n, 0)) if not (isinstance(b, int) and b == 0) else \
                    n
                for c in range(KC):
                    src = c_split0[:, c, 2 * n:2 * n + 2].rearrange("p g two d -> p (g two d)") if layer == 0 \
                        else c_split1[:, c, n, :]
                    last = pe.transpose(pair_flat(no, F16)[:, 128 * c:128 * (c + 1)], src, ident16[:])
                last.then_inc(sem(f"ct_turned{layer}"), 1)

        def pe_pv0(pe, b, par, g, part):
            if part == 0:
                pe.wait_ge(sem("low_done0"), b * (2 * T0) + 4 * (g + 1))
                wait(pe, sem("u_done0"), b * G + g)
                pe.wait_ge(sem("kept0"), (b + 1) * 16)
            for c in range(UC * part, UC * part + UC):
                for lo, p in ((0, p_high0), (64, p_low0)):
                    last = pe.matmul(bank[lo:lo + 64, U_BANK, 0:GC], c_group[par][:, c, g, :],
                                     p[g % 2][:, c, :], start=(c == 0), stop=(c == KC - 1))
            if part == 1:
                last.then_inc(sem("pv_done0"), 1)
                pe.wait_ge(sem("inv_done0"), b * G + g + 1)
                for n in range(2):
                    t = 2 * g + n
                    last = pe.matmul(bank[:, U_BANK, 256 + R0 * n:256 + R0 * (n + 1)],
                                     row_inv[0:R0, t:t + 1].broadcast_to((R0, 128)),
                                     ident[0:R0, 0:R0], start=True, stop=True)
                last.then_inc(sem("inv_spread"), 1)

        def projected(layer):
            return bank[:, U_BANK, 0:2 * S] if layer == 1 else pair(unit_no(0, 0, PROJ))[:, 0, 0:2 * S]

        def pe_proj(pe, layer, b):
            pe.wait_ge(sem("u_done0"), b * G) if layer == 0 else pe.wait_ge(sem("u_done1"), b * 2)
            if layer == 0:
                wait_pair(pe, 0, b, 0, PROJ)
            for h in range(H):
                rhs = u0[:, :, h // HG, S * (h % HG):S * (h % HG + 1)] if layer == 0 else u1[:, :, S * h:S * (h + 1)]
                last = pe.matmul(projected(layer).rearrange("p (b s) -> p b s", b=2),
                                 (out0_w if layer == 0 else out1_w)[:, h, :], rhs, start=(h == 0), stop=(h == H - 1))
            last.then_inc(sem(f"projected{layer}"), 2)

        def pe_scores1(pe, b, par, t):
            if t == 0:
                for n in range(2):
                    pe.wait_ge(sem(f"ct_done1_{n}"), b + 1)
            wait(pe, sem("exp_done1"), b * T1 + t)
            for k in range(3):
                for ql, cl in ((0, 0), (0, 1), (1, 0)):
                    last = pe.matmul(bank[:, k, 0:4 * KP], q1[:, ql, b, 128 * t:128 * (t + 1)],
                                     c_t1[par][:, cl, 4 * k:4 * k + 4, 0:KP],
                                     start=(ql == 0 and cl == 0), stop=(ql == 1))
                last.then_inc(sem("scores1"), 1)

        def pe_pv1(pe, b, par, grp, first, end):
            a, z = GROUPS1[grp]
            cols = 128 * (z - a)
            if first == 0:
                pe.wait_ge(sem("low_done1"), b * (2 * T1) + 2 * z)
                wait(pe, sem("u_done1"), b * 2 + grp)
                if grp == 0 and par == 0:
                    wait(pe, sem("block_done1"), b)
            if first == 0 and grp == 0:
                pe.wait_ge(sem("kept1"), (b + 1) * 16)
            for c in range(first, end):
                for cl, p in ((0, p_high1), (0, p_low1), (1, p_high1)):
                    last = pe.matmul(bank[:, U_BANK, 0:cols], c_keep1[par][:, c, cl, :], p[grp][:, c, :],
                                     start=(c == 0 and cl == 0 and p is p_high1),
                                     stop=(c == KC - 1 and cl == 1))
            if end == KC:
                last.then_inc(sem("pv_done1"), 1)

        @block.tensor
        def _(pe):
            pe_norm_t(pe, 0)
            pe.wait_ge(sem("diag"), 3)
            pe.matmul(bank[:, 2, 0:E], block_diag[:, 0, :], block_diag[:, 1, :], start=True, stop=True)\
                .then_inc(sem("w0_a"), 1)
            pe.wait_ge(sem("in_w0"), 32)
            pe.transpose(bank[:, 3, 0:E], wo0_sb[:], ident[:]).then_inc(sem("w0_wo"), 1)
            pe.wait_ge(sem("ln_t"), 2)
            pe.wait_ge(sem("w0_place"), G)
            for n in range(2 * H):
                h, half = n // 2, n % 2
                if n >= 3:
                    pe.wait_ge(sem("q0_low"), n - 2)
                pe.matmul(bank[0:96, n % 3, 0:HALF], a_heads[:, h].rearrange("p a b -> p (a b)"),
                          x_norm_t[:, HALF * half:HALF * (half + 1)], start=True, stop=True)\
                    .then_inc(sem("q0_made"), 1)
                if n == 8:
                    pe.wait_ge(sem("w0_place"), 2 * G)
                    pe.wait_ge(sem("w0_sb"), 1)
                    for h in range(H):
                        last = pe.matmul(bank[:, 4 + h // 4, 128 * (h % 4):128 * (h % 4 + 1)],
                                         v_heads[:, h].rearrange("p a b -> p (a b)"), wo0_t[:], start=True, stop=True)
                    last.then_inc(sem("w0_out"), 1)
                if n == 20:
                    pe.wait_ge(sem("w0_out_sb"), 2)
                    pe_prep(pe, 0, 0, 0, (0, 1))
            pe.wait_ge(sem("q0_low"), 2 * H)
            pe_scores0(pe, 0, 0, 0)

            def layer0(b, par, first, last):
                for t in range(T0):
                    if t < T0 - 1:
                        pe_scores0(pe, b, par, t + 1)
                    elif not last:
                        pe_scores0(pe, b + 1, 1 - par, 0)
                    if t == PROJ_AT and par == 0 and not first:
                        pe_proj(pe, 0, b)
                    if t in PREP_AT[0] and not last:
                        pe_prep(pe, 0, b + 1, 1 - par, (PREP_AT[0].index(t),))
                    if t >= 3:
                        pe_pv0(pe, b, par, (t - 3) // 2, (t - 3) % 2)
                    elif not first:
                        pe_pv0(pe, b - 1, 1 - par, (t + T0 - 3) // 2, (t + T0 - 3) % 2)
                    if t > 0:
                        pe_turn(pe, 0, b, par, t - 1, (1,))
                    elif not first:
                        pe_turn(pe, 0, b - 1, 1 - par, T0 - 1, (1,))
                    pe_turn(pe, 0, b, par, t, (0,))
            batches(pe, layer0)
            pe_turn(pe, 0, B - 1, 1, T0 - 1, (1,))
            for k in range(T0 - 3, T0):
                pe_pv0(pe, B - 1, 1, k // 2, k % 2)
            pe_proj(pe, 0, B)

            pe_block_turn(pe, 1, range(TT), in_banks_56)
            pe.wait_ge(sem("in_w1"), 16 * 9)
            pe.wait_ge(sem("in_bv"), 16 * 2)
            for n in range(8):
                last = pe.transpose(bank[:, 3 + n // 4, 128 * (n % 4):128 * (n % 4 + 1)], wo1_sb[:, n, :], ident[:])
            last.then_inc(sem("w1_turned"), 1)

            def heads4(two, k, n, lhs, rhs, name):
                rows = slice(64 * two, 64 * two + 64)
                for j in range(4):
                    last = pe.matmul(bank[:, n, 128 * j:128 * (j + 1)], lhs[rows, 4 * k + j, :], rhs[rows, 4 * k + j, :],
                                     start=True, stop=True)
                last.then_inc(sem(name), 1)

            for k, two, n in ((0, 0, 7), (0, 1, 2), (1, 0, 0), (1, 1, 1)):
                heads4(two, k, n, wq1_sb, wk1_sb, "a1_made")
            pe.wait_ge(sem("w1_t"), 2)
            heads4(0, 0, 3, wv1_sb, wo1_t, "w1_out")
            heads4(1, 0, 4, wv1_sb, wo1_t, "w1_out")
            pe.wait_ge(sem("residual"), TT)
            heads4(0, 1, 5, wv1_sb, wo1_t, "w1_out")
            heads4(1, 1, 6, wv1_sb, wo1_t, "w1_out")
            pe.wait_ge(sem("a1_sb"), 4)
            pe_norm_t(pe, 1)
            pe.wait_ge(sem("in_ffn0"), 16 * 5)
            pe.wait_ge(sem("ln_t"), 4)
            for t in range(TT):
                last = pe.matmul(bank[:, 2, NE * t:NE * (t + 1)], x_norm_t[:, 128 * t:128 * (t + 1)],
                                 gate_w_sb[:], start=True, stop=True)
            last.then_inc(sem("logits"), 1)
            pe.wait_ge(sem("w1_out_sb"), 4)
            pe_prep(pe, 1, 0, 0, (0, 1))
            pe.wait_ge(sem("one_hot"), 1)
            for t in range(TT):
                last = pe.transpose(bank[0:NE, t // 4, 128 * (t % 4):128 * (t % 4 + 1)], one_hot[:, t, :], ident[:])
            last.then_inc(sem("hot_turned"), 1)
            pe.wait_ge(sem("x_scored"), 1)
            pe.wait_ge(sem("ct_done1_1"), 1)
            for t in range(TT):
                last = pe.transpose(in_banks_56(t), x_norm[:, t, :], ident[:])
            last.then_inc(sem("xs_turned"), 1)

            def hot_rows(n):
                half, e = n // (NE + 1), n % (NE + 1)
                if e < NE:
                    a, z = FFN_HALVES[half]
                    r = half * NE + e
                    wait(pe, sem("hot_mask"), r)
                    pe.matmul(bank[:, 0, 0:z - a], expert_row[:, e, :], one_hot_t[:, a:z],
                              start=True, stop=True).then_inc(sem("hot_rows"), 1)

            def down(m):
                n, ic = m // IC, m % IC
                half, e = n // (NE + 1), n % (NE + 1)
                a, z = FFN_HALVES[half]
                pe.wait_ge(sem("act_low"), m + 1)
                if m == 0:
                    pe.wait_ge(sem("d_low"), 3)
                for wl, al in ((0, 0), (0, 1), (1, 0)):
                    last = pe.matmul(bank[:, 5 + half, 0:z - a], d_split[:, e, wl, ic, :], act_split[m % 3][:, al, 0:z - a],
                                     start=(e == 0 and ic == 0 and wl + al == 0), stop=(e == NE and ic == IC - 1 and wl == 1))
                last.then_inc(sem("down0"), 1)

            pe.wait_ge(sem("hot_t"), 1)
            def turn_ternary(pe, n):
                pe.wait_ge(sem("w_tern"), n + 1)
                for j in range(JC):
                    last = pe.transpose(tern_turned(n)[:, 128 * j:128 * (j + 1)], w_tern[:, n, j, :], ident_b[:])
                last.then_inc(sem("w_turned"), 1)

            hot_rows(0)
            for k in range(8):
                last = pe.matmul(bank[:, 7, 2 * k:2 * k + 2], wk1_sb[:, k, :], bq1_pad[:, k, :], start=True, stop=True)
            for k in range(8):
                last = pe.matmul(bank[:, 7, H:H + 1], wo1_t[:, k, :], bv1_col[:, k:k + 1], start=(k == 0), stop=(k == 7))
            last.then_inc(sem("w1_bias"), 1)
            pe.wait_ge(sem("ct_done1_0"), 1)
            pe.wait_ge(sem("xs_t"), 4)
            for m in range(UNITS0):
                n, ic = m // IC, m % IC
                half, e = n // (NE + 1), n % (NE + 1)
                a, z = FFN_HALVES[half]
                if ic == 0:
                    if n + 1 < 2 * (NE + 1):
                        hot_rows(n + 1)
                    if e < NE:
                        pe.wait_ge(sem("x_exp"), half * NE + e + 1)
                    if half == 0 and e % 3 == 0:
                        pe.wait_ge(sem("gu_low"), 2 * (e // 3) + 2)
                    if n == NE:
                        pe.wait_ge(sem("xn_t"), 3)
                wait(pe, sem("act0"), m - 1)
                for w, at in ((g_split, 0), (u_split, 1)):
                    for wl, xl in ((0, 0), (0, 1), (1, 0)):
                        moving = x_exp[(half * NE + e) % 2][:, xl, 0:z - a] if e < NE else xn_split[:, xl, a:z]
                        last = pe.matmul(bank[:, 1 + 2 * (m % 2) + at, 0:z - a], w[:, e, wl, 128 * ic:128 * (ic + 1)], moving,
                                         start=(wl + xl == 0), stop=(wl == 1))
                    last.then_inc(sem("up0"), 1)
                if m >= 2:
                    down(m - 2)
                if m == 5:
                    pe.wait_ge(sem("bias1"), 2)
                    pe.wait_ge(sem("w_abs"), 3)
                    pe.matmul(bank[:, 7, 0:3], ones_f[:], abs_sum[:], start=True, stop=True).then_inc(sem("w_abs_all"), 1)
                if m == 18:
                    turn_ternary(pe, 0)
                    turn_ternary(pe, 1)
                if m == 20:
                    pe.wait_ge(sem("w_t"), 2)
                    turn_ternary(pe, 2)
                if m == UNITS0 // 2 + 5:
                    pe.wait_ge(sem("w_t"), 3)
                    pe_block_turn(pe, 2, range(4), in_bank_7)
                if m == UNITS0 // 2 + 15:
                    pe_norm_half(pe, range(4))
            down(UNITS0 - 2)
            down(UNITS0 - 1)

            for n in range(2 * H):
                h, half = n % H, n // H
                if n == 0:
                    pe.wait_ge(sem("ln_t"), 5)
                    pe.wait_ge(sem("act0"), UNITS0)
                if n == 4:
                    pe_block_turn(pe, 3, range(4, TT), in_bank_7)
                if n == H:
                    pe_norm_half(pe, range(4, TT))
                    pe.wait_ge(sem("ln_t"), 6)
                if n >= 4:
                    pe.wait_ge(sem("q1_low"), n - 3)
                pe.matmul(bank[:, n % 4, 0:HALF], a1_w[:, h, :], x_norm_t[:, HALF * half:HALF * (half + 1)],
                          start=True, stop=True).then_inc(sem("q1_made"), 1)
            pe.wait_ge(sem("q1_low"), 2 * H)
            pe_scores1(pe, 0, 0, 0)

            def layer1(b, par, first, last):
                for t in range(T1):
                    if t < T1 - 1:
                        pe_scores1(pe, b, par, t + 1)
                    elif not last:
                        pe_scores1(pe, b + 1, 1 - par, 0)
                    pe_turn(pe, 1, b, par, t, (0,))
                    if t == 0:
                        pe_turn(pe, 1, b, par, t, (1,))
                    if t < 3 and not first:
                        pe_pv1(pe, b - 1, 1 - par, 1, 4 * t, 4 * t + 4)
                    if t >= 4:
                        pe_pv1(pe, b, par, 0, 4 * (t - 4), 4 * (t - 3))
                    if t > 0:
                        pe_turn(pe, 1, b, par, t, (1,))
                    if t == PROJ_AT and par == 0 and not first:
                        pe_proj(pe, 1, b)
                    if t in PREP_AT[1] and not last:
                        pe_prep(pe, 1, b + 1, 1 - par, (PREP_AT[1].index(t),))
                    if t == PREP_AT[1][0] and last:
                        wait_pair(pe, 1, b, par, PREP_0)
                        pe_block_turn(pe, B - 2, range(EARLY), early_turned, "block_done1")
            batches(pe, layer1)
            pe_pv1(pe, B - 1, 1, 1, 0, 7)

            def up1(t):
                wait(pe, sem("act1"), t - 1)
                for n in range(2):
                    pe.matmul(bank[:, 2 * (t % 2) + n, :], xq_t[:, t, :],
                              w_tern_t[:, n].rearrange("p a b -> p (a b)"), start=True, stop=True)\
                        .then_inc(sem("up1"), 1)

            def down1(t):
                pe.wait_ge(sem("hq"), t + 1)
                into = bank[:, 4 + t % 2, :].bitcast(BF16)
                for j in range(JC):
                    last = pe.transpose(into[:, 128 * j:128 * (j + 1)], hq[:, t % 2, 128 * j:128 * (j + 1)], ident_b[:])
                if t == LATE_AT:
                    pe.wait_ge(sem("xq"), 2)
                    last = pe.transpose(into[:, 512:640], xq[:, TT - 1, :], ident_b[:])
                last.then_inc(sem("hq_turned"), 1)
                pe.wait_ge(sem("hq_t"), t + 1)
                wait(pe, sem("final"), t - 1)
                if t == 1:
                    pe.wait_ge(sem("residual"), 3 * TT)
                for j in range(JC):
                    last = pe.matmul(bank[:, 6 + t % 2, 0:128], hq_t[:, t % 2, j, :], w_tern_t[:, 2, j, :],
                                     start=(j == 0), stop=(j == JC - 1))
                last.then_inc(sem("down1"), 1)

            pe.wait_ge(sem("xq"), 1)
            for t in range(EARLY):
                last = pe.transpose(bank[:, 4, :].bitcast(BF16)[:, 128 * t:128 * (t + 1)], xq[:, t, :], ident_b[:])
            last.then_inc(sem("xq_turned"), 1)
            pe_pv1(pe, B - 1, 1, 1, 7, KC)
            pe.wait_ge(sem("xq_t"), 1)
            up1(0)
            for t in range(TT):
                if t + 1 < TT:
                    if t + 1 == EARLY:
                        pe.wait_ge(sem("xq_t"), 2)
                    up1(t + 1)
                if t == 0:
                    pe_proj(pe, 1, B)
                if t == 1:
                    pe_block_turn(pe, 4, range(EARLY, TT), late_turned)
                down1(t)

        def act_norm_t(act, layer):
            for n in range(2):
                act.wait_ge(sem("ln_turned"), TT * layer + (4 if n == 0 else TT))
                cols = 512 if n == 0 else NTOK - 512
                act.copy(x_norm_t[:, 512 * n:512 * n + cols], bank[:, n, 0:cols]).then_inc(sem("ln_t"), 1)

        def act_exp0(act, b, par, t):
            act.wait_ge(sem("max_done0"), b * T0 + t + 1)
            wait(act, sem("turned0"), (b * T0 + t - 1) * 2)
            act.activation(e_row[t % 2][0:R0, :], masked[t % 2][:], ACT.Exp, bias=neg_max[0:R0, t:t + 1],
                           scale=-1.0, accum_out=row_sum[0:R0, t:t + 1]).then_inc(sem("exp_done0"), 1)

        def act_high0(act, b, par, t, u):
            g = t // 2
            act.wait_ge(sem("turned0"), (b * T0 + t) * 2 + u + 1)
            if t % 2 == 0 and u == 0:
                wait(act, sem("pv_done0"), b * G + g - 1)
            act.activation(p_high0[g % 2][:, UC * u:UC * (u + 1), R0 * (t % 2):R0 * (t % 2 + 1)],
                           pair_chunks(unit_no(0, par, ("turn", t, u)), R0), ACT.Copy, scale=PSCALE)\
                .then_inc(sem("high_done0"), 1)

        def act_inv0(act, b, par, g):
            act.wait_ge(sem("inv_spread"), b * G + g + 1)
            wait(act, sem("u_done0"), b * G + g)
            act.copy(inv_b[:], bank[:, U_BANK, 256:256 + GC]).then_inc(sem("inv_sb"), 1)

        def act_block(act, layer, b):
            act.wait_ge(sem(f"projected{layer}"), b)
            act.activation(block_t[:, bass.ds((b - 2) * S, 2 * S)], projected(layer),
                           ACT.Identity, bias=(bo0_col if layer == 0 else bias1)[:]).then_inc(sem(f"block_done{layer}"), 2)

        def act_exp1(act, b, par, t):
            act.wait_ge(sem("max_done1"), b * T1 + t + 1)
            wait(act, sem("turned1"), (b * T1 + t - 1) * 2)
            act.activation(e_row[(t + par) % 2][:], bank[:, 0:3, 0:4 * KP], ACT.Exp, bias=neg_max[:, t:t + 1],
                           accum_out=row_sum[:, t:t + 1]).then_inc(sem("exp_done1"), 1)

        def act_high1(act, b, par, t, u):
            grp = 0 if t < 4 else 1
            at = t - GROUPS1[grp][0]
            act.wait_ge(sem("turned1"), (b * T1 + t) * 2 + u + 1)
            if at == 0 and u == 0:
                wait(act, sem("pv_done1"), (b - 1) * 2 + grp + 1)
            act.copy(p_high1[grp][:, UC * u:UC * (u + 1), 128 * at:128 * (at + 1)],
                     pair_chunks(unit_no(1, par, ("turn", t, u)), 128)).then_inc(sem("high_done1"), 1)

        def act_u1(act, b, par, grp):
            a, z = GROUPS1[grp]
            act.wait_ge(sem("pv_done1"), b * 2 + grp + 1)
            if grp == 0 and par == 0:
                wait(act, sem("projected1"), b)
            act.activation(u1[:, par, 128 * a:128 * z], bank[:, U_BANK, 0:128 * (z - a)], ACT.Copy, scale=1.0 / PSCALE)\
                .then_inc(sem("u_done1"), 1)

        def act_split1(act, b, par):
            act.wait_ge(sem(f"ctx_in1_{par}"), per_use(b, par, 16))
            wait(act, sem("ct_turned1"), 2 * b)
            wait(act, sem("kept1"), 16 * b)
            act.copy(c_split1[0:KP, :, 0, :], c_in[par][:]).then_inc(sem("high1"), 1)

        def act_context(act, layer, b, par, n):
            act.wait_ge(sem(f"ct_turned{layer}"), 2 * b + n + 1)
            if layer == 0:
                for g in (2 * n, 2 * n + 1):
                    act.wait_ge(sem(f"stack{1 - par}_{g}"), per_use(b - 1, 1 - par, 32))
            else:
                wait(act, sem("scores1"), (b - 1) * (3 * T1))
            act.copy((c_t0 if layer == 0 else c_t1[par])[:, n].rearrange("p c k -> p (c k)"),
                     pair_flat(unit_no(layer, 1 - par, ("prep", n, 0)), F16)[:, 0:KC * 128])\
                .then_inc(sem(f"ct_done{layer}_{n}"), 1)

        @block.scalar
        def _(act):
            def load_table(function):
                act.activation(warm[:], ones_f[:, 0:1], function).then_inc(sem("warm"), 1)

            load(act, "in_gates", [(gates[:, 0:2], g_xattn.rearrange("(o n) -> o n", o=1).broadcast_to((128, 2))),
                                   (gates[:, 2:4], g_ffn.rearrange("(o n) -> o n", o=1).broadcast_to((128, 2)))])
            load(act, "in_ffn0", [
                (gate_w_sb[:], gate_w),
                (g_w[:, 0:NE, :], rt_gate.rearrange("e h i -> h e i")), (g_w[:, NE, :], sh_gate),
                (u_w[:, 0:NE, :], rt_up.rearrange("e h i -> h e i")), (u_w[:, NE, :], sh_up)])
            bkv = bkv1.rearrange("(k two part d) -> two part d k", two=2, part=2, d=D1)
            act.wait_ge(sem("const_0"), 1)
            bq = bq1.rearrange("(k two p) -> two p k", two=2, p=D1)
            load(act, "in_w1", [(bq1_pad[0:64, :, 0], bq[0]), (bq1_pad[64:128, :, 1], bq[1]),
                                (bo1_col[:], bo1.rearrange("(e o) -> e o", o=1))])
            for two in range(2):
                load(act, "in_bv", [(bv1_col[64 * two:64 * two + 64], bkv[two, 1])])
            load(act, "in_wf", [(wg_sb[:, 0], w_gate.rearrange("(j p) h -> p j h", p=128)),
                                (wg_sb[:, 1], w_up.rearrange("(j p) h -> p j h", p=128)),
                                (wg_sb[:, 2], w_down.rearrange("h (j p) -> h j p", p=128))])
            act.wait_ge(sem("in_gates"), 32)
            act.activation(tanh_g[:], gates[:], ACT.Tanh).then_inc(sem("tanh_g"), 1)
            act_norm_t(act, 0)
            act.wait_ge(sem("w0_wo"), 1)
            act.copy(wo0_t[:], bank[:, 3, 0:E]).then_inc(sem("w0_sb"), 1)
            for n in range(2 * H):
                h, half = n // 2, n % 2
                act.wait_ge(sem("q0_made"), n + 1)
                act.copy(q0[:, 8 * half:8 * half + 8, S * h:S * (h + 1)],
                         bank[0:96, n % 3, 0:HALF].rearrange("p (b s) -> p b s", s=S)).then_inc(sem("q0_high"), 1)
                if n in (10, 12):
                    act.wait_ge(sem("w0_out"), 1)
                    act.copy(out0_w[:].rearrange("p (a h) e -> p a (h e)", a=4)[:, n - 10:n - 8], bank[:, n - 6:n - 4, :])\
                        .then_inc(sem("w0_out_sb"), 1)
            load_table(ACT.Exp)

            def layer0(b, par, first, last):
                for t in range(T0):
                    if t in PREP_AT[0] and not last:
                        act_context(act, 0, b + 1, 1 - par, PREP_AT[0].index(t))
                    if t % 2 == 0 and t >= 4:
                        act_inv0(act, b, par, t // 2 - 2)
                    elif t % 2 == 0 and not first:
                        act_inv0(act, b - 1, 1 - par, t // 2 + 2)
                    if t == PROJ_AT and par == 0 and not first:
                        act_block(act, 0, b)
                    if t > 0:
                        act_high0(act, b, par, t - 1, 1)
                    elif not first:
                        act_high0(act, b - 1, 1 - par, T0 - 1, 1)
                    act_high0(act, b, par, t, 0)
                    if t < T0 - 1:
                        act_exp0(act, b, par, t + 1)
                    elif not last:
                        act_exp0(act, b + 1, 1 - par, 0)
            act_exp0(act, 0, 0, 0)
            batches(act, layer0)
            act_high0(act, B - 1, 1, T0 - 1, 1)
            act_inv0(act, B - 1, 1, 2)
            act_inv0(act, B - 1, 1, 3)
            def gu_high(third):
                part = slice(3 * third, 3 * third + 3)
                for w, split in ((g_w, g_split), (u_w, u_split)):
                    act.copy(split[:, part, 0, :], w[:, part, :]).then_inc(sem("gu_high"), 1)
            act.wait_ge(sem("gu_scaled"), 2)
            act.wait_ge(sem("scores0"), B * T0)
            gu_high(0)
            gu_high(1)
            act_block(act, 0, B)
            act.wait_ge(sem("block_done0"), B)
            act.sem_inc(sem("block_ready"), 1)

            gu_high(2)
            act.wait_ge(sem("w1_turned"), 1)
            for n in range(2):
                act.copy(wo1_t[:, 4 * n:4 * n + 4, :].rearrange("p a b -> p (a b)"), bank[:, 3 + n, :]).then_inc(sem("w1_t"), 1)

            def heads_out(dst, two, k, n, name, scale):
                act.activation(dst[:].rearrange("p (k two) e -> p two k e", two=2)[:, two, 4 * k:4 * k + 4, :],
                               bank[:, n, :].rearrange("p (k e) -> p k e", k=4), ACT.Copy, scale=scale).then_inc(sem(name), 1)
            for i, (k, two, n) in enumerate(((0, 0, 7), (0, 1, 2), (1, 0, 0), (1, 1, 1))):
                act.wait_ge(sem("a1_made"), i + 1)
                heads_out(a1_w, two, k, n, "a1_sb", SCALE1)
            act_split1(act, 0, 0)
            act_norm_t(act, 1)
            for i, (k, two, n) in enumerate(((0, 0, 3), (0, 1, 4), (1, 0, 5), (1, 1, 6))):
                act.wait_ge(sem("w1_out"), i + 1)
                heads_out(out1_w, two, k, n, "w1_out_sb", 1.0)
            act.wait_ge(sem("top"), 1)
            act.activation(score[:], top[:], ACT.Exp, scale=-1.0).then_inc(sem("score_exp"), 1)
            load_table(ACT.Silu)
            act.wait_ge(sem("in_down0"), 32)
            act.wait_ge(sem("block_ready"), 1)
            for third in range(3):
                part = slice(3 * third, 3 * third + 3)
                act.activation(d_split[:, part, 0].rearrange("p e c h -> p e (c h)"),
                               d_w[:, part].rearrange("p e c h -> p e (c h)"), ACT.Copy, scale=W_SCALE)\
                    .then_inc(sem("d_high"), 1)
            act.wait_ge(sem("hot_turned"), 1)
            for n in range(2):
                cols = 512 if n == 0 else NTOK - 512
                last = act.copy(one_hot_t[:, 512 * n:512 * n + cols], bank[0:NE, n, 0:cols])
            last.then_inc(sem("hot_t"), 1)
            act.wait_ge(sem("xs_turned"), 1)
            for a, z in FFN_HALVES:
                act.copy(xs_split[:, 0, a:z], bank[:, 5 if a == 0 else 6, 0:z - a]).then_inc(sem("xs_t"), 1)

            def hot_mask_out(n):
                half, e = n // (NE + 1), n % (NE + 1)
                if e < NE:
                    a, z = FFN_HALVES[half]
                    r = half * NE + e
                    act.wait_ge(sem("hot_rows"), r + 1)
                    wait(act, sem("x_exp"), r - 1)
                    act.copy(hot_mask[r % 2][:, 0:z - a], bank[:, 0, 0:z - a]).then_inc(sem("hot_mask"), 1)

            def act_high(m):
                a, z = FFN_HALVES[m // (UNITS0 // 2)]
                act.wait_ge(sem("act0"), m + 1)
                wait(act, sem("down0"), m - 2)
                act.copy(act_split[m % 3][:, 0, 0:z - a], act0[:, m % 2, 0:z - a]).then_inc(sem("act_high"), 1)

            def block_out(half):
                a, z = FFN_HALVES[half]
                act.wait_ge(sem("down0"), (half + 1) * (UNITS0 // 2))
                act.activation(block_t[:, a:z], bank[:, 5 + half, 0:z - a], ACT.Copy, scale=1.0 / W_SCALE)\
                    .then_inc(sem("block_out"), 1)
                act.wait_ge(sem("block_out"), half + 1)
                act.sem_inc(sem("block_ready"), 1)

            def norm_half_out(tiles):
                act.wait_ge(sem("ln_turned"), TT * 2 + tiles[-1] + 1)
                act.wait_ge(sem("xn_t"), 3)
                act.copy(x_norm_t[:, 128 * tiles[0]:128 * (tiles[-1] + 1)], bank[:, 7, 0:128 * len(tiles)])\
                    .then_inc(sem("ln_t"), 1)
            hot_mask_out(0)
            act.wait_ge(sem("w1_bias"), 1)
            act.activation(q_bias[:], bank[:, 7, 0:H], ACT.Copy, scale=SCALE1).then_inc(sem("bias1"), 1)
            act.activation(bias1[:], bank[:, 7, H:H + 1], ACT.Identity, bias=bo1_col[:]).then_inc(sem("bias1"), 1)
            act.copy(xn_split[:, 0, :], x_norm_t[:]).then_inc(sem("xn_t"), 1)
            for m in range(UNITS0):
                a, z = FFN_HALVES[m // (UNITS0 // 2)]
                act.wait_ge(sem("up0"), 2 * m + 1)
                wait(act, sem("act0"), m - 1)
                act.activation(silu0[:, m % 2, 0:z - a], bank[:, 1 + 2 * (m % 2), 0:z - a], ACT.Silu, scale=1.0 / W_SCALE)\
                    .then_inc(sem("silu0"), 1)
                if m % IC == 0 and m // IC + 1 < 2 * (NE + 1):
                    hot_mask_out(m // IC + 1)
                if m >= 1:
                    act_high(m - 1)
                if m == UNITS0 // 2 + 2:
                    block_out(0)
                if m in (19, 21):
                    for n in ((0, 1), (2,))[(m - 19) // 2]:
                        act.wait_ge(sem("w_turned"), n + 1)
                        act.copy(w_tern_t[:, n].rearrange("p a b -> p (a b)"), tern_turned(n)).then_inc(sem("w_t"), 1)
                if m == UNITS0 // 2 + 16:
                    norm_half_out(range(4))
            act_high(UNITS0 - 1)
            for n in range(2 * H):
                h, half = n % H, n // H
                if n == H:
                    norm_half_out(range(4, TT))
                act.wait_ge(sem("q1_made"), n + 1)
                act.activation(q1[:, 0, 8 * half:8 * half + 8, S * h:S * (h + 1)],
                               bank[:, n % 4, 0:HALF].rearrange("p (b s) -> p b s", s=S), ACT.Identity,
                               bias=q_bias[:, h:h + 1]).then_inc(sem("q1_high"), 1)
                if n == 1:
                    block_out(1)
            load_table(ACT.Exp)

            def layer1(b, par, first, last):
                for t in range(T1):
                    if t == 0 and not first:
                        act_u1(act, b - 1, 1 - par, 0)
                    if t == 3 and not first:
                        act_u1(act, b - 1, 1 - par, 1)
                    if t == 1 and not last:
                        act_split1(act, b + 1, 1 - par)
                    if t == PROJ_AT + 1 and par == 0 and not first:
                        act_block(act, 1, b)
                    act_high1(act, b, par, t, 0)
                    if t < T1 - 1:
                        act_exp1(act, b, par, t + 1)
                    elif not last:
                        act_exp1(act, b + 1, 1 - par, 0)
                    act_high1(act, b, par, t, 1)
                    if t in PREP_AT[1] and not last:
                        act_context(act, 1, b + 1, 1 - par, PREP_AT[1].index(t))
            act_exp1(act, 0, 0, 0)
            batches(act, layer1)
            act_u1(act, B - 1, 1, 0)
            load_table(ACT.Silu)

            act.wait_ge(sem("xq_turned"), 1)
            act.copy(xq_t[:, 0:EARLY].rearrange("p a b -> p (a b)"), bank[:, 4, 0:64 * EARLY].bitcast(BF16)).then_inc(sem("xq_t"), 1)
            act_u1(act, B - 1, 1, 1)

            def turned_h(t):
                act.wait_ge(sem("hq_turned"), t + 1)
                wait(act, sem("down1"), t - 1)
                if t == LATE_AT:
                    act.copy(xq_t[:, TT - 1, :], bank[:, 4 + t % 2, 256:320].bitcast(BF16)).then_inc(sem("xq_t"), 1)
                act.copy(hq_t[:, t % 2].rearrange("p a b -> p (a b)"), bank[:, 4 + t % 2, 0:256].bitcast(BF16))\
                    .then_inc(sem("hq_t"), 1)
            for t in range(TT):
                act.wait_ge(sem("up1"), 2 * t + 1)
                wait(act, sem("act1"), t - 1)
                act.activation(silu1[:, t % 2, :], bank[:, 2 * (t % 2), :], ACT.Silu, scale=x_deq[:, t, 0:1])\
                    .then_inc(sem("silu1"), 1)
                if t == 1:
                    act_block(act, 1, B)
                    act.wait_ge(sem("block_done1"), B)
                    act.sem_inc(sem("block_ready"), 1)
                if t >= 1:
                    turned_h(t - 1)
            turned_h(TT - 1)

        def dve_stats(dve, layer, tiles):
            for t in tiles:
                if layer == 0:
                    dve.wait_ge(sem("in_x"), 16)
                else:
                    dve.wait_ge(sem("residual"), TT * (layer - 1) + t + 1)
                dve.bn_stats(stats[:, t, :], x_tok[:, t, :]).then_inc(sem("ln_stats"), 1)
            for t in tiles:
                dve.wait_ge(sem("ln_stats"), TT * layer + t + 1)
                dve.bn_aggr(mean_var[:, t, :], stats[:, t, :]).then_inc(sem("ln_var"), 1)

        def dve_norm(dve, number, tiles):
            dve.wait_ge(sem("ln_rstd"), number + 1)
            for t in tiles:
                dve.tensor_scalar(x_norm[:, t, :], x_tok[:, t, :], mean_var[:, t, 0:1], rstd[:, t:t + 1],
                                  ALU.subtract, ALU.mult).then_inc(sem("ln_norm"), 1)

        def dve_residual(dve, turned, gate, tiles, where):
            dve.wait_ge(sem("block_turned"), turned)
            for t in tiles:
                dve.scalar_tensor_tensor(x_tok[:, t, :], where(t), tanh_g[:, gate:gate + 1], x_tok[:, t, :],
                                         ALU.mult, ALU.add).then_inc(sem("residual"), 1)

        def dve_max0(dve, b, par, t):
            if t == 0:
                dve.wait_ge(sem("mask_done"), b + 1)
            wait_apart(dve, "dve", (sem("scores0"), b * T0 + t + 1), (sem("exp_done0"), b * T0 + t - 1))
            dve.tensor_tensor_reduce(out=masked[t % 2][:].rearrange("p (a k) -> p a k", a=3),
                                     in0=bank[0:R0, 0:3, 0:4 * KP],
                                     in1=mask_bias[par][:].rearrange("p (a c) k -> p a (c k)", a=3),
                                     scale=-SCALE0, scalar=3.0e38, op0=ALU.add, op1=ALU.min,
                                     accum_out=neg_max[0:R0, t:t + 1]).then_inc(sem("max_done0"), 1)

        def dve_low0(dve, b, par, t, u):
            g = t // 2
            dve.wait_ge(sem("high_done0"), (b * T0 + t) * 2 + u + 1)
            part = (slice(None), slice(UC * u, UC * (u + 1)), slice(R0 * (t % 2), R0 * (t % 2 + 1)))
            dve.scalar_tensor_tensor(p_low0[g % 2][part], pair_chunks(unit_no(0, par, ("turn", t, u)), R0), PSCALE,
                                     p_high0[g % 2][part], ALU.mult, ALU.subtract).then_inc(sem("low_done0"), 1)

        def dve_inv0(dve, b, par, g):
            dve.wait_ge(sem("exp_done0"), b * T0 + 2 * g + 2)
            wait(dve, sem("inv_spread"), (b - 1) * G + g + 1)
            dve.tensor_scalar(row_sum[0:R0, 2 * g:2 * g + 2], row_sum[0:R0, 2 * g:2 * g + 2], PSCALE, None, ALU.mult)\
                .then_inc(sem("sum_scaled"), 1)
            dve.wait_ge(sem("sum_scaled"), b * G + g + 1)
            dve.reciprocal(row_inv[0:R0, 2 * g:2 * g + 2], row_sum[0:R0, 2 * g:2 * g + 2]).then_inc(sem("inv_done0"), 1)

        def dve_u0(dve, b, par, g):
            dve.wait_ge(sem("inv_sb"), b * G + g + 1)
            if g == 0 and par == 0:
                wait(dve, sem("projected0"), b)
            dve.tensor_tensor(u0[:, par, g, :], bank[:, U_BANK, 0:GC], inv_b[:], ALU.mult).then_inc(sem("u_done0"), 1)

        def dve_context(dve, layer, halves):
            for n in halves:
                dve.wait_ge(sem(f"ct_turned{layer}"), n + 1)
                dve.tensor_copy((c_t0 if layer == 0 else c_t1[0])[:, n].rearrange("p c k -> p (c k)"),
                                pair_flat(n, F16)[:, 0:KC * 128]).then_inc(sem(f"ct_done{layer}_{n}"), 1)

        def dve_max1(dve, b, par, t):
            for k in range(3):
                dve.wait_ge(sem("scores1"), (b * T1 + t) * 3 + k + 1)
                dve.tensor_reduce(bank_max[:, t, k:k + 1], bank[:, k, 0:4 * KP], AX.X, ALU.max, negate=True)\
                    .then_inc(sem("bank_max"), 1)
            dve.wait_ge(sem("bank_max"), (b * T1 + t) * 3 + 3)
            wait(dve, sem("exp_done1"), (b - 1) * T1 + t + 1)
            dve.tensor_reduce(neg_max[:, t:t + 1], bank_max[:, t, :], AX.X, ALU.min).then_inc(sem("max_done1"), 1)

        def dve_norm1(dve, b, par, t):
            dve.wait_ge(sem("exp_done1"), b * T1 + t + 1)
            dve.reciprocal(row_inv[:, t:t + 1], row_sum[:, t:t + 1]).then_inc(sem("inv_done1"), 1)
            dve.wait_ge(sem("inv_done1"), b * T1 + t + 1)
            e = e_row[(t + par) % 2][:]
            dve.tensor_scalar(e, e, row_inv[:, t:t + 1], PSCALE, ALU.mult, ALU.mult).then_inc(sem("norm_done1"), 1)

        def dve_low1(dve, b, par, t, u):
            grp = 0 if t < 4 else 1
            at = t - GROUPS1[grp][0]
            dve.wait_ge(sem("high_done1"), (b * T1 + t) * 2 + u + 1)
            part = (slice(None), slice(UC * u, UC * (u + 1)), slice(128 * at, 128 * (at + 1)))
            dve.tensor_tensor(p_low1[grp][part], pair_chunks(unit_no(1, par, ("turn", t, u)), 128),
                              p_high1[grp][part], ALU.subtract).then_inc(sem("low_done1"), 1)

        @block.vector
        def _(dve):
            dve_stats(dve, 0, range(TT))
            dve_norm(dve, 0, range(TT))
            dve.wait_ge(sem("in_w8"), 16 * 3)
            dve.wait_ge(sem("const"), 8)
            for n in range(3):
                dve.tensor_tensor(block_diag[:, n, :].rearrange("p (h d) -> p h d", d=D0),
                                  w8[:, n, :].unsqueeze(1).broadcast_to((128, H, D0)),
                                  head_of[:].unsqueeze(2).broadcast_to((128, H, D0)), ALU.mult).then_inc(sem("diag"), 1)
            dve.wait_ge(sem("diag"), 3)
            dve.wait_ge(sem("w0_a"), 1)
            for heads, parts, src in ((a_heads, 3, bank[:, 2, 0:E]), (v_heads, 4, block_diag[:, 2, :])):
                for g in range(G):
                    shape = (128, HG, parts, 32)
                    dve.tensor_tensor(heads[:, HG * g:HG * (g + 1)],
                                      src[:, 32 * g:32 * g + 32].unsqueeze(1).unsqueeze(1).broadcast_to(shape),
                                      place[:].unsqueeze(2).broadcast_to(shape), ALU.mult).then_inc(sem("w0_place"), 1)
            for n in range(2 * H):
                h, half = n // 2, n % 2
                dve.wait_ge(sem("q0_high"), n + 1)
                low = q0[64:96, 8 * half:8 * half + 8, S * h:S * (h + 1)]
                dve.tensor_tensor(low, bank[64:96, n % 3, 0:HALF].rearrange("p (b s) -> p b s", s=S), low,
                                  ALU.subtract).then_inc(sem("q0_low"), 1)
                if n == 20:
                    dve_context(dve, 0, (0, 1))
            dve_max0(dve, 0, 0, 0)

            def layer0(b, par, first, last):
                for t in range(T0):
                    if t < T0 - 1:
                        dve_max0(dve, b, par, t + 1)
                    elif not last:
                        dve_max0(dve, b + 1, 1 - par, 0)
                    if t % 2 == 0 and t >= 4:
                        dve_u0(dve, b, par, t // 2 - 2)
                    elif t % 2 == 0 and not first:
                        dve_u0(dve, b - 1, 1 - par, t // 2 + 2)
                    if t > 0:
                        dve_low0(dve, b, par, t - 1, 1)
                    elif not first:
                        dve_low0(dve, b - 1, 1 - par, T0 - 1, 1)
                    dve_low0(dve, b, par, t, 0)
                    if t % 2 == 1:
                        dve_inv0(dve, b, par, t // 2)
            batches(dve, layer0)
            dve_low0(dve, B - 1, 1, T0 - 1, 1)
            dve_u0(dve, B - 1, 1, 2)
            dve_u0(dve, B - 1, 1, 3)
            dve.wait_ge(sem("tanh_g"), 1)
            dve_residual(dve, TT, 0, range(TT), in_banks_56)

            dve_stats(dve, 1, range(TT))
            dve_norm(dve, 1, range(TT))
            dve.wait_ge(sem("logits"), 1)
            dve.tensor_copy(logits[:].rearrange("p t e -> p (t e)"), bank[:, 2, 0:TT * NE]).then_inc(sem("route"), 1)
            dve.wait_ge(sem("route"), 1)
            dve.tensor_reduce(top[:], logits[:], AX.X, ALU.max).then_inc(sem("top"), 1)
            dve.wait_ge(sem("top"), 1)
            top_b = top[:].unsqueeze(2).broadcast_to((128, TT, NE))
            id_b = expert_id[:].unsqueeze(1).broadcast_to((128, TT, NE))
            dve.tensor_tensor(is_top[:], logits[:], top_b, ALU.is_equal).then_inc(sem("route"), 1)
            dve.wait_ge(sem("route"), 2)
            dve.tensor_tensor(is_top[:], is_top[:], id_b, ALU.mult).then_inc(sem("route"), 1)
            dve.wait_ge(sem("route"), 3)
            dve.tensor_reduce(first_top[:], is_top[:], AX.X, ALU.min).then_inc(sem("route"), 1)
            dve.wait_ge(sem("route"), 4)
            dve.tensor_tensor(one_hot[:], id_b, first_top[:].unsqueeze(2).broadcast_to((128, TT, NE)),
                              ALU.is_equal).then_inc(sem("one_hot"), 1)
            dve.wait_ge(sem("score_exp"), 1)
            dve.tensor_scalar(score[:], score[:], 1.0, None, ALU.add).then_inc(sem("route"), 1)
            dve.wait_ge(sem("route"), 5)
            dve.reciprocal(score[:], score[:]).then_inc(sem("route"), 1)
            dve.wait_ge(sem("route"), 6)
            dve.wait_ge(sem("ln_turned"), 2 * TT)
            dve.tensor_tensor(x_norm[:], x_norm[:], score[:].unsqueeze(2).broadcast_to((128, TT, E)), ALU.mult)\
                .then_inc(sem("x_scored"), 1)

            dve_context(dve, 1, (1,))
            dve_context(dve, 1, (0,))
            dve.wait_ge(sem("xs_t"), 2)
            for a, z in FFN_HALVES:
                dve.tensor_tensor(xs_split[:, 1, a:z], bank[:, 5 if a == 0 else 6, 0:z - a], xs_split[:, 0, a:z], ALU.subtract)\
                    .then_inc(sem("xs_t"), 1)
            for third in range(3):
                part = slice(3 * third, 3 * third + 3)
                dve.wait_ge(sem("d_high"), third + 1)
                dve.scalar_tensor_tensor(d_split[:, part, 1].rearrange("p e c h -> p e (c h)"),
                                         d_w[:, part].rearrange("p e c h -> p e (c h)"), W_SCALE,
                                         d_split[:, part, 0].rearrange("p e c h -> p e (c h)"), ALU.mult, ALU.subtract)\
                    .then_inc(sem("d_low"), 1)
            dve.wait_ge(sem("xn_t"), 1)
            for a, z in FFN_HALVES:
                dve.tensor_tensor(xn_split[:, 1, a:z], x_norm_t[:, a:z], xn_split[:, 0, a:z], ALU.subtract)\
                    .then_inc(sem("xn_t"), 1)

            def act_low(m):
                a, z = FFN_HALVES[m // (UNITS0 // 2)]
                dve.wait_ge(sem("act_high"), m + 1)
                dve.tensor_tensor(act_split[m % 3][:, 1, 0:z - a], act0[:, m % 2, 0:z - a], act_split[m % 3][:, 0, 0:z - a],
                                  ALU.subtract).then_inc(sem("act_low"), 1)
            def ternary(step):
                if step == 0:
                    dve.wait_ge(sem("in_wf"), 48)
                    dve.wait_ge(sem("gu_low"), 6)
                if step < 3:
                    dve.tensor_reduce(abs_sum[:, step:step + 1], wg_sb[:, step].rearrange("p a b -> p (a b)"), AX.X, ALU.add,
                                      apply_absolute_value=True).then_inc(sem("w_abs"), 1)
                elif step == 3:
                    dve.wait_ge(sem("w_abs_all"), 1)
                    dve.tensor_scalar(w_mean[:], bank[:, 7, 0:3], 1.0 / (INNER1 * E), 1e-5, ALU.mult, ALU.max)\
                        .then_inc(sem("w_stat"), 1)
                    dve.wait_ge(sem("w_stat"), 1)
                    dve.reciprocal(w_scale[:], w_mean[:]).then_inc(sem("w_stat"), 1)
                    dve.tensor_tensor(down_scale[:], w_mean[:, 2:3], tanh_g[:, 3:4], ALU.mult).then_inc(sem("w_stat"), 1)
                    dve.wait_ge(sem("w_stat"), 3)
                else:
                    n = (step - 4) // 3
                    w, r = wg_sb[:, n], w_round[:, n]
                    if step % 3 == 1:
                        dve.tensor_scalar(r, w, w_scale[:, n:n + 1], ROUND, ALU.mult, ALU.add).then_inc(sem("w_q"), 1)
                    elif step % 3 == 2:
                        dve.wait_ge(sem("w_q"), 2 * n + 1)
                        dve.tensor_scalar(r, r, -ROUND, 1.0, ALU.add, ALU.min).then_inc(sem("w_q"), 1)
                    else:
                        dve.wait_ge(sem("w_q"), 2 * n + 2)
                        dve.tensor_scalar(w_tern[:, n], r, -1.0, None, ALU.max).then_inc(sem("w_tern"), 1)
            for m in range(UNITS0):
                a, z = FFN_HALVES[m // (UNITS0 // 2)]
                if 2 <= m < 5:
                    ternary(m - 2)
                if 6 <= m < 16:
                    ternary(m - 3)
                dve.wait_ge(sem("silu0"), m + 1)
                dve.wait_ge(sem("up0"), 2 * m + 2)
                wait(dve, sem("act_low"), m - 1)
                dve.scalar_tensor_tensor(act0[:, m % 2, 0:z - a], bank[:, 2 + 2 * (m % 2), 0:z - a], 1.0 / W_SCALE,
                                         silu0[:, m % 2, 0:z - a], ALU.mult, ALU.mult).then_inc(sem("act0"), 1)
                if m >= 1:
                    act_low(m - 1)
                if m == UNITS0 // 2 + 6:
                    dve_residual(dve, TT + 4, 2, range(4), in_bank_7)
                    dve_stats(dve, 2, range(4))
                if m == UNITS0 // 2 + 12:
                    dve_norm(dve, 2, range(4))
            act_low(UNITS0 - 1)
            for n in range(2 * H):
                h, half = n % H, n // H
                dve.wait_ge(sem("q1_high"), n + 1)
                part = (slice(None), slice(8 * half, 8 * half + 8), slice(S * h, S * (h + 1)))
                dve.scalar_tensor_tensor(q1[:, 1][part], bank[:, n % 4, 0:HALF].rearrange("p (b s) -> p b s", s=S),
                                         q_bias[:, h:h + 1], q1[:, 0][part], ALU.add, ALU.subtract).then_inc(sem("q1_low"), 1)
                if n == 4:
                    dve_residual(dve, 2 * TT, 2, range(4, TT), in_bank_7)
                    dve_stats(dve, 2, range(4, TT))
                if n == 9:
                    dve_norm(dve, 3, range(4, TT))
            LATE_LOW = (0, 1, 5)
            dve_max1(dve, 0, 0, 0)
            dve_norm1(dve, 0, 0, 0)

            def layer1(b, par, first, last):
                for t in range(T1):
                    nxt = (b, par, t + 1) if t < T1 - 1 else (b + 1, 1 - par, 0)
                    if last and t == PREP_AT[1][0] + 1:
                        dve_residual(dve, 2 * TT + EARLY, 1, range(EARLY), early_turned)
                        dve_stats(dve, 3, range(EARLY))
                    if last and t == T1 - 1:
                        dve_norm(dve, 4, range(EARLY))
                    if not (last and t == T1 - 1):
                        dve_max1(dve, *nxt)
                    if t - 1 in LATE_LOW:
                        dve_low1(dve, b, par, t - 1, 1)
                    dve_low1(dve, b, par, t, 0)
                    if not (last and t == T1 - 1):
                        dve_norm1(dve, *nxt)
                    if t not in LATE_LOW:
                        dve_low1(dve, b, par, t, 1)
            batches(dve, layer1)

            def quantise(call, a, z):
                dve.wait_ge(sem("ln_norm"), 3 * TT + z)
                done = 9 * call
                amax, scale, x = x_amax[:, a:z], x_qscale[:, a:z], x_norm[:, a:z]
                dve.tensor_reduce(amax, x, AX.X, ALU.max, apply_absolute_value=True).then_inc(sem("xq_s"), 1)
                dve.wait_ge(sem("xq_s"), done + 1)
                dve.tensor_scalar(amax, amax, 1e-5, None, ALU.max).then_inc(sem("xq_s"), 1)
                dve.wait_ge(sem("xq_s"), done + 2)
                dve.reciprocal(scale, amax).then_inc(sem("xq_s"), 1)
                dve.wait_ge(sem("xq_s"), done + 3)
                dve.tensor_scalar(scale, scale, 127.0, None, ALU.mult).then_inc(sem("xq_s"), 1)
                for n in range(2):
                    dve.tensor_scalar(x_deq[:, a:z, n], amax, 1.0 / 127.0, w_mean[:, n:n + 1], ALU.mult, ALU.mult)\
                        .then_inc(sem("xq_s"), 1)
                dve.wait_ge(sem("xq_s"), done + 6)
                dve.tensor_tensor(x, x, scale.unsqueeze(2).broadcast_to((128, z - a, E)), ALU.mult).then_inc(sem("xq_s"), 1)
                dve.wait_ge(sem("xq_s"), done + 7)
                dve.tensor_scalar(x, x, ROUND, None, ALU.add).then_inc(sem("xq_s"), 1)
                dve.wait_ge(sem("xq_s"), done + 8)
                dve.tensor_scalar(x, x, -ROUND, 127.0, ALU.add, ALU.min).then_inc(sem("xq_s"), 1)
                dve.wait_ge(sem("xq_s"), done + 9)
                dve.tensor_scalar(xq[:, a:z], x, -128.0, None, ALU.max).then_inc(sem("xq"), 1)
            quantise(0, 0, EARLY)

            def finish(t):
                dve.wait_ge(sem("down1"), t + 1)
                dve.scalar_tensor_tensor(x_tok[:, t, :], bank[:, 6 + t % 2, 0:128], h_deq[:, t:t + 1], x_tok[:, t, :],
                                         ALU.mult, ALU.add).then_inc(sem("final"), 1)
            for t in range(TT):
                if t == 2:
                    dve_residual(dve, 3 * TT, 1, range(EARLY, TT), late_turned)
                    dve_stats(dve, 3, range(EARLY, TT))
                if t == LATE_AT:
                    dve_norm(dve, 5, range(EARLY, TT))
                    quantise(1, EARLY, TT)
                dve.wait_ge(sem("up1"), 2 * t + 2)
                dve.wait_ge(sem("silu1"), t + 1)
                a = act1[:, t % 2, :]
                dve.scalar_tensor_tensor(a, bank[:, 2 * (t % 2) + 1, :], x_deq[:, t, 1:2], silu1[:, t % 2, :],
                                         ALU.mult, ALU.mult).then_inc(sem("act1"), 1)
                dve.wait_ge(sem("act1"), t + 1)
                dve.tensor_reduce(h_amax[:, t:t + 1], a, AX.X, ALU.max, apply_absolute_value=True).then_inc(sem("hq_s"), 1)
                dve.wait_ge(sem("hq_s"), 5 * t + 1)
                dve.tensor_scalar(h_amax[:, t:t + 1], h_amax[:, t:t + 1], 1e-5, 1.0 / 127.0, ALU.max, ALU.mult)\
                    .then_inc(sem("hq_s"), 1)
                dve.wait_ge(sem("hq_s"), 5 * t + 2)
                dve.reciprocal(h_qscale[:, t:t + 1], h_amax[:, t:t + 1]).then_inc(sem("hq_s"), 1)
                dve.tensor_scalar(h_deq[:, t:t + 1], h_amax[:, t:t + 1], down_scale[:], None, ALU.mult).then_inc(sem("hq_s"), 1)
                dve.wait_ge(sem("hq_s"), 5 * t + 4)
                dve.tensor_scalar(a, a, h_qscale[:, t:t + 1], ROUND, ALU.mult, ALU.add).then_inc(sem("hq_s"), 1)
                dve.wait_ge(sem("hq_s"), 5 * t + 5)
                dve.tensor_scalar(a, a, -ROUND, 127.0, ALU.add, ALU.min).then_inc(sem("hq_r"), 1)
                dve.wait_ge(sem("hq_r"), t + 1)
                wait(dve, sem("hq_turned"), t - 1)
                dve.tensor_scalar(hq[:, t % 2, :], a, -128.0, None, ALU.max).then_inc(sem("hq"), 1)
                if t >= 1:
                    finish(t - 1)
            finish(TT - 1)


_INS = ['x', 'ctx_1024', 'mask_Bx1xSxS2_if1', 'g_xattn', 'g_ffn', 'L0_xattn_Wv', 'L0_xattn_Wk', 'L0_xattn_Wq',
        'L0_xattn_Wo', 'L0_xattn_bo', 'L0_ffn_gate_w', 'L0_ffn_sh_gate', 'L0_ffn_sh_up', 'L0_ffn_sh_down',
        'L0_ffn_rt_gate', 'L0_ffn_rt_up', 'L0_ffn_rt_down', 'L1_xattn_Wq', 'L1_xattn_bq', 'L1_xattn_Wkv',
        'L1_xattn_bkv', 'L1_xattn_Wo', 'L1_xattn_bo', 'L1_ffn_w_gate', 'L1_ffn_w_up', 'L1_ffn_w_down']


def build(nc, arrays_of):
    args = [nc.dram_tensor(f"in_{n}", a.shape, mybir.dt.from_np(a.dtype), kind="ExternalInput").ap()
            for n, a in arrays_of.items()]
    out = nc.dram_tensor("out_x", arrays_of['x'].shape, F32, kind="ExternalOutput").ap()
    flamingo_kernel(nc, *args, out)


def kernel(**inputs):
    import numpy as np
    import concourse.bacc as bacc
    from concourse.bass_utils import run_bass_kernel_spmd

    nc = bacc.Bacc("TRN2", target_bir_lowering=False, num_devices=1)
    arrays = {n: np.ascontiguousarray(inputs[n]) for n in _INS}
    build(nc, arrays)
    r = run_bass_kernel_spmd(nc, [{f"in_{n}": a for n, a in arrays.items()}], core_ids=[0])
    return r.results[0]["out_x"]
```
